# Optimizing a Trainium2 kernel written in Bass

```python
import numpy as np
import jax
import jax.numpy as jnp

def _softmax(x, axis=-1):
    return jax.nn.softmax(x, axis=axis)
def _gelu(x):
    return jax.nn.gelu(x, approximate=True)
def _silu(x):
    return jax.nn.silu(x)
def _sigmoid(x):
    return jax.nn.sigmoid(x)
def _layernorm(x, axis=-1, eps=1e-5):
    m = jnp.mean(x, axis=axis, keepdims=True)
    v = jnp.var(x, axis=axis, keepdims=True)
    return (x - m) / jnp.sqrt(v + eps)
def _scatter_add(tgt, idx, src, axis=0):
    return tgt.at[idx].add(src)
def _segment_sum(src, seg, n):
    return jax.ops.segment_sum(src, seg, n)

kernel_name = 'mk_conv_preact_d2_conv_nchw384_f95906'

def setup_inputs(seed: int = 0):
    np.random.seed(seed)
    _w = jnp.asarray
    def _rec_inputs():
        import jax
        import jax.numpy as jnp
        _gk = jax.random.key(seed)
        x = -9.309e-05 + 1 * jax.random.normal(jax.random.fold_in(_gk, 1), (4, 384, 56, 56), jnp.float32)
        return x
    x = _rec_inputs()
    def _L0_conv_setup():
        import jax, jax.numpy as jnp
        import numpy as np
        from jax import lax
        B, C, H, W = (4, 384, 56, 56)
        NH, HC, STRIDE = (12, 32, 2)
        SCALE = HC ** (-0.5)

        def _dwconv(x, w, b, stride):
            y = lax.conv_general_dilated(x, w, (stride, stride), [(1, 1), (1, 1)], dimension_numbers=('NCHW', 'OIHW', 'NCHW'), feature_group_count=x.shape[1])
            return y + b[None, :, None, None]

        def _grid_sample_bilinear(value, grid):
            Hh, Ww = (value.shape[2], value.shape[3])
            ix = (grid[..., 0] + 1.0) * 0.5 * (Ww - 1)
            iy = (grid[..., 1] + 1.0) * 0.5 * (Hh - 1)
            x0 = jnp.floor(ix)
            y0 = jnp.floor(iy)
            wx = ix - x0
            wy = iy - y0
            x0i = jnp.clip(x0, 0, Ww - 1).astype(jnp.int32)
            x1i = jnp.clip(x0 + 1, 0, Ww - 1).astype(jnp.int32)
            y0i = jnp.clip(y0, 0, Hh - 1).astype(jnp.int32)
            y1i = jnp.clip(y0 + 1, 0, Hh - 1).astype(jnp.int32)

            def per_b(img, y0i, y1i, x0i, x1i, wx, wy):
                v00 = img[:, y0i, x0i]
                v01 = img[:, y0i, x1i]
                v10 = img[:, y1i, x0i]
                v11 = img[:, y1i, x1i]
                return v00 * (1 - wx) * (1 - wy) + v01 * wx * (1 - wy) + v10 * (1 - wx) * wy + v11 * wx * wy
            return jax.vmap(per_b)(value, y0i, y1i, x0i, x1i, wx, wy)

        def _ref_points(Hk, Wk):
            ref_y = jnp.linspace(0.5, Hk - 0.5, Hk)
            ref_x = jnp.linspace(0.5, Wk - 0.5, Wk)
            ry, rx = jnp.meshgrid(ref_y, ref_x, indexing='ij')
            return jnp.stack([ry / Hk * 2 - 1, rx / Wk * 2 - 1], axis=-1)
        key = jax.random.key(seed)
        ks = jax.random.split(key, 10)
        s = 0.05
        return {'x': jax.random.normal(ks[0], (B, C, H, W), jnp.float32), 'w_v': jax.random.normal(ks[1], (C, 1, 3, 3), jnp.float32) * s, 'b_v': jnp.zeros((C,), jnp.float32), 'w_q': jax.random.normal(ks[2], (C, 1, 3, 3), jnp.float32) * s, 'b_q': jnp.zeros((C,), jnp.float32), 'w_k': jax.random.normal(ks[3], (C, 1, 3, 3), jnp.float32) * s, 'b_k': jnp.zeros((C,), jnp.float32), 'w_off1': jax.random.normal(ks[4], (C, 1, 3, 3), jnp.float32) * s, 'b_off1': jnp.zeros((C,), jnp.float32), 'ln_g': jnp.ones((C,), jnp.float32), 'ln_b': jnp.zeros((C,), jnp.float32), 'w_off2': jax.random.normal(ks[5], (2, C), jnp.float32) * s, 'w_out': jax.random.normal(ks[6], (C, C), jnp.float32) * s}
    _L0_conv_all = _L0_conv_setup()
    _L0_conv_in = {k: v for k, v in _L0_conv_all.items() if k in ('w_v', 'b_v', 'w_q', 'b_q', 'w_k', 'b_k', 'w_off1', 'b_off1', 'ln_g', 'ln_b', 'w_off2', 'w_out', )}
    del _L0_conv_all

    def _L1_conv_setup():
        import math
        import jax, jax.numpy as jnp
        import numpy as np
        C = 384
        NH = 8
        HD = C // NH
        HIDDEN = int(C * 4.0)
        EPS = 1e-05
        key = jax.random.key(seed)
        ks = jax.random.split(key, 8)
        s = 0.02
        return {'x': jax.random.normal(ks[0], (32, C, 32, 32), dtype=jnp.float32), 'qkv_w': jax.random.normal(ks[1], (C, 3 * C), dtype=jnp.float32) * s, 'proj_w': jax.random.normal(ks[2], (C, C), dtype=jnp.float32) * s, 'proj_b': jnp.zeros((C,), dtype=jnp.float32), 'ln_g': jnp.ones((C,), dtype=jnp.float32), 'ln_b': jnp.zeros((C,), dtype=jnp.float32), 'fc1_w': jax.random.normal(ks[3], (C, HIDDEN), dtype=jnp.float32) * s, 'fc1_b': jnp.zeros((HIDDEN,), dtype=jnp.float32), 'fc2_w': jax.random.normal(ks[4], (HIDDEN, C), dtype=jnp.float32) * s, 'fc2_b': jnp.zeros((C,), dtype=jnp.float32)}
    _L1_conv_all = _L1_conv_setup()
    _L1_conv_in = {k: v for k, v in _L1_conv_all.items() if k in ('qkv_w', 'proj_w', 'proj_b', 'ln_g', 'ln_b', 'fc1_w', 'fc1_b', 'fc2_w', 'fc2_b', )}
    del _L1_conv_all

    return {
        "x": x,
        "L0_conv_w_v": _L0_conv_in["w_v"],
        "L0_conv_b_v": _L0_conv_in["b_v"],
        "L0_conv_w_q": _L0_conv_in["w_q"],
        "L0_conv_b_q": _L0_conv_in["b_q"],
        "L0_conv_w_k": _L0_conv_in["w_k"],
        "L0_conv_b_k": _L0_conv_in["b_k"],
        "L0_conv_w_off1": _L0_conv_in["w_off1"],
        "L0_conv_b_off1": _L0_conv_in["b_off1"],
        "L0_conv_ln_g": _L0_conv_in["ln_g"],
        "L0_conv_ln_b": _L0_conv_in["ln_b"],
        "L0_conv_w_off2": _L0_conv_in["w_off2"],
        "L0_conv_w_out": _L0_conv_in["w_out"],
        "L1_conv_qkv_w": _L1_conv_in["qkv_w"],
        "L1_conv_proj_w": _L1_conv_in["proj_w"],
        "L1_conv_proj_b": _L1_conv_in["proj_b"],
        "L1_conv_ln_g": _L1_conv_in["ln_g"],
        "L1_conv_ln_b": _L1_conv_in["ln_b"],
        "L1_conv_fc1_w": _L1_conv_in["fc1_w"],
        "L1_conv_fc1_b": _L1_conv_in["fc1_b"],
        "L1_conv_fc2_w": _L1_conv_in["fc2_w"],
        "L1_conv_fc2_b": _L1_conv_in["fc2_b"],
    }

def reference(x, L0_conv_w_v, L0_conv_b_v, L0_conv_w_q, L0_conv_b_q, L0_conv_w_k, L0_conv_b_k, L0_conv_w_off1, L0_conv_b_off1, L0_conv_ln_g, L0_conv_ln_b, L0_conv_w_off2, L0_conv_w_out, L1_conv_qkv_w, L1_conv_proj_w, L1_conv_proj_b, L1_conv_ln_g, L1_conv_ln_b, L1_conv_fc1_w, L1_conv_fc1_b, L1_conv_fc2_w, L1_conv_fc2_b):
    import jax
    import jax.numpy as jnp
    def _L0_conv_ref(x, w_v, b_v, w_q, b_q, w_k, b_k, w_off1, b_off1, ln_g, ln_b, w_off2, w_out):
        import jax, jax.numpy as jnp
        import numpy as np
        from jax import lax
        B, C, H, W = (4, 384, 56, 56)
        NH, HC, STRIDE = (12, 32, 2)
        SCALE = HC ** (-0.5)

        def _dwconv(x, w, b, stride):
            y = lax.conv_general_dilated(x, w, (stride, stride), [(1, 1), (1, 1)], dimension_numbers=('NCHW', 'OIHW', 'NCHW'), feature_group_count=x.shape[1])
            return y + b[None, :, None, None]

        def _grid_sample_bilinear(value, grid):
            Hh, Ww = (value.shape[2], value.shape[3])
            ix = (grid[..., 0] + 1.0) * 0.5 * (Ww - 1)
            iy = (grid[..., 1] + 1.0) * 0.5 * (Hh - 1)
            x0 = jnp.floor(ix)
            y0 = jnp.floor(iy)
            wx = ix - x0
            wy = iy - y0
            x0i = jnp.clip(x0, 0, Ww - 1).astype(jnp.int32)
            x1i = jnp.clip(x0 + 1, 0, Ww - 1).astype(jnp.int32)
            y0i = jnp.clip(y0, 0, Hh - 1).astype(jnp.int32)
            y1i = jnp.clip(y0 + 1, 0, Hh - 1).astype(jnp.int32)

            def per_b(img, y0i, y1i, x0i, x1i, wx, wy):
                v00 = img[:, y0i, x0i]
                v01 = img[:, y0i, x1i]
                v10 = img[:, y1i, x0i]
                v11 = img[:, y1i, x1i]
                return v00 * (1 - wx) * (1 - wy) + v01 * wx * (1 - wy) + v10 * (1 - wx) * wy + v11 * wx * wy
            return jax.vmap(per_b)(value, y0i, y1i, x0i, x1i, wx, wy)

        def _ref_points(Hk, Wk):
            ref_y = jnp.linspace(0.5, Hk - 0.5, Hk)
            ref_x = jnp.linspace(0.5, Wk - 0.5, Wk)
            ry, rx = jnp.meshgrid(ref_y, ref_x, indexing='ij')
            return jnp.stack([ry / Hk * 2 - 1, rx / Wk * 2 - 1], axis=-1)
        Bx, Cx, Hx, Wx = x.shape
        value = _dwconv(x, w_v, b_v, 1)
        query = _dwconv(x, w_q, b_q, 1).reshape(Bx * NH, HC, -1)
        key = _dwconv(x, w_k, b_k, STRIDE).reshape(Bx * NH, HC, -1)
        off = _dwconv(x, w_off1, b_off1, STRIDE)
        o = jnp.transpose(off, (0, 2, 3, 1))
        mu = o.mean(-1, keepdims=True)
        var = o.var(-1, keepdims=True)
        o = (o - mu) / jnp.sqrt(var + 1e-05) * ln_g + ln_b
        o = jax.nn.gelu(o, approximate=False)
        offset = jnp.einsum('bhwc,pc->bhwp', o, w_off2)
        Hk, Wk = (offset.shape[1], offset.shape[2])
        ref = _ref_points(Hk, Wk)[None]
        pos = jnp.tanh(offset + ref)
        grid = pos[..., ::-1]
        v_sampled = _grid_sample_bilinear(value, grid)
        v_sampled = v_sampled.reshape(Bx * NH, HC, -1)
        attn = jnp.einsum('bcm,bcn->bmn', query, key) * SCALE
        out = jnp.einsum('bmn,bcn->bcm', attn, v_sampled)
        out = out.reshape(Bx, Cx, Hx, Wx)
        y = jnp.einsum('bchw,oc->bohw', out, w_out)
        return y

    def _L1_conv_ref(x, qkv_w, proj_w, proj_b, ln_g, ln_b, fc1_w, fc1_b, fc2_w, fc2_b):
        import math
        import jax, jax.numpy as jnp
        import numpy as np
        C = 384
        NH = 8
        HD = C // NH
        HIDDEN = int(C * 4.0)
        EPS = 1e-05
        B, Cc, H, W = x.shape
        L = H * W
        xs = jnp.transpose(x, (0, 2, 3, 1)).reshape(B, L, Cc)
        mu = jnp.mean(xs, axis=-1, keepdims=True)
        var = jnp.mean((xs - mu) ** 2, axis=-1, keepdims=True)
        xn = (xs - mu) / jnp.sqrt(var + EPS) * ln_g + ln_b
        mid = jax.nn.silu(xn @ fc1_w + fc1_b) @ fc2_w + fc2_b
        mid = mid.reshape(B, L, NH, HD).transpose(0, 2, 1, 3)
        qkv = (xs @ qkv_w).reshape(B, L, 3, NH, HD).transpose(2, 0, 3, 1, 4)
        q, k, v = (qkv[0], qkv[1], qkv[2])
        q = q / jnp.linalg.norm(q, axis=-1, keepdims=True)
        k = k / jnp.linalg.norm(k, axis=-1, keepdims=True)
        attn = jnp.einsum('bhld,bhle->bhde', k, v)
        o = 0.5 * v + 1.0 / math.pi * jnp.einsum('bhld,bhde->bhle', q, attn)
        o = o / jnp.linalg.norm(o, axis=-1, keepdims=True)
        o = o + mid
        o = o.transpose(0, 2, 1, 3).reshape(B, L, Cc)
        o = o @ proj_w + proj_b
        return jnp.transpose(o, (0, 2, 1)).reshape(B, Cc, H, W)

    def _gn(v, G=32, eps=1e-5):
        B_, C_, H_, W_ = v.shape
        g = v.reshape(B_, G, C_ // G, H_, W_)
        m = jnp.mean(g, axis=(2, 3, 4), keepdims=True)
        s = jnp.var(g, axis=(2, 3, 4), keepdims=True)
        return ((g - m) / jnp.sqrt(s + eps)).reshape(v.shape)

    def _ln_c(v, eps=1e-6):
        m = jnp.mean(v, axis=1, keepdims=True)
        s = jnp.var(v, axis=1, keepdims=True)
        return (v - m) / jnp.sqrt(s + eps)

    def _ln_t(v, eps=1e-5):
        m = jnp.mean(v, axis=-1, keepdims=True)
        s = jnp.var(v, axis=-1, keepdims=True)
        return (v - m) / jnp.sqrt(s + eps)

    def _to_tokens(v):
        B_, C_, H_, W_ = v.shape
        return v.reshape(B_, C_, H_ * W_).transpose(0, 2, 1)
    def _from_tokens(t, like):
        B_, C_, H_, W_ = like.shape
        return t.transpose(0, 2, 1).reshape(B_, C_, H_, W_)

    x = x + _L0_conv_ref(_gn(x), L0_conv_w_v, L0_conv_b_v, L0_conv_w_q, L0_conv_b_q, L0_conv_w_k, L0_conv_b_k, L0_conv_w_off1, L0_conv_b_off1, L0_conv_ln_g, L0_conv_ln_b, L0_conv_w_off2, L0_conv_w_out)
    x = x + _L1_conv_ref(_gn(x), L1_conv_qkv_w, L1_conv_proj_w, L1_conv_proj_b, L1_conv_ln_g, L1_conv_ln_b, L1_conv_fc1_w, L1_conv_fc1_b, L1_conv_fc2_w, L1_conv_fc2_b)
    return x


_drawn_inputs = setup_inputs


def setup_inputs(seed=0):
    import zlib

    import numpy as np

    out = dict(_drawn_inputs(seed))
    spreads = {'L0_conv_b_v': (0.0, 0.1),
     'L0_conv_b_q': (0.0, 0.1),
     'L0_conv_b_k': (0.0, 0.1),
     'L0_conv_b_off1': (0.0, 0.1),
     'L0_conv_ln_g': (1.0, 0.2),
     'L0_conv_ln_b': (0.0, 0.1),
     'L1_conv_proj_b': (0.0, 0.1),
     'L1_conv_ln_g': (1.0, 0.6),
     'L1_conv_ln_b': (0.0, 0.8),
     'L1_conv_fc1_b': (0.0, 0.794),
     'L1_conv_fc2_b': (0.0, 0.348)}
    factors = {}
    for name, (base, spread) in spreads.items():
        noise = np.random.default_rng([zlib.crc32(name.encode()), seed]).standard_normal(out[name].shape)
        drawn = base * np.exp(spread * noise) if base else spread * noise
        out[name] = jnp.asarray(drawn.astype(out[name].dtype))
    for name, factor in factors.items():
        out[name] = (out[name] * factor).astype(out[name].dtype)
    return out
```

```python
import numpy as np
import concourse.bass as bass
from concourse import mybir
from contextlib import ExitStack

F32 = mybir.dt.float32
F32R = mybir.dt.float32r
I32 = mybir.dt.int32
ALU = mybir.AluOpType
ACT = mybir.ActivationFunctionType
AX = mybir.AxisListType

P = 128
C, H, W = 384, 56, 56
KC = C // P
L = H * W
STRIPS = 7
RS = H // STRIPS
T = RS * W
SUB = 4
TS = T // SUB
HK = WK = 28
SR = HK // STRIPS
TK = SR * WK
GROUPS = 32
CG = C // GROUPS
HC0 = 32
NH1, HD = 8, 48
HID = 4 * C
JC = HID // P
WIN = ((0, 144), (96, 288), (240, 384))
WOFF = (0, 144, 336)
WTOT = 480
TAPS = [(ky, kx) for ky in range(3) for kx in range(3)]
EPS_GN = 1e-5
EPS_LN = 1e-5


def constants():
    f = np.float32
    ch = np.arange(C)
    grp = (ch[:, None] // CG == ch[None, :] // CG).astype(f) / f(CG)
    head0 = (np.arange(P)[:, None] // HC0 == np.arange(P)[None, :] // HC0).astype(f) * f(HC0 ** -0.5)
    head1 = np.zeros((P, WTOT), f)
    for k, (lo, hi) in enumerate(WIN):
        same = (P * k + np.arange(P))[:, None] // HD == np.arange(lo, hi)[None, :] // HD
        head1[:, WOFF[k]:WOFF[k] + hi - lo] = same * f(1.0 / np.pi)
    hsel = (ch[:, None] // HD == np.arange(NH1)[None, :]).astype(f).reshape(KC, P, NH1).transpose(1, 0, 2)
    ref = (np.linspace(0.5, HK - 0.5, HK, dtype=f) / f(HK) * f(2) - f(1)).astype(f)
    ry, rx = np.meshgrid(ref, ref, indexing="ij")
    refp = np.stack([ry, rx], -1).reshape(STRIPS, TK, 2).transpose(1, 0, 2)
    edge = np.ones((P, 2, STRIPS), f)
    edge[:, 0, 0] = 0
    edge[:, 1, STRIPS - 1] = 0
    return {
        "ident": np.eye(P, dtype=f),
        "grp": grp.reshape(KC, P, C).transpose(1, 0, 2),
        "head0": head0, "head1": head1, "hsel": hsel, "refp": refp, "edge": edge,
    }


def build(nc, d, out, debug=None):
    B = d["x"].shape[0]
    debug = debug or {}

    def scratch(name, shape):
        return nc.dram_tensor(name, shape, F32, kind="Internal").ap()

    x1_d = scratch("x1_scr", (B, C, L))
    q_d = scratch("q_scr", (C, L))
    pair_d = scratch("pair_scr", (L + 1, 2 * C))
    kt_d = scratch("kt_scr", (HK * WK, C))
    ln_d = scratch("ln_scr", (HK * WK, C))
    v1_d = scratch("v1_scr", (L, C))
    x1_v = x1_d.rearrange("b (k p) l -> b p k l", p=P)
    q_v = q_d.rearrange("(k p) l -> p k l", p=P)
    out_v = out.rearrange("b (k p) h w -> b p k (h w)", p=P)
    xin_v = d["x"].rearrange("b (k p) h w -> b p k h w", p=P)

    ctx = ExitStack()
    with ctx:
        def sem(name):
            return ctx.enter_context(nc.semaphore(name))

        top = [(nc.sbuf_base + 31) // 32 * 32]
        limit = nc.sbuf_usable_end

        def sb(name, shape, dt=F32, at=top):
            size = int(np.prod(shape[1:])) * 4
            t = nc.alloc_sbuf_tensor_at(name, shape, dt, offset=at[0])
            at[0] += (size + 31) // 32 * 32
            assert at[0] <= limit, (name, at[0], limit)
            return t

        W1H, W1L = sb("W1H", [P, KC, HID], F32R), sb("W1L", [P, KC, HID], F32R)
        W2H, W2L = sb("W2H", [P, JC, C], F32R), sb("W2L", [P, JC, C], F32R)
        WQH, WQL = sb("WQH", [P, KC, 3 * C], F32R), sb("WQL", [P, KC, 3 * C], F32R)
        WPH, WPL = sb("WPH", [P, KC, C], F32R), sb("WPL", [P, KC, C], F32R)
        ident = sb("ident_s", [P, P])
        head0, head1 = sb("head0_s", [P, P]), sb("head1_s", [P, WTOT])
        hsel = sb("hsel_s", [P, KC, NH1])
        edge = sb("edge_s", [P, 2, STRIPS])
        wconv = sb("wconv", [P, 4, KC, 9])
        bconv = sb("bconv", [P, 4, KC])
        b1p, b1 = sb("b1p", [P, JC]), sb("b1", [P, JC])
        b2, bp = sb("b2", [P, KC]), sb("bp", [P, KC])
        lng, lnb = sb("lng", [P, KC]), sb("lnb", [P, KC])
        nhalf = sb("nhalf", [P, 32])
        gst, gmv = sb("gst", [P, KC, 2]), sb("gmv", [P, KC, 2])
        gdev, gvar, gmean = sb("gdev", [P, KC, 2]), sb("gvar", [P, KC]), sb("gmean", [P, KC])
        coefA, coefB = sb("coefA", [P, 2, KC]), sb("coefB", [P, 2, KC])
        bst = sb("bst", [P, KC, STRIPS, 6])
        zero = sb("zero", [P, P])
        AB = sb("AB", [P, WTOT])
        shared = top[0]

        at = [shared]
        stg = sb("stg", [P, KC * HID], at=at)
        ones = sb("ones", [P, P], at=at)

        at = [shared]
        grp = sb("grp_s", [P, KC, C], at=at)
        base0 = at[0]
        X0 = sb("X0", [P, KC, H, W], at=at)
        at = [base0]
        XR = sb("XR", [P, KC, RS + 2, W], at=at)
        XG = sb("XG", [P, KC, RS + 2, W + 2], at=at)
        VA, QA = sb("VA", [P, KC, T], at=at), sb("QA", [P, KC, T], at=at)
        KA, OA = sb("KA", [P, KC, TK], at=at), sb("OA", [P, KC, TK], at=at)
        KT, VT = sb("KT", [TS, C], at=at), sb("VT", [TS, SUB, C], at=at)
        LN = sb("LN", [TK, C], at=at)
        olng, olnb = sb("olng", [TK, C], at=at), sb("olnb", [TK, C], at=at)
        obn, oag = sb("obn", [TK, 6], at=at), sb("oag", [TK, 2], at=at)
        orv = sb("orv", [TK, 2], at=at)
        at = [base0]
        LN7 = sb("LN7", [TK, STRIPS, C], at=at)
        KT7 = sb("KT7", [TK, STRIPS, C], at=at)
        G7 = sb("G7", [TK, 4, 2, 2, C], at=at)
        VS = sb("VS", [TK, 4, C], at=at)
        woff2 = sb("woff2", [TK, 2, C], at=at)
        prod = VS
        refp = sb("refp_s", [TK, STRIPS, 2], at=at)
        OFF = sb("OFF", [TK, STRIPS, 2], at=at)
        POS = sb("POS", [TK, STRIPS, 2], at=at)
        FI = sb("FI", [TK, STRIPS, 2], I32, at=at)
        FF, FG = sb("FF", [TK, STRIPS, 2], at=at), sb("FG", [TK, STRIPS, 2], at=at)
        WG, WN = sb("WG", [TK, STRIPS, 2], at=at), sb("WN", [TK, STRIPS, 2], at=at)
        W4 = sb("W4", [TK, STRIPS, 4], at=at)
        IXF = sb("IXF", [TK, 2, STRIPS], at=at)
        IX = sb("IX", [TK, 2, STRIPS], I32, at=at)
        MT = sb("MT", [P, KC, P], at=at)
        woT = sb("woT", [P, KC, C], at=at)
        W2TH, W2TL = sb("W2TH", [P, KC, C], F32R, at=at), sb("W2TL", [P, KC, C], F32R, at=at)
        at = [base0]
        CQ = sb("CQ", [P, 2, KC, T], at=at)
        CX = sb("CX", [P, 2, KC, T], at=at)
        CH, CL = sb("CH", [P, KC, T], F32R, at=at), sb("CL", [P, KC, T], F32R, at=at)

        at = [shared]
        X = sb("X", [P, KC, T], at=at)
        XH, XL = sb("XH", [P, KC, T], F32R, at=at), sb("XL", [P, KC, T], F32R, at=at)
        base1 = at[0]
        K1, V1 = sb("K1", [TS, SUB, C], at=at), sb("V1", [TS, SUB, C], at=at)
        KS = sb("KS", [TS, SUB, C], at=at)
        kn, rk = sb("kn", [TS, SUB * NH1], at=at), sb("rk", [TS, SUB * NH1], at=at)

        at = [base1]
        XRH, XRL = sb("XRH", [P, KC, T], F32R, at=at), sb("XRL", [P, KC, T], F32R, at=at)
        Q = sb("Q", [P, KC, T], at=at)
        QQ = sb("QQ", [P, SUB * C], at=at)
        V = sb("V", [TS, SUB, C], at=at)
        OT = sb("OT", [P, KC, T], at=at)
        S = sb("S", [P, 2, T], at=at)
        SH, SL = sb("SH", [P, 3, T], F32R, at=at), sb("SL", [P, 3, T], F32R, at=at)
        MH = sb("MH", [P, KC, T], F32R, at=at)
        ML = sb("ML", [P, KC, T], F32R, at=at)
        Y = sb("Y", [P, KC, T], at=at)
        DH, DL = sb("DH", [TS, SUB, TS], F32R, at=at), sb("DL", [TS, SUB, TS], F32R, at=at)
        o1r = sb("o1r", [TS, P], F32R, at=at)
        xbn, xag = sb("xbn", [TS, SUB, 6], at=at), sb("xag", [TS, SUB, 2], at=at)
        rve, rr = sb("rve", [TS, SUB], at=at), sb("rr", [TS, SUB], at=at)
        rh, rl = sb("rh", [TS, SUB], F32R, at=at), sb("rl", [TS, SUB], at=at)
        qn, rq = sb("qn", [TS, SUB * NH1], at=at), sb("rq", [TS, SUB * NH1], at=at)
        on, ro = sb("on", [TS, SUB * NH1], at=at), sb("ro", [TS, SUB * NH1], at=at)
        OS = QQ[0:TS, :]

        bank = [ctx.enter_context(nc.psum_tensor(f"bank{i}", [P, 512], F32)) for i in range(8)]

        stage_done = sem("stage_done")
        held = sem("held")
        names = """const_ld stg_ld stg_used set_sum set_mean set_ctr set_bias set_ones set_ps
            x0_ld gn_part gn_st gn_mm gn_s1 gn_dev gn_mm2 gn_mean gn_var gn_rstd gn_nb
            grp_ld ln_ld
            xr_ld xg edged va qa ka oa otp ktp vtp kt_ev vt_ev obn_s orv_s orr_s ln1 ln2 ln_s
            q_st kt_st ln_st pair_st
            b_ld gelu dots offr tanh_s ixs fint ffl fgt ff0 ff1 wgt wneg w4s ixf ixf2 ixi gath0 gath1 gath2 gath3 vs_ch vs_s mt_mm mt_ev w2_mm w2_ev
            cq_ld0 cq_ld1 cx_ld0 cx_ld1 ch cl y0 x1a x1bn x1_st0 x1_st1
            kv_ld kxs kxh kxl k_mm v_mm k_sq k_ev v_ev k_red k_rs k_hat v1_st at_mm at_z ab_s
            x_ld v_ld y_ld y_st xs xh xl xt_mm bn_s ag_s rve_s rr_s rh_s rl_s dg rb_mm xsr xrh xrl
            q_mm q_ev qq qs_mm qn_s rq_s qa_mm o_sc o_mx o_sq o_red ro_s o_fin ot_mm ot_ev
            f1 s_s sh sl f2 mid mh ml pj y_s cc pair_z""".split()
        s = {n: sem("s_" + n) for n in names}

        def slot_uses(t, slots):
            return len(range(t % slots, STRIPS, slots)), t // slots + 1

        def slot_at(b, t, slots, each):
            per, upto = slot_uses(t, slots)
            return b * (per * each) + upto * each

        HEAD = 16
        ahead = """otp ktp vtp q_st kt_st pair_st ln_st va qa ka oa at_mm k_hat v1_st k_ev v_ev s_s sl f2""".split()

        block = ctx.enter_context(nc.Block())

        def alone(eng):
            eng.sem_inc(held, 1)

        def stage_end(eng, n):
            alone(eng)
            eng.drain().then_inc(stage_done, 1)
            eng.wait_ge(stage_done, n * 5 + 5)
            alone(eng)

        STAGES = 7

        def strip_px(t):
            return bass.ts(t, T)

        @block.sync
        def _(sp):
            n_const = 0
            for dst, src in [
                (ident, d["ident"]), (head0, d["head0"]), (head1, d["head1"]), (hsel, d["hsel"]), (edge, d["edge"]),
                (b1, d["fc1_b"]), (b2, d["fc2_b"]), (bp, d["proj_b"]), (lng, d["ln_g"]), (lnb, d["ln_b"]),
                (wconv, d["w_conv"]), (bconv, d["b_conv"]),
            ]:
                sp.dma_start(dst.ap(), src).then_inc(s["const_ld"], 16)
                n_const += 1
            for i, (name, cols) in enumerate([("fc1_w", KC * HID), ("fc2_w", JC * C), ("qkv_w", KC * 3 * C), ("proj_w", KC * C)]):
                if i:
                    sp.wait_ge(s["stg_used"], i)
                sp.dma_start(stg[:, 0:cols], d[name]).then_inc(s["stg_ld"], 16)
            sp.wait_ge(s["set_ones"], 1)
            sp.dma_start(pair_d[0, 0:C].rearrange("(a c) -> a c", a=3), zero[0:3, :]).then_inc(s["pair_z"], 16)
            sp.dma_start(pair_d[L, C:2 * C].rearrange("(a c) -> a c", a=3), zero[0:3, :]).then_inc(s["pair_z"], 16)
            sp.wait_ge(s["pair_z"], 32)
            stage_end(sp, 0)
            with sp.Fori(0, B) as b:
                for k in range(KC):
                    sp.dma_start(X0[:, k, :, :], xin_v[b, :, k, 1:H + 1, :]).then_inc(s["x0_ld"], 16)
                sp.dma_start(grp[:, :, :], d["grp"]).then_inc(s["grp_ld"], 16)
                stage_end(sp, b * STAGES + 1)
                sp.dma_start(olng[:, :], d["off_g"]).then_inc(s["ln_ld"], 16)
                sp.dma_start(olnb[:, :], d["off_b"]).then_inc(s["ln_ld"], 16)

                def load_strip(t, n):
                    sp.dma_start(XR[:, :, :, :], xin_v[b, :, :, bass.ds(t * RS, RS + 2), :]).then_inc(s["xr_ld"], 16)

                def store_strip(t, n):
                    sp.wait_ge(s["qa"], HEAD + n * 24 + 24)
                    sp.dma_start(q_v[:, :, strip_px(t)], QA[:, :, :]).then_inc(s["q_st"], 16)
                    sp.wait_ge(s["kt_ev"], n + 1)
                    sp.dma_start(kt_d[bass.ts(t, TK), :], KT[:, :]).then_inc(s["kt_st"], 16)
                    sp.wait_ge(s["ln_s"], n + 1)
                    sp.dma_start(ln_d[bass.ts(t, TK), :], LN[:, :]).then_inc(s["ln_st"], 16)
                    sp.wait_ge(s["vt_ev"], n * SUB + SUB)
                    sp.dma_start(pair_d[bass.ds(t * T + 1, T), 0:C].rearrange("(s p) c -> p s c", p=TS),
                                 VT[:, :, :]).then_inc(s["pair_st"], 16)
                    sp.dma_start(pair_d[bass.ds(t * T, T), C:2 * C].rearrange("(s p) c -> p s c", p=TS),
                                 VT[:, :, :]).then_inc(s["pair_st"], 16)

                load_strip(0, None)
                with sp.Fori(0, STRIPS - 1) as t:
                    n = b * STRIPS + t
                    sp.wait_ge(s["xg"], n * KC + KC)
                    load_strip(t + 1, n + 1)
                    store_strip(t, n)
                store_strip(STRIPS - 1, b * STRIPS + STRIPS - 1)
                sp.wait_ge(s["q_st"], HEAD + (b + 1) * (16 * STRIPS))
                sp.wait_ge(s["kt_st"], HEAD + (b + 1) * (16 * STRIPS))
                sp.wait_ge(s["ln_st"], HEAD + (b + 1) * (16 * STRIPS))
                sp.wait_ge(s["pair_st"], HEAD + (b + 1) * (32 * STRIPS))
                stage_end(sp, b * STAGES + 2)
                for dst, src in [(LN7[:, :, :], ln_d.rearrange("(t p) c -> p t c", p=TK)),
                                 (KT7[:, :, :], kt_d.rearrange("(t p) c -> p t c", p=TK)),
                                 (woff2[:, :, :], d["w_off2"]), (refp[:, :, :], d["refp"]),
                                 (woT[:, :, :], d["w_outT"])]:
                    sp.dma_start(dst, src).then_inc(s["b_ld"], 16)
                stage_end(sp, b * STAGES + 3)
                for t in range(STRIPS):
                    if t >= 2:
                        sp.wait_ge(s["cl"], b * STRIPS + t - 1)
                    sp.dma_start(CQ[:, t % 2, :, :], q_v[:, :, t * T:(t + 1) * T]).then_inc(s[f"cq_ld{t % 2}"], 16)
                    if t >= 2:
                        sp.wait_ge(s[f"x1_st{t % 2}"], slot_at(b, t - 2, 2, 16))
                        alone(sp)
                        sp.wait_ge(s["x1bn"], b * STRIPS + t - 1)
                    sp.dma_start(CX[:, t % 2, :, :].rearrange("p k (r w) -> p k r w", w=W),
                                 xin_v[b, :, :, 1 + t * RS:1 + (t + 1) * RS, :]).then_inc(s[f"cx_ld{t % 2}"], 16)
                    if t >= 1:
                        sp.wait_ge(s["x1a"], (b * STRIPS + t) * KC)
                        sp.dma_start(x1_v[b, :, :, (t - 1) * T:t * T], CX[:, (t - 1) % 2, :, :]).then_inc(s[f"x1_st{(t - 1) % 2}"], 16)
                sp.wait_ge(s["x1a"], (b * STRIPS + STRIPS) * KC)
                sp.dma_start(x1_v[b, :, :, (STRIPS - 1) * T:L], CX[:, (STRIPS - 1) % 2, :, :]).then_inc(s[f"x1_st{(STRIPS - 1) % 2}"], 16)
                for t in range(STRIPS - 2, STRIPS):
                    sp.wait_ge(s[f"x1_st{t % 2}"], slot_at(b, t, 2, 16))
                    alone(sp)
                stage_end(sp, b * STAGES + 4)
                sp.dma_start(X[:, :, :], x1_v[b, :, :, 0:T]).then_inc(s["kv_ld"], 16)
                with sp.Fori(0, STRIPS - 1) as t:
                    n = b * STRIPS + t
                    sp.wait_ge(s["kxl"], n + 1)
                    sp.dma_start(X[:, :, :], x1_v[b, :, :, strip_px(t + 1)]).then_inc(s["kv_ld"], 16)
                    sp.wait_ge(s["v_ev"], HEAD + n * SUB + SUB)
                    sp.dma_start(v1_d[bass.ts(t, T), :].rearrange("(s p) c -> p s c", p=TS), V1[:, :, :]).then_inc(s["v1_st"], 16)
                sp.wait_ge(s["v_ev"], HEAD + b * (STRIPS * SUB) + STRIPS * SUB)
                sp.dma_start(v1_d[(STRIPS - 1) * T:L, :].rearrange("(s p) c -> p s c", p=TS), V1[:, :, :]).then_inc(s["v1_st"], 16)
                sp.wait_ge(s["v1_st"], HEAD + (b + 1) * (16 * STRIPS))
                stage_end(sp, b * STAGES + 5)
                stage_end(sp, b * STAGES + 6)

                def load_pre(t):
                    sp.dma_start(X[:, :, :], x1_v[b, :, :, strip_px(t)]).then_inc(s["x_ld"], 16)

                def load_v(t):
                    sp.dma_start(V[:, :, :], v1_d[bass.ts(t, T), :].rearrange("(s p) c -> p s c", p=TS)).then_inc(s["v_ld"], 16)

                def load_res(t):
                    sp.dma_start(Y[:, :, :], x1_v[b, :, :, strip_px(t)]).then_inc(s["y_ld"], 16)

                def store_out(t, n):
                    sp.wait_ge(s["y_s"], n * KC + KC)
                    sp.dma_start(out_v[b, :, :, strip_px(t)], Y[:, :, :]).then_inc(s["y_st"], 16)

                load_pre(0)
                load_v(0)
                load_res(0)
                n0 = b * STRIPS
                sp.wait_ge(s["xrl"], n0 + 1)
                load_pre(1)
                sp.wait_ge(s["ot_mm"], n0 * KC + KC)
                load_v(1)
                with sp.Fori(1, STRIPS - 1) as t:
                    n = b * STRIPS + t
                    sp.wait_ge(s["xrl"], n + 1)
                    load_pre(t + 1)
                    store_out(t - 1, n - 1)
                    sp.wait_ge(s["y_st"], n * 16)
                    load_res(t)
                    sp.wait_ge(s["ot_mm"], n * KC + KC)
                    load_v(t + 1)
                nl = b * STRIPS + STRIPS - 1
                store_out(STRIPS - 2, nl - 1)
                sp.wait_ge(s["y_st"], nl * 16)
                load_res(STRIPS - 1)
                store_out(STRIPS - 1, nl)
                sp.wait_ge(s["y_st"], nl * 16 + 16)
                stage_end(sp, b * STAGES + 7)

        @block.gpsimd
        def _(pool):
            for name in ahead:
                pool.sem_inc(s[name], HEAD)
            pool.memset(nhalf[:, :], -0.5)
            pool.memset(ones[:, :], 1.0 / C)
            pool.memset(zero[:, :], 0.0).then_inc(s["set_ones"], 1)
            stage_end(pool, 0)

            def gn_coef(g):
                pool.wait_ge(s["gn_var"], g * 2 + 2)
                pool.tensor_tensor(gvar[:, :], gvar[:, :], nhalf[:, 0:KC], ALU.pow).then_inc(s["gn_rstd"], 1)

            with pool.Fori(0, B) as b:
                gn_coef(b * 2)
                stage_end(pool, b * STAGES + 1)
                with pool.Fori(0, STRIPS) as t:
                    n = b * STRIPS + t
                    pool.wait_ge(s["orv_s"], n + 1)
                    pool.tensor_tensor(orv[:, 1:2], orv[:, 0:1], nhalf[0:TK, 0:1], ALU.pow).then_inc(s["orr_s"], 1)
                stage_end(pool, b * STAGES + 2)
                pool.wait_ge(s["ixi"], b + 1)
                alone(pool)
                for t in range(STRIPS):
                    if t >= 4:
                        pool.wait_ge(s["vs_s"], b * STRIPS + t - 3)
                        alone(pool)
                    for r in range(2):
                        pool.indirect_dma_start(
                            out=G7[:, t % 4, r, :, :].rearrange("p a c -> p (a c)"), out_offset=None,
                            in_=pair_d, in_offset=bass.IndirectOffsetOnAxis(ap=IX[:, r, t:t + 1], axis=0),
                        ).then_inc(s[f"gath{t % 4}"], 16)
                for t in range(STRIPS - 4, STRIPS):
                    pool.wait_ge(s[f"gath{t % 4}"], slot_at(b, t, 4, 32))
                stage_end(pool, b * STAGES + 3)
                gn_coef(b * 2 + 1)
                stage_end(pool, b * STAGES + 4)
                with pool.Fori(0, STRIPS) as t:
                    n = b * STRIPS + t
                    for h, (lo, hi) in enumerate(((0, 24), (24, 32))):
                        pool.wait_ge(s["k_red"], n * 2 + h + 1)
                        pool.tensor_tensor(rk[:, lo:hi], kn[:, lo:hi], nhalf[0:TS, lo:hi], ALU.pow).then_inc(s["k_rs"], 1)
                stage_end(pool, b * STAGES + 5)
                stage_end(pool, b * STAGES + 6)
                with pool.Fori(0, STRIPS) as t:
                    n = b * STRIPS + t
                    pool.wait_ge(s["rve_s"], n + 1)
                    pool.tensor_tensor(rr[:, :], rve[:, :], nhalf[0:TS, 0:SUB], ALU.pow).then_inc(s["rr_s"], 1)
                    pool.wait_ge(s["qn_s"], n + 1)
                    pool.tensor_tensor(rq[:, :], qn[:, :], nhalf[0:TS, :], ALU.pow).then_inc(s["rq_s"], 1)
                    pool.wait_ge(s["o_red"], n + 1)
                    pool.tensor_tensor(ro[:, :], on[:, :], nhalf[0:TS, :], ALU.pow).then_inc(s["ro_s"], 1)
                stage_end(pool, b * STAGES + 7)

        @block.tensor
        def _(pe):
            mm, tr = pe.matmul, pe.transpose

            pe.wait_ge(s["const_ld"], 12 * 16)
            pe.wait_ge(s["stg_ld"], 16)
            pe.wait_ge(s["set_ones"], 1)
            for j in range(JC):
                for k in range(KC):
                    last = mm(bank[0][:, j:j + 1], stg[:, k * HID + j * P:k * HID + (j + 1) * P], lnb[:, k:k + 1],
                              start=(k == 0), stop=(k == KC - 1))
            last.then_inc(s["set_ps"], 1)
            pe.wait_ge(s["set_sum"], 1)
            for q in range(3):
                for k in range(KC):
                    last = mm(bank[1 + q][:, :], ones[:, :], stg[:, k * HID + q * 512:k * HID + (q + 1) * 512],
                              start=(k == 0), stop=(k == KC - 1))
            last.then_inc(s["set_ps"], 1)
            stage_end(pe, 0)

            def gn_groups(g):
                pe.wait_ge(s["gn_st"], g + 1)
                for ko in range(KC):
                    for ki in range(KC):
                        last = mm(bank[0][:, 2 * ko:2 * ko + 2], grp[:, ki, ko * P:(ko + 1) * P], gst[:, ki, :],
                                  start=(ki == 0), stop=(ki == KC - 1))
                last.then_inc(s["gn_mm"], 1)
                pe.wait_ge(s["gn_dev"], g + 1)
                for ko in range(KC):
                    for ki in range(KC):
                        last = mm(bank[1][:, 2 * ko:2 * ko + 2], grp[:, ki, ko * P:(ko + 1) * P], gdev[:, ki, :],
                                  start=(ki == 0), stop=(ki == KC - 1))
                last.then_inc(s["gn_mm2"], 1)

            def three_pass(o, wh, wl, xh, xl, first, stop):
                mm(o, wh, xh, start=first, stop=False)
                mm(o, wh, xl, start=False, stop=False)
                return mm(o, wl, xh, start=False, stop=stop)

            with pe.Fori(0, B) as b:
                pe.wait_ge(s["grp_ld"], b * 16 + 16)
                gn_groups(b * 2)
                stage_end(pe, b * STAGES + 1)
                with pe.Fori(0, STRIPS) as t:
                    n = b * STRIPS + t
                    pe.wait_ge(s["oa"], HEAD + n * 24 + 24)
                    for k in range(KC):
                        last = tr(bank[0][0:TK, k * P:(k + 1) * P], OA[:, k, :], ident[:, :])
                    last.then_inc(s["otp"], 1)
                    pe.wait_ge(s["ka"], HEAD + n * 24 + 24)
                    for k in range(KC):
                        last = tr(bank[1][0:TK, k * P:(k + 1) * P], KA[:, k, :], ident[:, :])
                    last.then_inc(s["ktp"], 1)
                    pe.wait_ge(s["va"], HEAD + n * 24 + 24)
                    for u in range(SUB):
                        for k in range(KC):
                            last = tr(bank[2 + u][0:TS, k * P:(k + 1) * P], VA[:, k, u * TS:(u + 1) * TS], ident[:, :])
                        last.then_inc(s["vtp"], 1)
                stage_end(pe, b * STAGES + 2)
                pe.wait_ge(s["b_ld"], b * 80 + 80)
                for t in range(STRIPS):
                    pe.wait_ge(s["vs_s"], b * STRIPS + t + 1)
                    for k in range(KC):
                        last = mm(bank[k][:, 0:P], VS[:, t % 4, k * P:(k + 1) * P], KT7[:, t, k * P:(k + 1) * P],
                                  start=(t == 0), stop=(t == STRIPS - 1))
                    last.then_inc(s["mt_mm"], 1)
                pe.wait_ge(s["mt_ev"], b + 1)
                for k in range(KC):
                    last = mm(bank[3 + k][:, 0:C], MT[:, k, :], woT[:, k, :], start=True, stop=True)
                last.then_inc(s["w2_mm"], 1)
                stage_end(pe, b * STAGES + 3)
                for t in range(STRIPS):
                    pe.wait_ge(s["cl"], b * STRIPS + t + 1)
                    pe.wait_ge(s["ch"], b * STRIPS + t + 1)
                    for o in range(KC):
                        if t >= 2:
                            pe.wait_ge(s["x1a"], (b * STRIPS + t - 2) * KC + o + 1)
                        p = bank[2 + 3 * (t % 2) + o][:, 0:T]
                        for k in range(KC):
                            last = three_pass(p, W2TH[:, k, o * P:(o + 1) * P], W2TL[:, k, o * P:(o + 1) * P],
                                              CH[:, k, :], CL[:, k, :], k == 0, k == KC - 1)
                        last.then_inc(s["y0"], 1)
                gn_groups(b * 2 + 1)
                stage_end(pe, b * STAGES + 4)

                KB, VB, ATB = (0, 1, 2), (3, 4, 5), 6
                mm(bank[ATB][:, 0:WTOT], zero[:, :], head1[:, :], start=True, stop=False, skip_group_check=True)

                def kv(n, u):
                    if u == 0:
                        pe.wait_ge(s["kxl"], n + 1)
                        pe.wait_ge(s["kxh"], n + 1)
                    for bk, c0, free, sg in ((KB, C, "k_ev", "k_mm"), (VB, 2 * C, "v_ev", "v_mm")):
                        if u == 3:
                            pe.wait_ge(s[free], HEAD + n * SUB + 1)
                        elif u == 0:
                            pe.wait_ge(s[free], HEAD + n * SUB)
                        p = bank[bk[u % 3]][0:TS, 0:C]
                        for k in range(KC):
                            xh, xl = XH[:, k, u * TS:(u + 1) * TS], XL[:, k, u * TS:(u + 1) * TS]
                            mm(p, xh, WQH[:, k, c0:c0 + C], start=(k == 0), stop=False)
                            mm(p, xh, WQL[:, k, c0:c0 + C], start=False, stop=False)
                            last = mm(p, xl, WQH[:, k, c0:c0 + C], start=False, stop=(k == KC - 1))
                        last.then_inc(s[sg], 1)

                def state(n):
                    pe.wait_ge(s["k_hat"], HEAD + n * 2 + 2)
                    pe.wait_ge(s["v_ev"], HEAD + n * SUB + SUB)
                    for u in range(SUB):
                        for k, (lo, hi) in enumerate(WIN):
                            last = mm(bank[ATB][:, WOFF[k]:WOFF[k] + hi - lo], K1[:, u, k * P:(k + 1) * P], V1[:, u, lo:hi],
                                      start=False, stop=False, skip_group_check=True)
                    last.then_inc(s["at_mm"], 1)

                n0 = b * STRIPS
                for u in range(3):
                    if u == 0:
                        pe.wait_ge(s["kxl"], n0 + 1)
                        pe.wait_ge(s["kxh"], n0 + 1)
                    for bk, c0, sg in ((KB, C, "k_mm"), (VB, 2 * C, "v_mm")):
                        p = bank[bk[u]][0:TS, 0:C]
                        for k in range(KC):
                            xh, xl = XH[:, k, u * TS:(u + 1) * TS], XL[:, k, u * TS:(u + 1) * TS]
                            mm(p, xh, WQH[:, k, c0:c0 + C], start=(k == 0), stop=False)
                            mm(p, xh, WQL[:, k, c0:c0 + C], start=False, stop=False)
                            last = mm(p, xl, WQH[:, k, c0:c0 + C], start=False, stop=(k == KC - 1))
                        last.then_inc(s[sg], 1)
                kv(n0, 3)
                with pe.Fori(1, STRIPS) as t:
                    n = b * STRIPS + t
                    kv(n, 0)
                    kv(n, 1)
                    kv(n, 2)
                    state(n - 1)
                    kv(n, 3)
                state(n0 + STRIPS - 1)
                stage_end(pe, b * STAGES + 5)
                stage_end(pe, b * STAGES + 6)

                CB = (5, 6, 7)

                def turn_x(n, u):
                    if u == 0:
                        pe.wait_ge(s["xs"], n * KC + KC)
                    if u == 3:
                        pe.wait_ge(s["bn_s"], n * SUB + 1)
                    for k in range(KC):
                        last = tr(bank[CB[u % 3]][0:TS, k * P:(k + 1) * P], X[:, k, u * TS:(u + 1) * TS], ident[:, :])
                    last.then_inc(s["xt_mm"], 1)

                def query(n, o):
                    if o == 0:
                        pe.wait_ge(s["xl"], n + 1)
                        pe.wait_ge(s["xh"], n + 1)
                        pe.wait_ge(s["bn_s"], n * SUB + 2)
                    if o == 1:
                        pe.wait_ge(s["bn_s"], n * SUB + 3)
                    if o == 2:
                        pe.wait_ge(s["bn_s"], n * SUB + 4)
                    p = bank[(6, 7, 5)[o]][:, 0:T]
                    for k in range(KC):
                        last = three_pass(p, WQH[:, k, o * P:(o + 1) * P], WQL[:, k, o * P:(o + 1) * P],
                                          XH[:, k, :], XL[:, k, :], k == 0, k == KC - 1)
                    last.then_inc(s["q_mm"], 1)

                def spread_r(n):
                    pe.wait_ge(s["dg"], n * 2 + 2)
                    pe.wait_ge(s["q_ev"], n * KC + 1)
                    pe.wait_ge(s["qq"], n * KC + 1)
                    for u in range(SUB):
                        mm(bank[6][:, u * TS:(u + 1) * TS], o1r[:, :], DH[:, u, :], start=True, stop=False)
                        last = mm(bank[6][:, u * TS:(u + 1) * TS], o1r[:, :], DL[:, u, :], start=False, stop=True)
                    last.then_inc(s["rb_mm"], 1)

                def query_norms(n):
                    pe.wait_ge(s["q_ev"], n * KC + 2)
                    pe.wait_ge(s["qq"], n * KC + KC)
                    for u in range(SUB):
                        for k in range(KC):
                            last = mm(bank[7][0:TS, u * NH1:(u + 1) * NH1], QQ[:, k * T + u * TS:k * T + (u + 1) * TS],
                                      hsel[:, k, :], start=(k == 0), stop=(k == KC - 1))
                    last.then_inc(s["qs_mm"], 1)

                def attend(n, u):
                    if u == 0:
                        pe.wait_ge(s["q_ev"], n * KC + KC)
                    if u == 1:
                        pe.wait_ge(s["xsr"], n + 1)
                    if u == 2:
                        pe.wait_ge(s["qn_s"], n + 1)
                    if u == 3:
                        pe.wait_ge(s["o_sc"], n * SUB + 1)
                    p = bank[(5, 6, 7, 5)[u]]
                    for k, (lo, hi) in enumerate(WIN):
                        last = mm(p[0:TS, lo:hi], Q[:, k, u * TS:(u + 1) * TS], AB[:, WOFF[k]:WOFF[k] + hi - lo],
                                  start=(k == 0), stop=(k == KC - 1), skip_group_check=True)
                    last.then_inc(s["qa_mm"], 1)

                def fc1(n, j):
                    if j == 0:
                        pe.wait_ge(s["xrl"], n + 1)
                        pe.wait_ge(s["xrh"], n + 1)
                    pe.wait_ge(s["s_s"], HEAD + n * JC + (j - 1))
                    p = bank[j % 2][:, 0:T]
                    for k in range(KC):
                        last = three_pass(p, W1H[:, k, j * P:(j + 1) * P], W1L[:, k, j * P:(j + 1) * P],
                                          XRH[:, k, :], XRL[:, k, :], k == 0, k == KC - 1)
                    last.then_inc(s["f1"], 1)

                def fc2(n, j, first):
                    pe.wait_ge(s["sl"], HEAD + n * JC + j + 1)
                    pe.wait_ge(s["sh"], n * JC + j + 1)
                    if j == 0 and not first:
                        pe.wait_ge(s["mid"], n * KC)
                    for o in range(KC):
                        last = three_pass(bank[2 + o][:, 0:T], W2H[:, j, o * P:(o + 1) * P], W2L[:, j, o * P:(o + 1) * P],
                                          SH[:, j % 3, :], SL[:, j % 3, :], j == 0, j == JC - 1)
                    last.then_inc(s["f2"], 1)

                def proj(n):
                    pe.wait_ge(s["mh"], n + 1)
                    pe.wait_ge(s["ml"], n + 1)
                    for o in range(KC):
                        p = bank[CB[o]][:, 0:T]
                        for k in range(KC):
                            last = three_pass(p, WPH[:, k, o * P:(o + 1) * P], WPL[:, k, o * P:(o + 1) * P],
                                              MH[:, k, :], ML[:, k, :], k == 0, k == KC - 1)
                        last.then_inc(s["pj"], 1)

                def turn_o(n, prev):
                    pe.wait_ge(s["o_fin"], n + 1)
                    for k in range(KC):
                        if prev:
                            pe.wait_ge(s["y_s"], (n - 1) * KC + k + 1)
                        for u in range(SUB):
                            last = tr(bank[CB[k]][:, u * TS:(u + 1) * TS], V[:, u, k * P:(k + 1) * P], ident[0:TS, 0:TS])
                        last.then_inc(s["ot_mm"], 1)

                def pre(n, step):
                    if step == 1:
                        pe.wait_ge(s["xs"], n * KC + KC)
                        turn_x(n, 0)
                        turn_x(n, 1)
                        turn_x(n, 2)
                    elif step == 2:
                        turn_x(n, 3)
                        query(n, 0)
                    elif step == 3:
                        query(n, 1)
                        query(n, 2)
                    elif step == 4:
                        spread_r(n)
                        query_norms(n)
                    elif step == 5:
                        attend(n, 0)
                        attend(n, 1)
                    elif step == 6:
                        attend(n, 2)
                        attend(n, 3)

                def tile(n, first, last):
                    fc1(n, 0)
                    fc1(n, 1)
                    fc1(n, 2)
                    if not first:
                        pe.wait_ge(s["o_sc"], n * SUB + SUB)
                        proj(n - 1)
                    fc2(n, 0, first)
                    fc1(n, 3)
                    if first:
                        pe.wait_ge(s["o_sc"], n * SUB + SUB)
                    turn_o(n, not first)
                    fc2(n, 1, first)
                    fc1(n, 4)
                    if not last:
                        pe.wait_ge(s["ot_ev"], n * KC + KC)
                        pre(n + 1, 1)
                    fc2(n, 2, first)
                    fc1(n, 5)
                    for i in range(3, JC):
                        if not last and 2 <= i - 1 <= 6:
                            pre(n + 1, i - 1)
                        fc2(n, i, first)
                        if i + 3 < JC:
                            fc1(n, i + 3)

                for step in range(1, 7):
                    pre(n0, step)
                tile(n0, True, False)
                with pe.Fori(1, STRIPS - 1) as t:
                    tile(b * STRIPS + t, False, False)
                tile(n0 + STRIPS - 1, False, True)
                pe.wait_ge(s["ot_ev"], (n0 + STRIPS) * KC)
                proj(n0 + STRIPS - 1)
                stage_end(pe, b * STAGES + 7)

        @block.scalar
        def _(act):
            fn = act.activation
            act.wait_ge(s["const_ld"], 12 * 16)
            stage_end(act, 0)
            with act.Fori(0, B) as b:
                stage_end(act, b * STAGES + 1)

                def strip(n):
                    act.wait_ge(s["xr_ld"], n * 16 + 16)
                    act.wait_ge(s["va"], HEAD + n * 24)
                    act.wait_ge(s["qa"], HEAD + n * 24)
                    act.wait_ge(s["ka"], HEAD + n * 24)
                    act.wait_ge(s["oa"], HEAD + n * 24)
                    for k in range(KC):
                        fn(XG[:, k, :, 1:W + 1], XR[:, k, :, :], ACT.Identity, bias=coefB[:, 0, k:k + 1],
                           scale=coefA[:, 0, k:k + 1]).then_inc(s["xg"], 1)

                def strip_out(n):
                    act.wait_ge(s["ktp"], HEAD + n + 1)
                    act.wait_ge(s["kt_st"], HEAD + n * 16)
                    fn(KT[:, :], bank[1][0:TK, 0:C], ACT.Copy).then_inc(s["kt_ev"], 1)
                    act.wait_ge(s["pair_st"], HEAD + n * 32)
                    for u in range(SUB):
                        act.wait_ge(s["vtp"], HEAD + n * SUB + u + 1)
                        fn(VT[:, u, :], bank[2 + u][0:TS, 0:C], ACT.Copy).then_inc(s["vt_ev"], 1)

                with act.Fori(0, STRIPS) as t:
                    n = b * STRIPS + t
                    strip(n)
                    strip_out(n)
                stage_end(act, b * STAGES + 2)
                act.wait_ge(s["b_ld"], b * 80 + 80)
                fn(LN7[:, :, :], LN7[:, :, :], ACT.Gelu).then_inc(s["gelu"], 1)
                act.wait_ge(s["offr"], b + 1)
                fn(POS[:, :, :], OFF[:, :, :], ACT.Tanh).then_inc(s["tanh_s"], 1)
                stage_end(act, b * STAGES + 3)
                for t in range(STRIPS):
                    act.wait_ge(s[f"cq_ld{t % 2}"], slot_at(b, t, 2, 16))
                    if t >= 1:
                        act.wait_ge(s["y0"], (b * STRIPS + t) * KC)
                    fn(CH[:, :, :], CQ[:, t % 2, :, :], ACT.Copy).then_inc(s["ch"], 1)
                stage_end(act, b * STAGES + 4)

                def norm_in(n, ld, sg):
                    act.wait_ge(s[ld], n * 16 + 16)
                    for k in range(KC):
                        fn(X[:, k, :], X[:, k, :], ACT.Identity, bias=coefB[:, 1, k:k + 1],
                           scale=coefA[:, 1, k:k + 1]).then_inc(s[sg], 1)

                def kv_out(n, u):
                    act.wait_ge(s["k_mm"], n * SUB + u + 1)
                    fn(KS[:, u, :], bank[u % 3][0:TS, 0:C], ACT.Square).then_inc(s["k_sq"], 1)
                    fn(K1[:, u, :], bank[u % 3][0:TS, 0:C], ACT.Copy).then_inc(s["k_ev"], 1)
                    act.wait_ge(s["v_mm"], n * SUB + u + 1)
                    fn(V1[:, u, :], bank[3 + u % 3][0:TS, 0:C], ACT.Copy).then_inc(s["v_ev"], 1)

                n0 = b * STRIPS
                norm_in(n0, "kv_ld", "kxs")
                with act.Fori(0, STRIPS) as t:
                    n = b * STRIPS + t
                    act.wait_ge(s["at_mm"], HEAD + n)
                    act.wait_ge(s["k_hat"], HEAD + n * 2)
                    act.wait_ge(s["v1_st"], HEAD + n * 16)
                    kv_out(n, 0)
                    kv_out(n, 1)
                    kv_out(n, 2)
                    kv_out(n, 3)
                    with act.If(t < STRIPS - 1):
                        norm_in(n + 1, "kv_ld", "kxs")
                    with act.Else():
                        act.nop()
                stage_end(act, b * STAGES + 5)
                stage_end(act, b * STAGES + 6)

                def query_out(n, o):
                    act.wait_ge(s["q_mm"], n * KC + o + 1)
                    p = bank[(6, 7, 5)[o]][:, 0:T]
                    fn(Q[:, o, :], p, ACT.Copy).then_inc(s["q_ev"], 1)
                    fn(QQ[:, o * T:(o + 1) * T], p, ACT.Square).then_inc(s["qq"], 1)

                def silu(n, j):
                    act.wait_ge(s["f1"], n * JC + j + 1)
                    act.wait_ge(s["sl"], HEAD + n * JC + j - 1)
                    fn(S[:, j % 2, :], bank[j % 2][:, 0:T], ACT.Silu, bias=b1p[:, j:j + 1]).then_inc(s["s_s"], 1)
                    act.wait_ge(s["f2"], HEAD + n * JC + j - 2)
                    act.wait_ge(s["s_s"], HEAD + n * JC + j + 1)
                    fn(SH[:, j % 3, :], S[:, j % 2, :], ACT.Copy).then_inc(s["sh"], 1)

                def o_square(n):
                    act.wait_ge(s["o_mx"], n + 1)
                    fn(OS, V[:, :, :].rearrange("p s c -> p (s c)"), ACT.Square).then_inc(s["o_sq"], 1)

                def mid_h(n):
                    act.wait_ge(s["mid"], n * KC + KC)
                    fn(MH[:, :, :], OT[:, :, :], ACT.Copy).then_inc(s["mh"], 1)

                def tile(n, first, last):
                    if not first:
                        mid_h(n - 1)
                    silu(n, 0)
                    silu(n, 1)
                    silu(n, 2)
                    if not last:
                        norm_in(n + 1, "x_ld", "xs")
                    silu(n, 3)
                    if not first:
                        act.wait_ge(s["ml"], n)
                    for k in range(KC):
                        act.wait_ge(s["ot_mm"], n * KC + k + 1)
                        fn(OT[:, k, :], bank[5 + k][:, 0:T], ACT.Copy).then_inc(s["ot_ev"], 1)
                    silu(n, 4)
                    silu(n, 5)
                    if not last:
                        query_out(n + 1, 0)
                    silu(n, 6)
                    if not last:
                        query_out(n + 1, 1)
                        query_out(n + 1, 2)
                    for j in range(7, JC):
                        silu(n, j)
                    if not last:
                        o_square(n + 1)

                norm_in(n0, "x_ld", "xs")
                for o in range(KC):
                    query_out(n0, o)
                o_square(n0)
                tile(n0, True, False)
                with act.Fori(1, STRIPS - 1) as t:
                    tile(b * STRIPS + t, False, False)
                tile(n0 + STRIPS - 1, False, True)
                mid_h(n0 + STRIPS - 1)
                stage_end(act, b * STAGES + 7)

        @block.vector
        def _(dve):
            tt, ts_, stt, cp = dve.tensor_tensor, dve.tensor_scalar, dve.scalar_tensor_tensor, dve.tensor_copy

            def f(ap):
                return ap.bitcast(F32)

            dve.wait_ge(s["const_ld"], 12 * 16)
            dve.wait_ge(s["set_ps"], 1)
            tt(b1p[:, :], b1[:, :], bank[0][:, 0:JC], ALU.add).then_inc(s["set_bias"], 1)
            for k in range(KC):
                last = ts_(stg[:, k * HID:(k + 1) * HID], stg[:, k * HID:(k + 1) * HID], lng[:, k:k + 1], None, ALU.mult)
            last.then_inc(s["set_sum"], 1)
            dve.wait_ge(s["set_sum"], 1)
            dve.wait_ge(s["set_ps"], 2)
            for k in range(KC):
                for q in range(3):
                    v = stg[:, k * HID + q * 512:k * HID + (q + 1) * 512]
                    last = tt(v, v, bank[1 + q][:, :], ALU.subtract)
            last.then_inc(s["set_ctr"], 1)
            dve.wait_ge(s["set_ctr"], 1)
            for i, (h, l, cols) in enumerate([(W1H, W1L, KC * HID), (W2H, W2L, JC * C), (WQH, WQL, KC * 3 * C), (WPH, WPL, KC * C)]):
                dve.wait_ge(s["stg_ld"], 16 * (i + 1))
                hf = h[:, :, :].rearrange("p k n -> p (k n)")
                lf = l[:, :, :].rearrange("p k n -> p (k n)")
                cp(hf, stg[:, 0:cols]).then_inc(s["cc"], 1)
                dve.wait_ge(s["cc"], i + 1)
                tt(lf, stg[:, 0:cols], f(hf), ALU.subtract).then_inc(s["stg_used"], 1)
            stage_end(dve, 0)

            def gn_stats(g, which):
                for k in range(KC):
                    last = dve.bn_aggr(gst[:, k, :], bst[:, k, :, :].rearrange("p a c -> p (a c)"))
                last.then_inc(s["gn_st"], 1)
                dve.wait_ge(s["gn_mm"], g + 1)
                cp(gmv[:, :, :], bank[0][:, 0:2 * KC].rearrange("p (k c) -> p k c", c=2)).then_inc(s["gn_s1"], 1)
                dve.wait_ge(s["gn_s1"], g + 1)
                tt(gdev[:, :, 0], gst[:, :, 0], gmv[:, :, 0], ALU.subtract)
                tt(gdev[:, :, 1], gst[:, :, 0], gmv[:, :, 0], ALU.subtract).then_inc(s["gn_nb"], 1)
                dve.wait_ge(s["gn_nb"], g * 3 + 1)
                tt(gdev[:, :, :], gdev[:, :, :], gdev[:, :, :], ALU.mult).then_inc(s["gn_dev"], 1)
                dve.wait_ge(s["gn_mm2"], g + 1)
                tt(gvar[:, :], gmv[:, :, 1], bank[1][:, 0:2 * KC:2], ALU.add).then_inc(s["gn_var"], 1)
                dve.wait_ge(s["gn_var"], g * 2 + 1)
                ts_(gvar[:, :], gvar[:, :], EPS_GN, None, ALU.add).then_inc(s["gn_var"], 1)
                dve.wait_ge(s["gn_rstd"], g + 1)
                cp(coefA[:, which, :], gvar[:, :])
                tt(gmean[:, :], gmv[:, :, 0], gvar[:, :], ALU.mult).then_inc(s["gn_nb"], 1)
                dve.wait_ge(s["gn_nb"], g * 3 + 2)
                ts_(coefB[:, which, :], gmean[:, :], -1.0, None, ALU.mult).then_inc(s["gn_nb"], 1)

            with dve.Fori(0, B) as b:
                for k in range(KC):
                    dve.wait_ge(s["x0_ld"], b * (16 * KC) + 16 * KC) if k == 0 else None
                    flat = X0[:, k, :, :].rearrange("p h w -> p (h w)")
                    for t in range(STRIPS):
                        last = dve.bn_stats(bst[:, k, t, :], flat[:, t * T:(t + 1) * T])
                last.then_inc(s["gn_part"], 1)
                dve.wait_ge(s["gn_part"], b + 1)
                alone(dve)
                gn_stats(b * 2, 0)
                stage_end(dve, b * STAGES + 1)

                for col in (0, W + 1):
                    last = dve.memset(XG[:, :, :, col:col + 1], 0.0)
                last.then_inc(s["cc"], 1)

                def strip(t, n):
                    dve.wait_ge(s["xg"], n * KC + KC)
                    ts_(XG[:, :, 0, 1:W + 1], XG[:, :, 0, 1:W + 1], edge[:, 0, bass.ds(t, 1)], None, ALU.mult)
                    ts_(XG[:, :, RS + 1, 1:W + 1], XG[:, :, RS + 1, 1:W + 1], edge[:, 1, bass.ds(t, 1)], None,
                        ALU.mult).then_inc(s["edged"], 1)
                    dve.wait_ge(s["edged"], n + 1)
                    for acc, which, st, sg, used, uval in (
                            (OA, 3, 2, "oa", "otp", n), (KA, 2, 2, "ka", "ktp", n),
                            (VA, 0, 1, "va", "vtp", n * SUB), (QA, 1, 1, "qa", "q_st", n * 16)):
                        rows, cols = (RS, W) if st == 1 else (SR, WK)
                        dve.wait_ge(s[used], HEAD + uval)
                        for i, (ky, kx) in enumerate(TAPS):
                            for k in range(KC):
                                src = XG[:, k, ky:ky + st * (rows - 1) + 1:st, kx:kx + st * (cols - 1) + 1:st]
                                o = acc[:, k, :].rearrange("p (r w) -> p r w", w=cols)
                                if i == 0:
                                    last = ts_(o, src, wconv[:, which, k, 0:1], bconv[:, which, k:k + 1], ALU.mult, ALU.add)
                                    if k == KC - 1:
                                        last.then_inc(s["cc"], 1)
                                else:
                                    if i > 1:
                                        dve.wait_ge(s[sg], HEAD + n * 24 + (i - 2) * KC + k + 1)
                                    stt(o, src, wconv[:, which, k, i:i + 1], o, ALU.mult, ALU.add).then_inc(s[sg], 1)
                            if i == 0:
                                dve.wait_ge(s["cc"], 4 + b + 1 + n * 4 + {3: 1, 2: 2, 0: 3, 1: 4}[which])

                def strip_ln(n):
                    dve.wait_ge(s["otp"], HEAD + n + 1)
                    dve.bn_stats(obn[:, :], bank[0][0:TK, 0:C]).then_inc(s["obn_s"], 1)
                    dve.wait_ge(s["obn_s"], n * 2 + 1)
                    alone(dve)
                    dve.bn_aggr(oag[:, :], obn[:, :]).then_inc(s["obn_s"], 1)
                    dve.wait_ge(s["obn_s"], n * 2 + 2)
                    ts_(orv[:, 0:1], oag[:, 1:2], EPS_LN, None, ALU.add).then_inc(s["orv_s"], 1)
                    dve.wait_ge(s["orr_s"], n + 1)
                    dve.wait_ge(s["ln_st"], HEAD + n * 16)
                    ts_(LN[:, :], bank[0][0:TK, 0:C], oag[:, 0:1], orv[:, 1:2], ALU.subtract, ALU.mult).then_inc(s["ln1"], 1)
                    dve.wait_ge(s["ln1"], n + 1)
                    tt(LN[:, :], LN[:, :], olng[:, :], ALU.mult).then_inc(s["ln2"], 1)
                    dve.wait_ge(s["ln2"], n + 1)
                    tt(LN[:, :], LN[:, :], olnb[:, :], ALU.add).then_inc(s["ln_s"], 1)

                dve.wait_ge(s["ln_ld"], b * 32 + 32)
                alone(dve)
                with dve.Fori(0, STRIPS) as t:
                    n = b * STRIPS + t
                    strip(t, n)
                    strip_ln(n)
                stage_end(dve, b * STAGES + 2)

                dve.wait_ge(s["b_ld"], b * 80 + 80)
                dve.wait_ge(s["gelu"], b + 1)
                for t in range(STRIPS):
                    for p in range(2):
                        i = 2 * t + p
                        if i >= 4:
                            dve.wait_ge(s["dots"], b * 14 + i - 3)
                        dve.tensor_tensor_reduce(out=prod[:, i % 4, :], in0=LN7[:, t, :], in1=woff2[:, p, :], scale=1.0, scalar=0.0,
                                                 op0=ALU.mult, op1=ALU.add, accum_out=OFF[:, t, p:p + 1]).then_inc(s["dots"], 1)
                dve.wait_ge(s["dots"], b * 14 + 14)
                tt(OFF[:, :, :], OFF[:, :, :], refp[:, :, :], ALU.add).then_inc(s["offr"], 1)
                dve.wait_ge(s["tanh_s"], b + 1)
                ts_(POS[:, :, :], POS[:, :, :], 1.0, 0.5 * (W - 1), ALU.add, ALU.mult).then_inc(s["ixs"], 1)
                dve.wait_ge(s["ixs"], b + 1)
                cp(FI[:, :, :], POS[:, :, :]).then_inc(s["fint"], 1)
                dve.wait_ge(s["fint"], b + 1)
                cp(FF[:, :, :], FI[:, :, :]).then_inc(s["ffl"], 1)
                dve.wait_ge(s["ffl"], b + 1)
                tt(FG[:, :, :], FF[:, :, :], POS[:, :, :], ALU.is_gt).then_inc(s["fgt"], 1)
                dve.wait_ge(s["fgt"], b + 1)
                tt(FF[:, :, :], FF[:, :, :], FG[:, :, :], ALU.subtract).then_inc(s["ff0"], 1)
                dve.wait_ge(s["ff0"], b + 1)
                ts_(FF[:, :, :], FF[:, :, :], 0.0, float(W - 2), ALU.max, ALU.min).then_inc(s["ff1"], 1)
                dve.wait_ge(s["ff1"], b + 1)
                tt(WG[:, :, :], POS[:, :, :], FF[:, :, :], ALU.subtract).then_inc(s["wgt"], 1)
                ts_(IXF[:, 0, :], FF[:, :, 0], float(W), 1.0, ALU.mult, ALU.add).then_inc(s["ixf"], 1)
                dve.wait_ge(s["ixf"], b + 1)
                tt(IXF[:, 0, :], IXF[:, 0, :], FF[:, :, 1], ALU.add).then_inc(s["ixf2"], 1)
                dve.wait_ge(s["ixf2"], b * 2 + 1)
                ts_(IXF[:, 1, :], IXF[:, 0, :], float(W), None, ALU.add).then_inc(s["ixf2"], 1)
                dve.wait_ge(s["ixf2"], b * 2 + 2)
                cp(IX[:, :, :], IXF[:, :, :]).then_inc(s["ixi"], 1)
                dve.wait_ge(s["wgt"], b + 1)
                ts_(WN[:, :, :], WG[:, :, :], -1.0, 1.0, ALU.mult, ALU.add).then_inc(s["wneg"], 1)
                dve.wait_ge(s["wneg"], b + 1)
                for c, (wy, wx) in enumerate(((WN, WN), (WN, WG), (WG, WN), (WG, WG))):
                    last = tt(W4[:, :, c], wy[:, :, 0], wx[:, :, 1], ALU.mult)
                last.then_inc(s["w4s"], 1)
                dve.wait_ge(s["w4s"], b + 1)
                for t in range(STRIPS):
                    dve.wait_ge(s[f"gath{t % 4}"], slot_at(b, t, 4, 32))
                    if t >= 4:
                        dve.wait_ge(s["mt_mm"], b * STRIPS + t - 3)
                    ts_(VS[:, t % 4, :], G7[:, t % 4, 0, 0, :], W4[:, t, 0:1], None, ALU.mult).then_inc(s["vs_ch"], 1)
                    for c in range(1, 4):
                        dve.wait_ge(s["vs_ch"], b * (3 * STRIPS) + 3 * t + c)
                        last = stt(VS[:, t % 4, :], G7[:, t % 4, c // 2, c % 2, :], W4[:, t, c:c + 1], VS[:, t % 4, :], ALU.mult, ALU.add)
                        last.then_inc(s["vs_ch"] if c < 3 else s["vs_s"], 1)
                dve.wait_ge(s["mt_mm"], b * STRIPS + STRIPS)
                for k in range(KC):
                    last = tt(MT[:, k, :], head0[:, :], bank[k][:, 0:P], ALU.mult)
                last.then_inc(s["mt_ev"], 1)
                dve.wait_ge(s["w2_mm"], b + 1)
                for k in range(KC):
                    last = cp(W2TH[:, k, :], bank[3 + k][:, 0:C])
                last.then_inc(s["w2_ev"], 1)
                dve.wait_ge(s["w2_ev"], b + 1)
                for k in range(KC):
                    tt(W2TL[:, k, :], bank[3 + k][:, 0:C], f(W2TH[:, k, :]), ALU.subtract)
                stage_end(dve, b * STAGES + 3)

                for t in range(STRIPS + 1):
                    if t < STRIPS:
                        dve.wait_ge(s["ch"], b * STRIPS + t + 1)
                        tt(CL[:, :, :], CQ[:, t % 2, :, :], f(CH[:, :, :]), ALU.subtract).then_inc(s["cl"], 1)
                    if t >= 1:
                        u = t - 1
                        dve.wait_ge(s[f"cx_ld{u % 2}"], slot_at(b, u, 2, 16))
                        for o in range(KC):
                            dve.wait_ge(s["y0"], (b * STRIPS + u) * KC + o + 1)
                            tt(CX[:, u % 2, o, :], CX[:, u % 2, o, :], bank[2 + 3 * (u % 2) + o][:, 0:T], ALU.add).then_inc(s["x1a"], 1)
                        for o in range(KC):
                            dve.wait_ge(s["x1a"], (b * STRIPS + u) * KC + o + 1)
                            last = dve.bn_stats(bst[:, o, u, :], CX[:, u % 2, o, :])
                        last.then_inc(s["x1bn"], 1)
                dve.wait_ge(s["x1bn"], b * STRIPS + STRIPS)
                alone(dve)
                gn_stats(b * 2 + 1, 1)
                stage_end(dve, b * STAGES + 4)

                n0 = b * STRIPS

                def kv_split(n, first):
                    dve.wait_ge(s["kxs"], n * KC + KC)
                    if not first:
                        dve.wait_ge(s["v_mm"], n * SUB)
                    cp(XH[:, :, :], X[:, :, :]).then_inc(s["kxh"], 1)
                    dve.wait_ge(s["kxh"], n + 1)
                    tt(XL[:, :, :], X[:, :, :], f(XH[:, :, :]), ALU.subtract).then_inc(s["kxl"], 1)

                def key_norm(n, h, lo, hi):
                    dve.wait_ge(s["k_sq"], n * SUB + hi)
                    dve.tensor_reduce(kn[:, lo * NH1:hi * NH1],
                                      KS[:, lo:hi, :].rearrange("p s (h c) -> p (s h) c", c=HD), AX.X, ALU.add).then_inc(s["k_red"], 1)

                def key_scale(n, h, lo, hi):
                    dve.wait_ge(s["k_rs"], n * 2 + h + 1)
                    dve.wait_ge(s["k_ev"], HEAD + n * SUB + hi)
                    v = K1[:, lo:hi, :].rearrange("p s (h c) -> p (s h) c", c=HD)
                    r = rk[:, lo * NH1:hi * NH1].unsqueeze(2).to_broadcast([TS, (hi - lo) * NH1, HD])
                    tt(v, v, r, ALU.mult).then_inc(s["k_hat"], 1)

                kv_split(n0, True)
                with dve.Fori(0, STRIPS) as t:
                    n = b * STRIPS + t
                    key_norm(n, 0, 0, 3)
                    key_norm(n, 1, 3, 4)
                    key_scale(n, 0, 0, 3)
                    with dve.If(t < STRIPS - 1):
                        kv_split(n + 1, False)
                    with dve.Else():
                        dve.nop()
                    key_scale(n, 1, 3, 4)
                stage_end(dve, b * STAGES + 5)
                tt(AB[:, :], head1[:, :], bank[6][:, 0:WTOT], ALU.mult).then_inc(s["ab_s"], 1)
                dve.memset(f(o1r[:, :]), 1.0)
                stage_end(dve, b * STAGES + 6)

                def split_x(n):
                    dve.wait_ge(s["xs"], n * KC + KC)
                    cp(XH[:, :, :], X[:, :, :]).then_inc(s["xh"], 1)
                    dve.wait_ge(s["xh"], n + 1)
                    tt(XL[:, :, :], X[:, :, :], f(XH[:, :, :]), ALU.subtract).then_inc(s["xl"], 1)

                def token_stats(n, u):
                    dve.wait_ge(s["xt_mm"], n * SUB + u + 1)
                    dve.bn_stats(xbn[:, u, :], bank[(5, 6, 7, 5)[u]][0:TS, 0:C]).then_inc(s["bn_s"], 1)

                def token_var(n):
                    dve.wait_ge(s["bn_s"], n * SUB + SUB)
                    alone(dve)
                    for u in range(SUB):
                        last = dve.bn_aggr(xag[:, u, :], xbn[:, u, :])
                    last.then_inc(s["ag_s"], 1)
                    dve.wait_ge(s["ag_s"], n + 1)
                    ts_(rve[:, :], xag[:, :, 1], EPS_LN, None, ALU.add).then_inc(s["rve_s"], 1)

                def token_diag(n):
                    dve.wait_ge(s["rr_s"], n + 1)
                    cp(rh[:, :], rr[:, :]).then_inc(s["rh_s"], 1)
                    dve.wait_ge(s["rh_s"], n + 1)
                    tt(rl[:, :], rr[:, :], f(rh[:, :]), ALU.subtract).then_inc(s["rl_s"], 1)
                    dve.wait_ge(s["rl_s"], n + 1)
                    idb = ident[0:TS, 0:TS].unsqueeze(1).to_broadcast([TS, SUB, TS])
                    tt(DH[:, :, :], idb, f(rh[:, :]).unsqueeze(2).to_broadcast([TS, SUB, TS]), ALU.mult).then_inc(s["dg"], 1)
                    tt(DL[:, :, :], idb, rl[:, :].unsqueeze(2).to_broadcast([TS, SUB, TS]), ALU.mult).then_inc(s["dg"], 1)

                def scale_x(n):
                    dve.wait_ge(s["rb_mm"], n + 1)
                    tt(X[:, :, :], X[:, :, :], bank[6][:, 0:T].unsqueeze(1).to_broadcast([P, KC, T]), ALU.mult).then_inc(s["xsr"], 1)

                def query_norm(n):
                    dve.wait_ge(s["qs_mm"], n + 1)
                    cp(qn[:, :], bank[7][0:TS, 0:SUB * NH1]).then_inc(s["qn_s"], 1)

                def heads(ap):
                    return ap.rearrange("p (h c) -> p h c", c=HD)

                def o_scale(n, u):
                    if u == 0:
                        dve.wait_ge(s["rq_s"], n + 1)
                    dve.wait_ge(s["qa_mm"], n * SUB + u + 1)
                    r = rq[:, u * NH1:(u + 1) * NH1].unsqueeze(2).to_broadcast([TS, NH1, HD])
                    tt(heads(OS[:, u * C:(u + 1) * C]), heads(bank[(5, 6, 7, 5)[u]][0:TS, 0:C]), r, ALU.mult).then_inc(s["o_sc"], 1)

                def o_mix(n):
                    dve.wait_ge(s["o_sc"], n * SUB + SUB)
                    dve.wait_ge(s["v_ld"], n * 16 + 16)
                    vf = V[:, :, :].rearrange("p s c -> p (s c)")
                    stt(vf, vf, 0.5, OS, ALU.mult, ALU.add).then_inc(s["o_mx"], 1)

                def o_norm(n):
                    dve.wait_ge(s["o_sq"], n + 1)
                    dve.tensor_reduce(on[:, :], heads(OS), AX.X, ALU.add).then_inc(s["o_red"], 1)

                def o_final(n):
                    dve.wait_ge(s["ro_s"], n + 1)
                    v = heads(V[:, :, :].rearrange("p s c -> p (s c)"))
                    tt(v, v, ro[:, :].unsqueeze(2).to_broadcast([TS, SUB * NH1, HD]), ALU.mult).then_inc(s["o_fin"], 1)

                def split_xr(n, first):
                    dve.wait_ge(s["xsr"], n + 1)
                    if not first:
                        dve.wait_ge(s["f1"], n * JC)
                    cp(XRH[:, :, :], X[:, :, :]).then_inc(s["xrh"], 1)
                    dve.wait_ge(s["xrh"], n + 1)
                    tt(XRL[:, :, :], X[:, :, :], f(XRH[:, :, :]), ALU.subtract).then_inc(s["xrl"], 1)

                def split_s(n, j):
                    dve.wait_ge(s["sh"], n * JC + j + 1)
                    tt(SL[:, j % 3, :], S[:, j % 2, :], f(SH[:, j % 3, :]), ALU.subtract).then_inc(s["sl"], 1)

                def middle(n):
                    dve.wait_ge(s["ot_ev"], n * KC + KC)
                    dve.wait_ge(s["f2"], HEAD + n * JC + JC)
                    for k in range(KC):
                        stt(OT[:, k, :], bank[2 + k][:, 0:T], b2[:, k:k + 1], OT[:, k, :], ALU.add, ALU.add).then_inc(s["mid"], 1)
                    dve.wait_ge(s["mh"], n + 1)
                    tt(ML[:, :, :], OT[:, :, :], f(MH[:, :, :]), ALU.subtract).then_inc(s["ml"], 1)

                def output(n):
                    dve.wait_ge(s["y_ld"], n * 16 + 16)
                    for k in range(KC):
                        dve.wait_ge(s["pj"], n * KC + k + 1)
                        stt(Y[:, k, :], bank[5 + k][:, 0:T], bp[:, k:k + 1], Y[:, k, :], ALU.add, ALU.add).then_inc(s["y_s"], 1)

                def tile(n, first, last):
                    if not first:
                        middle(n - 1)
                    split_s(n, 0)
                    o_final(n)
                    split_s(n, 1)
                    split_s(n, 2)
                    if not first:
                        output(n - 1)
                    split_s(n, 3)
                    if not last:
                        split_x(n + 1)
                    split_s(n, 4)
                    if not last:
                        token_stats(n + 1, 0)
                        token_stats(n + 1, 1)
                        token_stats(n + 1, 2)
                    split_s(n, 5)
                    if not last:
                        token_stats(n + 1, 3)
                        token_var(n + 1)
                    split_s(n, 6)
                    if not last:
                        token_diag(n + 1)
                    split_s(n, 7)
                    if not last:
                        scale_x(n + 1)
                        query_norm(n + 1)
                    split_s(n, 8)
                    split_s(n, 9)
                    if not last:
                        o_scale(n + 1, 0)
                        o_scale(n + 1, 1)
                    split_s(n, 10)
                    if not last:
                        o_scale(n + 1, 2)
                        o_scale(n + 1, 3)
                    split_s(n, 11)
                    if not last:
                        split_xr(n + 1, False)
                        o_mix(n + 1)
                        o_norm(n + 1)

                split_x(n0)
                for u in range(SUB):
                    token_stats(n0, u)
                token_var(n0)
                token_diag(n0)
                scale_x(n0)
                query_norm(n0)
                split_xr(n0, True)
                for u in range(SUB):
                    o_scale(n0, u)
                o_mix(n0)
                o_norm(n0)
                tile(n0, True, False)
                with dve.Fori(1, STRIPS - 1) as t:
                    tile(b * STRIPS + t, False, False)
                tile(n0 + STRIPS - 1, False, True)
                middle(n0 + STRIPS - 1)
                output(n0 + STRIPS - 1)
                stage_end(dve, b * STAGES + 7)


def kernel(**inputs):
    import numpy as _np
    import concourse.bacc as _bacc
    from concourse import mybir as _mybir
    from concourse.bass_utils import run_bass_kernel_spmd as _run

    def a(name):
        return _np.asarray(inputs[name])

    def rows(w):
        k = w.shape[0] // P
        return w.reshape(k, P, -1).transpose(1, 0, 2).reshape(P, -1)

    def cols(v):
        return v.reshape(-1, P).T

    def chunks(w):
        return w.reshape(-1, P, w.shape[-1]).transpose(1, 0, 2)

    x = a("x")
    arrays = dict(constants())
    arrays.update({
        "x": _np.pad(x, ((0, 0), (0, 0), (1, 1), (0, 0))),
        "fc1_w": rows(a("L1_conv_fc1_w")), "fc2_w": rows(a("L1_conv_fc2_w")),
        "qkv_w": rows(a("L1_conv_qkv_w")), "proj_w": rows(a("L1_conv_proj_w")),
        "fc1_b": cols(a("L1_conv_fc1_b")), "fc2_b": cols(a("L1_conv_fc2_b")), "proj_b": cols(a("L1_conv_proj_b")),
        "ln_g": cols(a("L1_conv_ln_g")), "ln_b": cols(a("L1_conv_ln_b")),
        "w_conv": _np.stack([chunks(a("L0_conv_w_" + n).reshape(C, 9)) for n in ("v", "q", "k", "off1")], 1),
        "b_conv": _np.stack([cols(a("L0_conv_b_" + n)) for n in ("v", "q", "k", "off1")], 1),
        "off_g": _np.tile(a("L0_conv_ln_g"), (TK, 1)), "off_b": _np.tile(a("L0_conv_ln_b"), (TK, 1)),
        "w_off2": _np.tile(a("L0_conv_w_off2")[None], (TK, 1, 1)),
        "w_outT": chunks(a("L0_conv_w_out").T),
    })
    nc = _bacc.Bacc("TRN2", target_bir_lowering=False, num_devices=1)
    feed, d = {}, {}
    for name, v in arrays.items():
        v = _np.ascontiguousarray(v)
        feed[f"in_{name}"] = v
        d[name] = nc.dram_tensor(f"in_{name}", v.shape, _mybir.dt.from_np(v.dtype), kind="ExternalInput").ap()
    out = nc.dram_tensor("out_0", x.shape, F32, kind="ExternalOutput").ap()
    build(nc, d, out)
    r = _run(nc, [feed], core_ids=[0])
    return r.results[0]["out_0"]
```

```python
import numpy as np
import concourse.bass as bass
from concourse import mybir
from contextlib import ExitStack

F32 = mybir.dt.float32
F32R = mybir.dt.float32r
I32 = mybir.dt.int32
ALU = mybir.AluOpType
ACT = mybir.ActivationFunctionType
AX = mybir.AxisListType

P = 128
C, H, W = 384, 56, 56
KC = C // P
L = H * W
STRIPS = 7
RS = H // STRIPS
T = RS * W
SUB = 4
TS = T // SUB
HK = WK = 28
SR = HK // STRIPS
TK = SR * WK
GROUPS = 32
CG = C // GROUPS
HC0 = 32
NH1, HD = 8, 48
HID = 4 * C
JC = HID // P
WIN = ((0, 144), (96, 288), (240, 384))
WOFF = (0, 144, 336)
WTOT = 480
TAPS = [(1, 1)] + [(ky, kx) for ky in range(3) for kx in range(3) if (ky, kx) != (1, 1)]
EPS_GN = 1e-5
EPS_LN = 1e-5


def constants():
    f = np.float32
    ch = np.arange(C)
    grp = (ch[:, None] // CG == ch[None, :] // CG).astype(f) / f(CG)
    head0 = (np.arange(P)[:, None] // HC0 == np.arange(P)[None, :] // HC0).astype(f) * f(HC0 ** -0.5)
    head1 = np.zeros((P, WTOT), f)
    for k, (lo, hi) in enumerate(WIN):
        same = (P * k + np.arange(P))[:, None] // HD == np.arange(lo, hi)[None, :] // HD
        head1[:, WOFF[k]:WOFF[k] + hi - lo] = same * f(1.0 / np.pi)
    hsel = (ch[:, None] // HD == np.arange(NH1)[None, :]).astype(f).reshape(KC, P, NH1).transpose(1, 0, 2)
    ref = (np.linspace(0.5, HK - 0.5, HK, dtype=f) / f(HK) * f(2) - f(1)).astype(f)
    ry, rx = np.meshgrid(ref, ref, indexing="ij")
    refp = np.stack([ry, rx], -1).reshape(STRIPS, TK, 2).transpose(1, 0, 2)
    edge = np.ones((P, 2, STRIPS), f)
    edge[:, 0, 0] = 0
    edge[:, 1, STRIPS - 1] = 0
    return {
        "ident": np.eye(P, dtype=f),
        "grp": grp.reshape(KC, P, C).transpose(1, 0, 2),
        "head0": head0, "head1": head1, "hsel": hsel, "refp": refp, "edge": edge,
    }


def build(nc, d, out):
    B = d["x"].shape[0]

    def scratch(name, shape):
        return nc.dram_tensor(name, shape, F32, kind="Internal").ap()

    x1_d = scratch("x1_scr", (B, C, L))
    q_d = scratch("q_scr", (C, L))
    pair_d = scratch("pair_scr", (L + 1, 2 * C))
    kt_d = scratch("kt_scr", (HK * WK, C))
    wkv_d = nc.dram_tensor("wkv_scr", (2, P, KC, 2 * C), F32, kind="Internal").ap()
    v1_d = scratch("v1_scr", (L, C))
    x1_v = x1_d.rearrange("b (k p) l -> b p k l", p=P)
    q_v = q_d.rearrange("(k p) l -> p k l", p=P)
    out_v = out.rearrange("b (k p) h w -> b p k (h w)", p=P)
    xin_v = d["x"].rearrange("b (k p) h w -> b p k h w", p=P)

    ctx = ExitStack()
    with ctx:
        def sem(name):
            return ctx.enter_context(nc.semaphore(name))

        top = [(nc.sbuf_base + 31) // 32 * 32]
        limit = nc.sbuf_usable_end

        def sb(name, shape, dt=F32, at=top):
            size = int(np.prod(shape[1:])) * 4
            t = nc.alloc_sbuf_tensor_at(name, shape, dt, offset=at[0])
            at[0] += (size + 31) // 32 * 32
            assert at[0] <= limit, (name, at[0], limit)
            return t

        W1H, W1L = sb("W1H", [P, KC, HID], F32R), sb("W1L", [P, KC, HID], F32R)
        W2H, W2L = sb("W2H", [P, JC, C], F32R), sb("W2L", [P, JC, C], F32R)
        WQH, WQL = sb("WQH", [P, KC, C], F32R), sb("WQL", [P, KC, C], F32R)
        WPH, WPL = sb("WPH", [P, KC, C], F32R), sb("WPL", [P, KC, C], F32R)
        ident = sb("ident_s", [P, P])
        head1 = sb("head1_s", [P, WTOT])
        hsel = sb("hsel_s", [P, KC, NH1])
        edge = sb("edge_s", [P, 2, STRIPS])
        wconv = sb("wconv", [P, 4, KC, 9])
        bconv = sb("bconv", [P, 4, KC])
        b1p, b1 = sb("b1p", [P, JC]), sb("b1", [P, JC])
        b2, bp = sb("b2", [P, KC]), sb("bp", [P, KC])
        lng, lnb = sb("lng", [P, KC]), sb("lnb", [P, KC])
        nhalf = sb("nhalf", [P, 32])
        gst, gmv = sb("gst", [P, KC, 2, 2]), sb("gmv", [P, KC, 2, 2])
        gdev, gvar, gmean = sb("gdev", [P, KC, 2, 2]), sb("gvar", [P, KC, 2]), sb("gmean", [P, KC, 2])
        coefA, coefB = sb("coefA", [P, KC, 2]), sb("coefB", [P, KC, 2])
        bst = sb("bst", [P, KC, 2, STRIPS, 6])
        refp, OFF, POS = sb("refp_s", [TK, STRIPS, 2]), sb("OFF", [TK, STRIPS, 2]), sb("POS", [TK, STRIPS, 2])
        FI, FF, FG = sb("FI", [TK, STRIPS, 2], I32), sb("FF", [TK, STRIPS, 2]), sb("FG", [TK, STRIPS, 2])
        WG, WN, W4 = sb("WG", [TK, STRIPS, 2]), sb("WN", [TK, STRIPS, 2]), sb("W4", [TK, STRIPS, 4])
        IXF, IX = sb("IXF", [TK, 2, STRIPS]), sb("IX", [TK, 2, STRIPS], I32)
        AB = sb("AB", [P, WTOT])
        shared = top[0]

        at = [shared]
        W2TH, W2TL = sb("W2TH", [P, KC, C], F32R, at=at), sb("W2TL", [P, KC, C], F32R, at=at)
        after_w2t = at[0]
        KT7 = sb("KT7", [TK, STRIPS, C], at=at)
        G7 = sb("G7", [TK, STRIPS, 2, 2, C], at=at)
        VS = sb("VS", [TK, 2, C], at=at)
        MT = sb("MT", [P, KC, P], at=at)
        woT, head0 = sb("woT", [P, KC, C], at=at), sb("head0_s", [P, P], at=at)

        at = [after_w2t]
        CQ, CX = sb("CQ", [P, 2, KC, T], at=at), sb("CX", [P, 2, KC, T], at=at)
        CH, CL = sb("CH", [P, KC, T], F32R, at=at), sb("CL", [P, KC, T], F32R, at=at)
        X0S = sb("X0S", [P, 2, KC, T], at=at)
        grp = sb("grp_s", [P, KC, C], at=at)
        ones = sb("ones", [P, P], at=at)
        WKVH, WKVL = sb("WKVH", [P, KC, 2 * C], F32R, at=at), sb("WKVL", [P, KC, 2 * C], F32R, at=at)
        wkv_at = at[0] - 2 * KC * 2 * C * 4
        zero = sb("zero", [P, P], at=at)
        after_zero = at[0]

        at = [shared]
        stg = [sb("stg0", [P, KC * HID], at=at), sb("stg1", [P, KC * HID], at=at)]
        assert at[0] <= wkv_at - (KC * C + P + 2 * KC * T) * 4

        at = [shared]
        X = sb("X", [P, KC, T], at=at)
        XH, XL = sb("XH", [P, KC, T], F32R, at=at), sb("XL", [P, KC, T], F32R, at=at)
        base1 = at[0]
        K1, V1 = sb("K1", [TS, SUB, C], at=at), sb("V1", [TS, SUB, C], at=at)
        KS = sb("KS", [TS, SUB, C], at=at)
        kn, rk = sb("kn", [TS, SUB * NH1], at=at), sb("rk", [TS, SUB * NH1], at=at)

        KA, OA = sb("KA", [P, KC, TK], at=at), sb("OA", [P, KC, TK], at=at)
        KT, LN = sb("KT", [TK, C], at=at), sb("LN", [TK, C], at=at)
        olng, olnb = sb("olng", [TK, C], at=at), sb("olnb", [TK, C], at=at)
        woff2, prod = sb("woff2", [TK, 2, C], at=at), sb("prod", [TK, 2, C], at=at)
        obn, oag, orv = sb("obn", [TK, 6], at=at), sb("oag", [TK, 2], at=at), sb("orv", [TK, 2], at=at)
        dot = sb("dot", [TK, 2], at=at)
        assert at[0] <= wkv_at

        at = [base1]
        XRH, XRL = sb("XRH", [P, KC, T], F32R, at=at), sb("XRL", [P, KC, T], F32R, at=at)
        Q = sb("Q", [P, KC, T], at=at)
        QQ = sb("QQ", [P, SUB * C], at=at)
        V = sb("V", [TS, SUB, C], at=at)
        OT = sb("OT", [P, KC, T], at=at)
        S = sb("S", [P, 2, T], at=at)
        SH, SL = sb("SH", [P, 3, T], F32R, at=at), sb("SL", [P, 3, T], F32R, at=at)
        MH = sb("MH", [P, KC, T], F32R, at=at)
        ML = sb("ML", [P, KC, T], F32R, at=at)
        Y = sb("Y", [P, KC, T], at=at)
        DH, DL = sb("DH", [TS, SUB, TS], F32R, at=at), sb("DL", [TS, SUB, TS], F32R, at=at)
        o1r = sb("o1r", [TS, P], F32R, at=at)
        xbn, xag = sb("xbn", [TS, SUB, 6], at=at), sb("xag", [TS, SUB, 2], at=at)
        rve, rr = sb("rve", [TS, SUB], at=at), sb("rr", [TS, SUB], at=at)
        rh, rl = sb("rh", [TS, SUB], F32R, at=at), sb("rl", [TS, SUB], at=at)
        qn, rq = sb("qn", [TS, SUB * NH1], at=at), sb("rq", [TS, SUB * NH1], at=at)
        on, ro = sb("on", [TS, SUB * NH1], at=at), sb("ro", [TS, SUB * NH1], at=at)
        OS = QQ[0:TS, :]

        assert at[0] >= after_zero
        XR = sb("XR", [P, KC, RS + 2, W], at=at)
        XG = sb("XG", [P, KC, RS + 2, W + 2], at=at)
        VA, QA = sb("VA", [P, KC, T], at=at), sb("QA", [P, KC, T], at=at)
        VT = sb("VT", [TS, 2, C], at=at)

        bank = [ctx.enter_context(nc.psum_tensor(f"bank{i}", [P, 512], F32)) for i in range(8)]

        stage_done = sem("stage_done")
        held = sem("held")
        names = """const_ld stg_ld0 stg_ld1 stg_h stg_used set_sum set_ctr set_bias set_ones set_ps set_bst pair_z wkv_st
            x0_ld0 x0_ld1 x0bn grp_ld gn_st gn_mm gn_s1 gn_d gn_dev gn_mm2 gn_v1 gn_v2 gn_rstd gn_nb gn_coef
            off_ld xr1_ld xg1 edged1 o0 k0 oa ka otp ktp kt_ev kt_st obn_s oag_s orv_s orr_s ln1 ln2 ln_s gelu dots off_put
            xr2_ld xg2 edged2 v0 q0 va qa vtp vt_ev q_st pair_st0 pair_st1
            offr tanh_s point w4s ixi
            b_ld vs_ch vs_s mt_mm mt_ev w2_mm w2_ev
            cq_ld0 cq_ld1 cx_ld0 cx_ld1 ch cl y0 x1a x1bn x1_st0 x1_st1 wkv_ld
            kv_ld kxs kxh kxl k_mm v_mm k_sq k_ev v_ev k_red k_rs k_hat v1_st at_mm ab_s
            x_ld v_ld y_ld y_st xs xh xl xt_mm bn_s ag_s rve_s rr_s rh_s rl_s dg rb_mm xsr xrh xrl
            q_mm q_ev qq qs_mm qn_s rq_s qa_mm o_sc o_mx o_sq o_red ro_s o_fin ot_mm ot_ev
            f1 s_s sh sl f2 mid mh ml pj y_s""".split()
        names += [f"gath{t}" for t in range(STRIPS)]
        s = {n: sem("s_" + n) for n in names}

        def slot_uses(t, slots):
            return len(range(t % slots, STRIPS, slots)), t // slots + 1

        def slot_at(b, t, slots, each):
            per, upto = slot_uses(t, slots)
            return b * (per * each) + upto * each

        HEAD = 16
        ahead = """otp ktp oa ka kt_ev kt_st dots off_put va qa vtp vt_ev q_st pair_st0 pair_st1
            at_mm k_hat v1_st k_ev v_ev s_s sl f2""".split()

        block = ctx.enter_context(nc.Block())

        def alone(eng):
            eng.sem_inc(held, 1)

        def stage_end(eng, n):
            alone(eng)
            eng.drain().then_inc(stage_done, 1)
            eng.wait_ge(stage_done, n * 5 + 5)
            alone(eng)

        STAGES = 5

        def stage(b, i):
            return b * STAGES + 3 + i

        def strip_px(t):
            return bass.ts(t, T)

        CONSTS = 12

        @block.sync
        def _(sp):
            for dst, src in [
                (ident, d["ident"]), (head1, d["head1"]), (hsel, d["hsel"]), (edge, d["edge"]),
                (b1, d["fc1_b"]), (b2, d["fc2_b"]), (bp, d["proj_b"]), (lng, d["ln_g"]), (lnb, d["ln_b"]),
                (wconv, d["w_conv"]), (bconv, d["b_conv"]), (refp, d["refp"]),
            ]:
                sp.dma_start(dst.ap(), src).then_inc(s["const_ld"], 16)
            def stage_weights(i):
                name, cols = (("fc1_w", KC * HID), ("fc2_w", JC * C), ("qkv_w", KC * 3 * C), ("proj_w", KC * C))[i]
                if i >= 2:
                    sp.wait_ge(s["stg_used"], i - 1)
                sp.dma_start(stg[i % 2][:, 0:cols], d[name]).then_inc(s[f"stg_ld{i % 2}"], 16)

            def load_x0(g, t):
                if t >= 2:
                    sp.wait_ge(s["x0bn"], g * STRIPS + t - 1)
                sp.dma_start(X0S[:, t % 2, :, :].rearrange("p k (r w) -> p k r w", w=W),
                             xin_v[g, :, :, 1 + t * RS:1 + (t + 1) * RS, :]).then_inc(s[f"x0_ld{t % 2}"], 16)

            stage_weights(0)
            stage_weights(1)
            sp.dma_start(grp[:, :, :], d["grp"]).then_inc(s["grp_ld"], 16)
            load_x0(0, 0)
            load_x0(0, 1)
            sp.wait_ge(s["set_ones"], 1)
            sp.dma_start(pair_d[0, 0:C].rearrange("(a c) -> a c", a=3), zero[0:3, :]).then_inc(s["pair_z"], 16)
            sp.dma_start(pair_d[L, C:2 * C].rearrange("(a c) -> a c", a=3), zero[0:3, :]).then_inc(s["pair_z"], 16)
            stage_weights(2)
            stage_weights(3)
            for t in range(2, STRIPS):
                load_x0(0, t)
            sp.wait_ge(s["stg_used"], 3)
            sp.dma_start(wkv_d[0], WKVH[:, :, :].bitcast(F32)).then_inc(s["wkv_st"], 16)
            sp.dma_start(wkv_d[1], WKVL[:, :, :].bitcast(F32)).then_inc(s["wkv_st"], 16)
            sp.wait_ge(s["wkv_st"], 32)
            sp.wait_ge(s["pair_z"], 32)
            stage_end(sp, 0)

            def load_offset_tables():
                for dst, src in ((olng[:, :], d["off_g"]), (olnb[:, :], d["off_b"]), (woff2[:, :, :], d["w_off2"])):
                    sp.dma_start(dst, src).then_inc(s["off_ld"], 16)

            def load_strip(g, t, which):
                sp.dma_start(XR[:, :, :, :], xin_v[g, :, :, bass.ds(t * RS, RS + 2), :]).then_inc(s[f"xr{which}_ld"], 16)

            def strip_read(m, which):
                sp.wait_ge(s[f"xg{which}"], m * KC + KC)

            def store_keys(t, m):
                sp.wait_ge(s["kt_ev"], HEAD + m + 1)
                sp.dma_start(kt_d[bass.ts(t, TK), :], KT[:, :]).then_inc(s["kt_st"], 16)

            def store_values(t, m):
                for u in range(SUB):
                    sp.wait_ge(s["vt_ev"], HEAD + m * SUB + u + 1)
                    for half in range(2):
                        sp.dma_start(pair_d[bass.ds(t * T + (u * TS + 1 - half), TS), half * C:(half + 1) * C],
                                     VT[:, u % 2, :]).then_inc(s[f"pair_st{u % 2}"], 16)

            def store_queries(t, m):
                sp.wait_ge(s["qa"], HEAD + m * 24 + 24)
                alone(sp)
                sp.dma_start(q_v[:, :, strip_px(t)], QA[:, :, :]).then_inc(s["q_st"], 16)

            load_offset_tables()
            load_strip(0, 0, 1)
            with sp.Fori(0, STRIPS - 1) as t:
                strip_read(t, 1)
                load_strip(0, t + 1, 1)
                store_keys(t, t)
            store_keys(STRIPS - 1, STRIPS - 1)
            sp.wait_ge(s["kt_st"], HEAD + 16 * STRIPS)
            stage_end(sp, 1)
            load_strip(0, 0, 2)
            with sp.Fori(0, STRIPS - 1) as t:
                strip_read(t, 2)
                load_strip(0, t + 1, 2)
                store_values(t, t)
                store_queries(t, t)
            store_values(STRIPS - 1, STRIPS - 1)
            store_queries(STRIPS - 1, STRIPS - 1)

            def front_stored(g):
                sp.wait_ge(s["q_st"], HEAD + (g + 1) * (16 * STRIPS))
                sp.wait_ge(s["pair_st0"], HEAD + (g + 1) * (64 * STRIPS))
                sp.wait_ge(s["pair_st1"], HEAD + (g + 1) * (64 * STRIPS))

            front_stored(0)
            stage_end(sp, 2)

            def image(b, nxt):
                for dst, src in [(KT7[:, :, :], kt_d.rearrange("(t p) c -> p t c", p=TK)), (woT[:, :, :], d["w_outT"]),
                                 (head0[:, :], d["head0"])]:
                    sp.dma_start(dst, src).then_inc(s["b_ld"], 16)
                stage_end(sp, stage(b, 0))
                sp.dma_start(grp[:, :, :], d["grp"]).then_inc(s["grp_ld"], 16)
                for t in range(STRIPS):
                    if t >= 2:
                        sp.wait_ge(s["cl"], b * STRIPS + t - 1)
                    sp.dma_start(CQ[:, t % 2, :, :], q_v[:, :, t * T:(t + 1) * T]).then_inc(s[f"cq_ld{t % 2}"], 16)
                    if t >= 2:
                        sp.wait_ge(s[f"x1_st{t % 2}"], slot_at(b, t - 2, 2, 16))
                        alone(sp)
                        sp.wait_ge(s["x1bn"], b * STRIPS + t - 1)
                    sp.dma_start(CX[:, t % 2, :, :].rearrange("p k (r w) -> p k r w", w=W),
                                 xin_v[b, :, :, 1 + t * RS:1 + (t + 1) * RS, :]).then_inc(s[f"cx_ld{t % 2}"], 16)
                    if nxt:
                        load_x0(b + 1, t)
                    if t == 1:
                        sp.dma_start(WKVH[:, :, :].bitcast(F32), wkv_d[0]).then_inc(s["wkv_ld"], 16)
                        sp.dma_start(WKVL[:, :, :].bitcast(F32), wkv_d[1]).then_inc(s["wkv_ld"], 16)
                    if t >= 1:
                        sp.wait_ge(s["x1a"], (b * STRIPS + t) * KC)
                        sp.dma_start(x1_v[b, :, :, (t - 1) * T:t * T], CX[:, (t - 1) % 2, :, :]).then_inc(s[f"x1_st{(t - 1) % 2}"], 16)
                sp.wait_ge(s["x1a"], (b * STRIPS + STRIPS) * KC)
                sp.dma_start(x1_v[b, :, :, (STRIPS - 1) * T:L], CX[:, (STRIPS - 1) % 2, :, :]).then_inc(s[f"x1_st{(STRIPS - 1) % 2}"], 16)
                for t in range(STRIPS - 2, STRIPS):
                    sp.wait_ge(s[f"x1_st{t % 2}"], slot_at(b, t, 2, 16))
                    alone(sp)
                stage_end(sp, stage(b, 1))
                n0 = b * STRIPS
                sp.dma_start(X[:, :, :], x1_v[b, :, :, 0:T]).then_inc(s["kv_ld"], 16)
                if nxt:
                    load_strip(b + 1, 0, 1)
                    load_offset_tables()

                def store_v1(t, n):
                    sp.wait_ge(s["v_ev"], HEAD + n * SUB + SUB)
                    sp.dma_start(v1_d[bass.ts(t, T), :].rearrange("(s p) c -> p s c", p=TS), V1[:, :, :]).then_inc(s["v1_st"], 16)

                with sp.Fori(0, STRIPS - 1) as t:
                    n = b * STRIPS + t
                    sp.wait_ge(s["kxl"], n + 1)
                    sp.dma_start(X[:, :, :], x1_v[b, :, :, strip_px(t + 1)]).then_inc(s["kv_ld"], 16)
                    if nxt:
                        strip_read(n + STRIPS, 1)
                        load_strip(b + 1, t + 1, 1)
                    store_v1(t, n)
                    if nxt:
                        store_keys(t, n + STRIPS)
                store_v1(STRIPS - 1, n0 + STRIPS - 1)
                sp.wait_ge(s["v1_st"], HEAD + (b + 1) * (16 * STRIPS))
                alone(sp)
                if nxt:
                    store_keys(STRIPS - 1, n0 + (2 * STRIPS - 1))
                    sp.wait_ge(s["kt_st"], HEAD + (b + 2) * (16 * STRIPS))
                stage_end(sp, stage(b, 2))
                stage_end(sp, stage(b, 3))

                def load_pre(t):
                    sp.dma_start(X[:, :, :], x1_v[b, :, :, strip_px(t)]).then_inc(s["x_ld"], 16)

                def load_v(t):
                    sp.dma_start(V[:, :, :], v1_d[bass.ts(t, T), :].rearrange("(s p) c -> p s c", p=TS)).then_inc(s["v_ld"], 16)

                def load_res(t):
                    sp.dma_start(Y[:, :, :], x1_v[b, :, :, strip_px(t)]).then_inc(s["y_ld"], 16)

                def store_out(t, n):
                    sp.wait_ge(s["y_s"], n * KC + KC)
                    sp.dma_start(out_v[b, :, :, strip_px(t)], Y[:, :, :]).then_inc(s["y_st"], 16)

                load_pre(0)
                load_v(0)
                load_res(0)
                if nxt:
                    load_strip(b + 1, 0, 2)
                sp.wait_ge(s["xrl"], n0 + 1)
                load_pre(1)
                if nxt:
                    strip_read(n0 + STRIPS, 2)
                    load_strip(b + 1, 1, 2)
                sp.wait_ge(s["ot_mm"], n0 * KC + KC)
                load_v(1)
                if nxt:
                    store_values(0, n0 + STRIPS)
                with sp.Fori(1, STRIPS - 1) as t:
                    n = b * STRIPS + t
                    if nxt:
                        store_queries(t - 1, n + (STRIPS - 1))
                    sp.wait_ge(s["xrl"], n + 1)
                    load_pre(t + 1)
                    if nxt:
                        strip_read(n + STRIPS, 2)
                        load_strip(b + 1, t + 1, 2)
                    store_out(t - 1, n - 1)
                    sp.wait_ge(s["y_st"], n * 16)
                    load_res(t)
                    sp.wait_ge(s["ot_mm"], n * KC + KC)
                    load_v(t + 1)
                    if nxt:
                        store_values(t, n + STRIPS)
                nl = n0 + STRIPS - 1
                if nxt:
                    store_queries(STRIPS - 2, nl + STRIPS - 1)
                store_out(STRIPS - 2, nl - 1)
                sp.wait_ge(s["y_st"], nl * 16)
                load_res(STRIPS - 1)
                if nxt:
                    store_values(STRIPS - 1, nl + STRIPS)
                    store_queries(STRIPS - 1, nl + STRIPS)
                store_out(STRIPS - 1, nl)
                sp.wait_ge(s["y_st"], nl * 16 + 16)
                if nxt:
                    front_stored(b + 1)
                stage_end(sp, stage(b, 4))

            with sp.Fori(0, B - 1) as b:
                image(b, True)
            image(B - 1, False)

        @block.gpsimd
        def _(pool):
            for name in ahead:
                pool.sem_inc(s[name], HEAD)
            pool.memset(nhalf[:, :], -0.5)
            pool.memset(ones[:, :], 1.0 / C)
            pool.memset(zero[:, :], 0.0).then_inc(s["set_ones"], 1)

            def gn_rstd(g):
                pool.wait_ge(s["gn_v2"], g + 1)
                pool.tensor_tensor(gvar[:, :, :].rearrange("p k s -> p (k s)"), gvar[:, :, :].rearrange("p k s -> p (k s)"),
                                   nhalf[:, 0:2 * KC], ALU.pow).then_inc(s["gn_rstd"], 1)

            def offset_rstd(m):
                pool.wait_ge(s["orv_s"], m + 1)
                pool.tensor_tensor(orv[:, 1:2], orv[:, 0:1], nhalf[0:TK, 0:1], ALU.pow).then_inc(s["orr_s"], 1)

            def gather(g):
                pool.wait_ge(s["ixi"], g + 1)
                alone(pool)
                for t in range(STRIPS):
                    for r in range(2):
                        pool.indirect_dma_start(
                            out=G7[:, t, r, :, :].rearrange("p a c -> p (a c)"), out_offset=None,
                            in_=pair_d, in_offset=bass.IndirectOffsetOnAxis(ap=IX[:, r, t:t + 1], axis=0),
                        ).then_inc(s[f"gath{t}"], 16)
                for t in range(STRIPS):
                    pool.wait_ge(s[f"gath{t}"], g * 32 + 32)
                    alone(pool)

            gn_rstd(0)
            stage_end(pool, 0)
            with pool.Fori(0, STRIPS) as t:
                offset_rstd(t)
            stage_end(pool, 1)
            stage_end(pool, 2)

            def image(b, nxt):
                gather(b)
                stage_end(pool, stage(b, 0))
                pool.memset(zero[:, :], 0.0)
                gn_rstd(b + 1)
                stage_end(pool, stage(b, 1))
                with pool.Fori(0, STRIPS) as t:
                    n = b * STRIPS + t
                    for h, (lo, hi) in enumerate(((0, 24), (24, 32))):
                        pool.wait_ge(s["k_red"], n * 2 + h + 1)
                        pool.tensor_tensor(rk[:, lo:hi], kn[:, lo:hi], nhalf[0:TS, lo:hi], ALU.pow).then_inc(s["k_rs"], 1)
                    if nxt:
                        offset_rstd(n + STRIPS)
                stage_end(pool, stage(b, 2))
                stage_end(pool, stage(b, 3))
                with pool.Fori(0, STRIPS) as t:
                    n = b * STRIPS + t
                    pool.wait_ge(s["rve_s"], n + 1)
                    pool.tensor_tensor(rr[:, :], rve[:, :], nhalf[0:TS, 0:SUB], ALU.pow).then_inc(s["rr_s"], 1)
                    pool.wait_ge(s["qn_s"], n + 1)
                    pool.tensor_tensor(rq[:, :], qn[:, :], nhalf[0:TS, :], ALU.pow).then_inc(s["rq_s"], 1)
                    pool.wait_ge(s["o_red"], n + 1)
                    pool.tensor_tensor(ro[:, :], on[:, :], nhalf[0:TS, :], ALU.pow).then_inc(s["ro_s"], 1)
                stage_end(pool, stage(b, 4))

            with pool.Fori(0, B - 1) as b:
                image(b, True)
            image(B - 1, False)

        @block.tensor
        def _(pe):
            mm, tr = pe.matmul, pe.transpose

            pe.wait_ge(s["const_ld"], CONSTS * 16)
            pe.wait_ge(s["stg_ld0"], 16)
            pe.wait_ge(s["set_ones"], 1)
            for j in range(JC):
                for k in range(KC):
                    last = mm(bank[0][:, j:j + 1], stg[0][:, k * HID + j * P:k * HID + (j + 1) * P], lnb[:, k:k + 1],
                              start=(k == 0), stop=(k == KC - 1))
            last.then_inc(s["set_ps"], 1)
            pe.wait_ge(s["set_sum"], 1)
            for q in range(3):
                for k in range(KC):
                    last = mm(bank[1 + q][:, :], ones[:, :], stg[0][:, k * HID + q * 512:k * HID + (q + 1) * 512],
                              start=(k == 0), stop=(k == KC - 1))
            last.then_inc(s["set_ps"], 1)

            def gn_groups(g):
                pe.wait_ge(s["grp_ld"], g * 16 + 16)
                pe.wait_ge(s["gn_st"], g + 1)
                for ko in range(KC):
                    for ki in range(KC):
                        last = mm(bank[0][:, 4 * ko:4 * ko + 4], grp[:, ki, ko * P:(ko + 1) * P],
                                  gst[:, ki, :, :].rearrange("p s c -> p (s c)"), start=(ki == 0), stop=(ki == KC - 1))
                last.then_inc(s["gn_mm"], 1)
                pe.wait_ge(s["gn_dev"], g + 1)
                for ko in range(KC):
                    for ki in range(KC):
                        last = mm(bank[1][:, 4 * ko:4 * ko + 4], grp[:, ki, ko * P:(ko + 1) * P],
                                  gdev[:, ki, :, :].rearrange("p s c -> p (s c)"), start=(ki == 0), stop=(ki == KC - 1))
                last.then_inc(s["gn_mm2"], 1)

            def three_pass(o, wh, wl, xh, xl, first, stop):
                mm(o, wh, xh, start=first, stop=False)
                mm(o, wh, xl, start=False, stop=False)
                return mm(o, wl, xh, start=False, stop=stop)

            def turn_offset(m):
                pe.wait_ge(s["oa"], HEAD + m * 24 + 24)
                pe.wait_ge(s["kt_ev"], HEAD + m)
                for k in range(KC):
                    last = tr(bank[7][0:TK, k * P:(k + 1) * P], OA[:, k, :], ident[:, :])
                last.then_inc(s["otp"], 1)

            def turn_keys(m):
                pe.wait_ge(s["ka"], HEAD + m * 24 + 24)
                pe.wait_ge(s["ln1"], m + 1)
                for k in range(KC):
                    last = tr(bank[7][0:TK, k * P:(k + 1) * P], KA[:, k, :], ident[:, :])
                last.then_inc(s["ktp"], 1)

            VTB = (6, 7, 5, 6)

            def turn_values(m, u):
                if u == 0:
                    pe.wait_ge(s["va"], HEAD + m * 24 + 24)
                if u == 3:
                    pe.wait_ge(s["vt_ev"], HEAD + m * SUB + 1)
                for k in range(KC):
                    last = tr(bank[VTB[u]][0:TS, k * P:(k + 1) * P], VA[:, k, u * TS:(u + 1) * TS], ident[:, :])
                last.then_inc(s["vtp"], 1)

            gn_groups(0)
            stage_end(pe, 0)
            with pe.Fori(0, STRIPS) as t:
                turn_offset(t)
                turn_keys(t)
            stage_end(pe, 1)
            with pe.Fori(0, STRIPS) as t:
                pe.wait_ge(s["vt_ev"], HEAD + t * SUB)
                for u in range(SUB):
                    turn_values(t, u)
            stage_end(pe, 2)

            def image(b, nxt):
                pe.wait_ge(s["b_ld"], b * 48 + 48)
                for t in range(STRIPS):
                    pe.wait_ge(s["vs_s"], b * STRIPS + t + 1)
                    for k in range(KC):
                        last = mm(bank[k][:, 0:P], VS[:, t % 2, k * P:(k + 1) * P], KT7[:, t, k * P:(k + 1) * P],
                                  start=(t == 0), stop=(t == STRIPS - 1))
                    last.then_inc(s["mt_mm"], 1)
                pe.wait_ge(s["mt_ev"], b + 1)
                for k in range(KC):
                    last = mm(bank[3 + k][:, 0:C], MT[:, k, :], woT[:, k, :], start=True, stop=True)
                last.then_inc(s["w2_mm"], 1)
                stage_end(pe, stage(b, 0))
                for t in range(STRIPS):
                    pe.wait_ge(s["cl"], b * STRIPS + t + 1)
                    pe.wait_ge(s["ch"], b * STRIPS + t + 1)
                    for o in range(KC):
                        if t >= 2:
                            pe.wait_ge(s["x1a"], (b * STRIPS + t - 2) * KC + o + 1)
                        p = bank[2 + 3 * (t % 2) + o][:, 0:T]
                        for k in range(KC):
                            last = three_pass(p, W2TH[:, k, o * P:(o + 1) * P], W2TL[:, k, o * P:(o + 1) * P],
                                              CH[:, k, :], CL[:, k, :], k == 0, k == KC - 1)
                        last.then_inc(s["y0"], 1)
                gn_groups(b + 1)
                stage_end(pe, stage(b, 1))

                KB, VB, ATB = (0, 1, 2), (3, 4, 5), 6
                mm(bank[ATB][:, 0:WTOT], zero[:, :], head1[:, :], start=True, stop=False, skip_group_check=True)

                def kv(n, u):
                    if u == 0:
                        pe.wait_ge(s["kxl"], n + 1)
                        pe.wait_ge(s["kxh"], n + 1)
                    for bk, c0, free, sg in ((KB, 0, "k_ev", "k_mm"), (VB, C, "v_ev", "v_mm")):
                        if u == 3:
                            pe.wait_ge(s[free], HEAD + n * SUB + 1)
                        elif u == 0:
                            pe.wait_ge(s[free], HEAD + n * SUB)
                        p = bank[bk[u % 3]][0:TS, 0:C]
                        for k in range(KC):
                            xh, xl = XH[:, k, u * TS:(u + 1) * TS], XL[:, k, u * TS:(u + 1) * TS]
                            mm(p, xh, WKVH[:, k, c0:c0 + C], start=(k == 0), stop=False)
                            mm(p, xh, WKVL[:, k, c0:c0 + C], start=False, stop=False)
                            last = mm(p, xl, WKVH[:, k, c0:c0 + C], start=False, stop=(k == KC - 1))
                        last.then_inc(s[sg], 1)

                def state(n):
                    pe.wait_ge(s["k_hat"], HEAD + n * 2 + 2)
                    pe.wait_ge(s["v_ev"], HEAD + n * SUB + SUB)
                    for u in range(SUB):
                        for k, (lo, hi) in enumerate(WIN):
                            last = mm(bank[ATB][:, WOFF[k]:WOFF[k] + hi - lo], K1[:, u, k * P:(k + 1) * P], V1[:, u, lo:hi],
                                      start=False, stop=False, skip_group_check=True)
                    last.then_inc(s["at_mm"], 1)

                n0 = b * STRIPS

                def kv_tile(n, first):
                    kv(n, 0)
                    kv(n, 1)
                    kv(n, 2)
                    if not first:
                        state(n - 1)
                    if nxt:
                        turn_offset(n + STRIPS)
                    kv(n, 3)
                    if nxt:
                        turn_keys(n + STRIPS)

                pe.wait_ge(s["wkv_ld"], b * 32 + 32)
                kv_tile(n0, True)
                with pe.Fori(1, STRIPS) as t:
                    kv_tile(b * STRIPS + t, False)
                state(n0 + STRIPS - 1)
                stage_end(pe, stage(b, 2))
                stage_end(pe, stage(b, 3))

                CB = (5, 6, 7)

                def turn_x(n, u):
                    if u == 0:
                        pe.wait_ge(s["xs"], n * KC + KC)
                    if u == 3:
                        pe.wait_ge(s["bn_s"], n * SUB + 1)
                    for k in range(KC):
                        last = tr(bank[CB[u % 3]][0:TS, k * P:(k + 1) * P], X[:, k, u * TS:(u + 1) * TS], ident[:, :])
                    last.then_inc(s["xt_mm"], 1)

                def query(n, o):
                    if o == 0:
                        pe.wait_ge(s["xl"], n + 1)
                        pe.wait_ge(s["xh"], n + 1)
                        pe.wait_ge(s["bn_s"], n * SUB + 2)
                    if o == 1:
                        pe.wait_ge(s["bn_s"], n * SUB + 3)
                    if o == 2:
                        pe.wait_ge(s["bn_s"], n * SUB + 4)
                    p = bank[(6, 7, 5)[o]][:, 0:T]
                    for k in range(KC):
                        last = three_pass(p, WQH[:, k, o * P:(o + 1) * P], WQL[:, k, o * P:(o + 1) * P],
                                          XH[:, k, :], XL[:, k, :], k == 0, k == KC - 1)
                    last.then_inc(s["q_mm"], 1)

                def spread_r(n):
                    pe.wait_ge(s["dg"], n * 2 + 2)
                    pe.wait_ge(s["q_ev"], n * KC + 1)
                    pe.wait_ge(s["qq"], n * KC + 1)
                    for u in range(SUB):
                        mm(bank[6][:, u * TS:(u + 1) * TS], o1r[:, :], DH[:, u, :], start=True, stop=False)
                        last = mm(bank[6][:, u * TS:(u + 1) * TS], o1r[:, :], DL[:, u, :], start=False, stop=True)
                    last.then_inc(s["rb_mm"], 1)

                def query_norms(n):
                    pe.wait_ge(s["q_ev"], n * KC + 2)
                    pe.wait_ge(s["qq"], n * KC + KC)
                    for u in range(SUB):
                        for k in range(KC):
                            last = mm(bank[7][0:TS, u * NH1:(u + 1) * NH1], QQ[:, k * T + u * TS:k * T + (u + 1) * TS],
                                      hsel[:, k, :], start=(k == 0), stop=(k == KC - 1))
                    last.then_inc(s["qs_mm"], 1)

                def attend(n, u):
                    if u == 0:
                        pe.wait_ge(s["q_ev"], n * KC + KC)
                    if u == 1:
                        pe.wait_ge(s["xsr"], n + 1)
                    if u == 2:
                        pe.wait_ge(s["qn_s"], n + 1)
                    if u == 3:
                        pe.wait_ge(s["o_sc"], n * SUB + 1)
                    p = bank[(5, 6, 7, 5)[u]]
                    for k, (lo, hi) in enumerate(WIN):
                        last = mm(p[0:TS, lo:hi], Q[:, k, u * TS:(u + 1) * TS], AB[:, WOFF[k]:WOFF[k] + hi - lo],
                                  start=(k == 0), stop=(k == KC - 1), skip_group_check=True)
                    last.then_inc(s["qa_mm"], 1)

                def fc1(n, j):
                    if j == 0:
                        pe.wait_ge(s["xrl"], n + 1)
                        pe.wait_ge(s["xrh"], n + 1)
                    pe.wait_ge(s["s_s"], HEAD + n * JC + (j - 1))
                    p = bank[j % 2][:, 0:T]
                    for k in range(KC):
                        last = three_pass(p, W1H[:, k, j * P:(j + 1) * P], W1L[:, k, j * P:(j + 1) * P],
                                          XRH[:, k, :], XRL[:, k, :], k == 0, k == KC - 1)
                    last.then_inc(s["f1"], 1)

                def fc2(n, j, first):
                    pe.wait_ge(s["sl"], HEAD + n * JC + j + 1)
                    pe.wait_ge(s["sh"], n * JC + j + 1)
                    if j == 0 and not first:
                        pe.wait_ge(s["mid"], n * KC)
                    for o in range(KC):
                        last = three_pass(bank[2 + o][:, 0:T], W2H[:, j, o * P:(o + 1) * P], W2L[:, j, o * P:(o + 1) * P],
                                          SH[:, j % 3, :], SL[:, j % 3, :], j == 0, j == JC - 1)
                    last.then_inc(s["f2"], 1)

                def proj(n):
                    pe.wait_ge(s["mh"], n + 1)
                    pe.wait_ge(s["ml"], n + 1)
                    for o in range(KC):
                        p = bank[CB[o]][:, 0:T]
                        for k in range(KC):
                            last = three_pass(p, WPH[:, k, o * P:(o + 1) * P], WPL[:, k, o * P:(o + 1) * P],
                                              MH[:, k, :], ML[:, k, :], k == 0, k == KC - 1)
                        last.then_inc(s["pj"], 1)

                def turn_o(n, prev):
                    pe.wait_ge(s["o_fin"], n + 1)
                    for k in range(KC):
                        if prev:
                            pe.wait_ge(s["y_s"], (n - 1) * KC + k + 1)
                        for u in range(SUB):
                            last = tr(bank[CB[k]][:, u * TS:(u + 1) * TS], V[:, u, k * P:(k + 1) * P], ident[0:TS, 0:TS])
                        last.then_inc(s["ot_mm"], 1)

                def pre(n, step):
                    if step == 1:
                        pe.wait_ge(s["xs"], n * KC + KC)
                        turn_x(n, 0)
                        turn_x(n, 1)
                        turn_x(n, 2)
                    elif step == 2:
                        turn_x(n, 3)
                        query(n, 0)
                    elif step == 3:
                        query(n, 1)
                        query(n, 2)
                    elif step == 4:
                        spread_r(n)
                        query_norms(n)
                    elif step == 5:
                        attend(n, 0)
                        attend(n, 1)
                    elif step == 6:
                        attend(n, 2)
                        attend(n, 3)

                def tile(n, first, last):
                    fc1(n, 0)
                    fc1(n, 1)
                    fc1(n, 2)
                    if not first:
                        pe.wait_ge(s["o_sc"], n * SUB + SUB)
                        if nxt:
                            pe.wait_ge(s["vt_ev"], HEAD + (n + (STRIPS - 1)) * SUB + SUB)
                        proj(n - 1)
                    fc2(n, 0, first)
                    fc1(n, 3)
                    if first:
                        pe.wait_ge(s["o_sc"], n * SUB + SUB)
                    turn_o(n, not first)
                    fc2(n, 1, first)
                    fc1(n, 4)
                    if not last:
                        pe.wait_ge(s["ot_ev"], n * KC + KC)
                        pre(n + 1, 1)
                    fc2(n, 2, first)
                    fc1(n, 5)
                    for i in range(3, JC):
                        if not last and 2 <= i - 1 <= 6:
                            pre(n + 1, i - 1)
                        fc2(n, i, first)
                        if i + 3 < JC:
                            fc1(n, i + 3)
                        if nxt and i == 9:
                            if last:
                                pe.wait_ge(s["ot_ev"], n * KC + KC)
                            else:
                                pe.wait_ge(s["o_sc"], (n + 1) * SUB + SUB)
                            for u in range(3):
                                turn_values(n + STRIPS, u)
                        if nxt and i == 10:
                            turn_values(n + STRIPS, 3)

                for step in range(1, 7):
                    pre(n0, step)
                tile(n0, True, False)
                with pe.Fori(1, STRIPS - 1) as t:
                    tile(b * STRIPS + t, False, False)
                tile(n0 + STRIPS - 1, False, True)
                pe.wait_ge(s["ot_ev"], (n0 + STRIPS) * KC)
                if nxt:
                    pe.wait_ge(s["vt_ev"], HEAD + (n0 + 2 * STRIPS) * SUB)
                proj(n0 + STRIPS - 1)
                stage_end(pe, stage(b, 4))

            with pe.Fori(0, B - 1) as b:
                image(b, True)
            image(B - 1, False)

        @block.scalar
        def _(act):
            fn = act.activation
            act.wait_ge(s["const_ld"], CONSTS * 16)

            def lead(dst, src):
                fn(dst, src, ACT.Copy).then_inc(s["stg_h"], 1)

            act.wait_ge(s["set_ctr"], 2)
            lead(W1H[:, :, :], stg[0][:, :].rearrange("p (k n) -> p k n", k=KC))
            act.wait_ge(s["stg_ld1"], 16)
            lead(W2H[:, :, :], stg[1][:, :].rearrange("p (k n) -> p k n", k=JC))
            act.wait_ge(s["stg_ld0"], 32)
            qkv = stg[0][:, 0:KC * 3 * C].rearrange("p (k n) -> p k n", k=KC)
            lead(WQH[:, :, :], qkv[:, :, 0:C])
            lead(WKVH[:, :, :], qkv[:, :, C:3 * C])
            act.wait_ge(s["stg_ld1"], 32)
            lead(WPH[:, :, :], stg[1][:, 0:KC * C].rearrange("p (k n) -> p k n", k=KC))
            stage_end(act, 0)

            def normalise(m, which, accs):
                act.wait_ge(s[f"xr{which}_ld"], m * 16 + 16)
                for acc in accs:
                    act.wait_ge(s[acc], HEAD + m * 24)
                for k in range(KC):
                    fn(XG[:, k, :, 1:W + 1], XR[:, k, :, :], ACT.Identity, bias=coefB[:, k, 0:1],
                       scale=coefA[:, k, 0:1]).then_inc(s[f"xg{which}"], 1)

            def centre_tap(m, acc, conv, st, which, used, value, sg):
                rows, cols = (RS, W) if st == 1 else (SR, WK)
                act.wait_ge(s[used], value)
                for k in range(KC):
                    act.wait_ge(s[f"xg{which}"], m * KC + k + 1)
                    fn(acc[:, k, :].rearrange("p (r w) -> p r w", w=cols),
                       XG[:, k, 1:2 + st * (rows - 1):st, 1:2 + st * (cols - 1):st],
                       ACT.Identity, bias=bconv[:, conv, k:k + 1], scale=wconv[:, conv, k, 4:5]).then_inc(s[sg], 1)

            def keys_start(m):
                normalise(m, 1, ("oa", "ka"))
                centre_tap(m, OA, 3, 2, 1, "otp", HEAD + m, "o0")
                centre_tap(m, KA, 2, 2, 1, "ktp", HEAD + m, "k0")

            def offset_gelu(m):
                act.wait_ge(s["ln_s"], m + 1)
                fn(LN[:, :], LN[:, :], ACT.Gelu).then_inc(s["gelu"], 1)

            def keys_out(m):
                act.wait_ge(s["ktp"], HEAD + m + 1)
                act.wait_ge(s["kt_st"], HEAD + m * 16)
                fn(KT[:, :], bank[7][0:TK, 0:C], ACT.Copy).then_inc(s["kt_ev"], 1)

            def values_start(m):
                centre_tap(m, VA, 0, 1, 2, "vtp", HEAD + m * SUB, "v0")

            def queries_start(m):
                centre_tap(m, QA, 1, 1, 2, "q_st", HEAD + m * 16, "q0")

            def values_out(m, u):
                act.wait_ge(s["vtp"], HEAD + m * SUB + u + 1)
                act.wait_ge(s[f"pair_st{u % 2}"], HEAD + m * 64 + (u // 2) * 32)
                fn(VT[:, u % 2, :], bank[(6, 7, 5, 6)[u]][0:TS, 0:C], ACT.Copy).then_inc(s["vt_ev"], 1)

            def tanh(g):
                act.wait_ge(s["offr"], g + 1)
                fn(POS[:, :, :], OFF[:, :, :], ACT.Tanh).then_inc(s["tanh_s"], 1)

            with act.Fori(0, STRIPS) as t:
                keys_start(t)
                offset_gelu(t)
                keys_out(t)
            stage_end(act, 1)
            tanh(0)
            with act.Fori(0, STRIPS) as t:
                normalise(t, 2, ("va", "qa"))
                values_start(t)
                queries_start(t)
                for u in range(SUB):
                    values_out(t, u)
            stage_end(act, 2)

            def image(b, nxt):
                stage_end(act, stage(b, 0))
                for t in range(STRIPS):
                    act.wait_ge(s[f"cq_ld{t % 2}"], slot_at(b, t, 2, 16))
                    if t >= 1:
                        act.wait_ge(s["y0"], (b * STRIPS + t) * KC)
                    fn(CH[:, :, :], CQ[:, t % 2, :, :], ACT.Copy).then_inc(s["ch"], 1)
                stage_end(act, stage(b, 1))

                def norm_in(n, ld, sg):
                    act.wait_ge(s[ld], n * 16 + 16)
                    for k in range(KC):
                        fn(X[:, k, :], X[:, k, :], ACT.Identity, bias=coefB[:, k, 1:2],
                           scale=coefA[:, k, 1:2]).then_inc(s[sg], 1)

                def kv_out(n, u):
                    act.wait_ge(s["k_mm"], n * SUB + u + 1)
                    fn(KS[:, u, :], bank[u % 3][0:TS, 0:C], ACT.Square).then_inc(s["k_sq"], 1)
                    fn(K1[:, u, :], bank[u % 3][0:TS, 0:C], ACT.Copy).then_inc(s["k_ev"], 1)
                    act.wait_ge(s["v_mm"], n * SUB + u + 1)
                    fn(V1[:, u, :], bank[3 + u % 3][0:TS, 0:C], ACT.Copy).then_inc(s["v_ev"], 1)

                n0 = b * STRIPS
                norm_in(n0, "kv_ld", "kxs")
                with act.Fori(0, STRIPS) as t:
                    n = b * STRIPS + t
                    if nxt:
                        keys_start(n + STRIPS)
                    act.wait_ge(s["at_mm"], HEAD + n)
                    act.wait_ge(s["k_hat"], HEAD + n * 2)
                    act.wait_ge(s["v1_st"], HEAD + n * 16)
                    kv_out(n, 0)
                    kv_out(n, 1)
                    kv_out(n, 2)
                    kv_out(n, 3)
                    with act.If(t < STRIPS - 1):
                        norm_in(n + 1, "kv_ld", "kxs")
                    with act.Else():
                        act.nop()
                    if nxt:
                        offset_gelu(n + STRIPS)
                        keys_out(n + STRIPS)
                stage_end(act, stage(b, 2))
                if nxt:
                    tanh(b + 1)
                stage_end(act, stage(b, 3))

                def query_out(n, o):
                    act.wait_ge(s["q_mm"], n * KC + o + 1)
                    p = bank[(6, 7, 5)[o]][:, 0:T]
                    fn(Q[:, o, :], p, ACT.Copy).then_inc(s["q_ev"], 1)
                    fn(QQ[:, o * T:(o + 1) * T], p, ACT.Square).then_inc(s["qq"], 1)

                def silu(n, j):
                    act.wait_ge(s["f1"], n * JC + j + 1)
                    act.wait_ge(s["sl"], HEAD + n * JC + j - 1)
                    fn(S[:, j % 2, :], bank[j % 2][:, 0:T], ACT.Silu, bias=b1p[:, j:j + 1]).then_inc(s["s_s"], 1)
                    act.wait_ge(s["f2"], HEAD + n * JC + j - 2)
                    act.wait_ge(s["s_s"], HEAD + n * JC + j + 1)
                    fn(SH[:, j % 3, :], S[:, j % 2, :], ACT.Copy).then_inc(s["sh"], 1)

                def o_square(n):
                    act.wait_ge(s["o_mx"], n + 1)
                    fn(OS, V[:, :, :].rearrange("p s c -> p (s c)"), ACT.Square).then_inc(s["o_sq"], 1)

                def mid_h(n):
                    act.wait_ge(s["mid"], n * KC + KC)
                    fn(MH[:, :, :], OT[:, :, :], ACT.Copy).then_inc(s["mh"], 1)

                def tile(n, first, last):
                    m = n + STRIPS
                    if not first:
                        mid_h(n - 1)
                    silu(n, 0)
                    if nxt:
                        normalise(m, 2, ("va", "qa"))
                    silu(n, 1)
                    if nxt:
                        values_start(m)
                    silu(n, 2)
                    if not last:
                        norm_in(n + 1, "x_ld", "xs")
                    silu(n, 3)
                    if not first:
                        act.wait_ge(s["ml"], n)
                    for k in range(KC):
                        act.wait_ge(s["ot_mm"], n * KC + k + 1)
                        fn(OT[:, k, :], bank[5 + k][:, 0:T], ACT.Copy).then_inc(s["ot_ev"], 1)
                    silu(n, 4)
                    if nxt:
                        queries_start(m)
                    silu(n, 5)
                    if not last:
                        query_out(n + 1, 0)
                    silu(n, 6)
                    if not last:
                        query_out(n + 1, 1)
                        query_out(n + 1, 2)
                    for j in range(7, JC):
                        silu(n, j)
                    if nxt:
                        values_out(m, 0)
                        values_out(m, 1)
                        values_out(m, 2)
                        values_out(m, 3)
                    if not last:
                        o_square(n + 1)

                norm_in(n0, "x_ld", "xs")
                for o in range(KC):
                    query_out(n0, o)
                o_square(n0)
                tile(n0, True, False)
                with act.Fori(1, STRIPS - 1) as t:
                    tile(b * STRIPS + t, False, False)
                tile(n0 + STRIPS - 1, False, True)
                mid_h(n0 + STRIPS - 1)
                stage_end(act, stage(b, 4))

            with act.Fori(0, B - 1) as b:
                image(b, True)
            image(B - 1, False)

        @block.vector
        def _(dve):
            tt, ts_, stt, cp = dve.tensor_tensor, dve.tensor_scalar, dve.scalar_tensor_tensor, dve.tensor_copy

            def f(ap):
                return ap.bitcast(F32)

            dve.wait_ge(s["const_ld"], CONSTS * 16)
            dve.memset(bst[:, :, 1, :, :], 1.0).then_inc(s["set_bst"], 1)
            for col in (0, W + 1):
                dve.memset(XG[:, :, :, col:col + 1], 0.0)
            dve.wait_ge(s["set_ps"], 1)
            tt(b1p[:, :], b1[:, :], bank[0][:, 0:JC], ALU.add).then_inc(s["set_bias"], 1)
            for k in range(KC):
                last = ts_(stg[0][:, k * HID:(k + 1) * HID], stg[0][:, k * HID:(k + 1) * HID], lng[:, k:k + 1], None, ALU.mult)
            last.then_inc(s["set_sum"], 1)
            dve.wait_ge(s["set_sum"], 1)
            dve.wait_ge(s["set_ps"], 2)
            for k in range(KC):
                for q in range(3):
                    v = stg[0][:, k * HID + q * 512:k * HID + (q + 1) * 512]
                    last = tt(v, v, bank[1 + q][:, :], ALU.subtract)
            last.then_inc(s["set_ctr"], 2)
            dve.wait_ge(s["stg_h"], 1)
            tt(W1L[:, :, :], stg[0][:, :].rearrange("p (k n) -> p k n", k=KC), f(W1H[:, :, :]), ALU.subtract).then_inc(s["stg_used"], 1)
            dve.wait_ge(s["stg_h"], 2)
            tt(W2L[:, :, :], stg[1][:, :].rearrange("p (k n) -> p k n", k=JC), f(W2H[:, :, :]), ALU.subtract).then_inc(s["stg_used"], 1)
            qkv = stg[0][:, 0:KC * 3 * C].rearrange("p (k n) -> p k n", k=KC)
            dve.wait_ge(s["stg_h"], 4)
            tt(WQL[:, :, :], qkv[:, :, 0:C], f(WQH[:, :, :]), ALU.subtract)
            tt(WKVL[:, :, :], qkv[:, :, C:3 * C], f(WKVH[:, :, :]), ALU.subtract).then_inc(s["stg_used"], 1)
            dve.wait_ge(s["stg_h"], 5)
            tt(WPL[:, :, :], stg[1][:, 0:KC * C].rearrange("p (k n) -> p k n", k=KC), f(WPH[:, :, :]), ALU.subtract)

            def strip_stats(g, t):
                dve.wait_ge(s[f"x0_ld{t % 2}"], slot_at(g, t, 2, 16))
                for k in range(KC):
                    last = dve.bn_stats(bst[:, k, 0, t, :], X0S[:, t % 2, k, :])
                last.then_inc(s["x0bn"], 1)

            def gn_coefs(g):
                for k in range(KC):
                    for w in range(2):
                        last = dve.bn_aggr(gst[:, k, w, :], bst[:, k, w, :, :].rearrange("p a c -> p (a c)"))
                last.then_inc(s["gn_st"], 1)
                dve.wait_ge(s["gn_mm"], g + 1)
                cp(gmv[:, :, :, :].rearrange("p k s c -> p (k s c)"), bank[0][:, 0:4 * KC]).then_inc(s["gn_s1"], 1)
                dve.wait_ge(s["gn_s1"], g + 1)
                tt(gdev[:, :, :, 0], gst[:, :, :, 0], gmv[:, :, :, 0], ALU.subtract)
                tt(gdev[:, :, :, 1], gst[:, :, :, 0], gmv[:, :, :, 0], ALU.subtract).then_inc(s["gn_d"], 1)
                dve.wait_ge(s["gn_d"], g + 1)
                tt(gdev[:, :, :, :], gdev[:, :, :, :], gdev[:, :, :, :], ALU.mult).then_inc(s["gn_dev"], 1)
                dve.wait_ge(s["gn_mm2"], g + 1)
                tt(gvar[:, :, :].rearrange("p k s -> p (k s)"), gmv[:, :, :, 1].rearrange("p k s -> p (k s)"),
                   bank[1][:, 0:4 * KC:2], ALU.add).then_inc(s["gn_v1"], 1)
                dve.wait_ge(s["gn_v1"], g + 1)
                ts_(gvar[:, :, :], gvar[:, :, :], EPS_GN, None, ALU.add).then_inc(s["gn_v2"], 1)
                dve.wait_ge(s["gn_rstd"], g + 1)
                cp(coefA[:, :, :], gvar[:, :, :])
                tt(gmean[:, :, :], gmv[:, :, :, 0], gvar[:, :, :], ALU.mult).then_inc(s["gn_nb"], 1)
                dve.wait_ge(s["gn_nb"], g + 1)
                ts_(coefB[:, :, :], gmean[:, :, :], -1.0, None, ALU.mult).then_inc(s["gn_coef"], 1)

            for t in range(STRIPS):
                strip_stats(0, t)
            dve.wait_ge(s["x0bn"], STRIPS)
            alone(dve)
            gn_coefs(0)
            stage_end(dve, 0)

            def edges(t, m, which):
                dve.wait_ge(s[f"xg{which}"], m * KC + KC)
                ts_(XG[:, :, 0, 1:W + 1], XG[:, :, 0, 1:W + 1], edge[:, 0, bass.ds(t, 1)], None, ALU.mult)
                ts_(XG[:, :, RS + 1, 1:W + 1], XG[:, :, RS + 1, 1:W + 1], edge[:, 1, bass.ds(t, 1)], None,
                    ALU.mult).then_inc(s[f"edged{which}"], 1)
                dve.wait_ge(s[f"edged{which}"], m + 1)

            def taps(m, acc, conv, st, start, sg, first, count):
                rows, cols = (RS, W) if st == 1 else (SR, WK)
                for q in range(first, first + count):
                    i, k = 1 + q // KC, q % KC
                    ky, kx = TAPS[i]
                    if i == 1:
                        dve.wait_ge(s[start], m * KC + k + 1)
                    else:
                        dve.wait_ge(s[sg], HEAD + m * 24 + (q - KC + 1))
                    src = XG[:, k, ky:ky + st * (rows - 1) + 1:st, kx:kx + st * (cols - 1) + 1:st]
                    o = acc[:, k, :].rearrange("p (r w) -> p r w", w=cols)
                    stt(o, src, wconv[:, conv, k, 3 * ky + kx:3 * ky + kx + 1], o, ALU.mult, ALU.add).then_inc(s[sg], 1)

            def offset_taps(m, first, count):
                taps(m, OA, 3, 2, "o0", "oa", first, count)

            def key_taps(m, first, count):
                taps(m, KA, 2, 2, "k0", "ka", first, count)

            def value_taps(m, first, count):
                taps(m, VA, 0, 1, "v0", "va", first, count)

            def query_taps(m, first, count):
                taps(m, QA, 1, 1, "q0", "qa", first, count)

            def offset_stats(m):
                dve.wait_ge(s["otp"], HEAD + m + 1)
                dve.bn_stats(obn[:, :], bank[7][0:TK, 0:C]).then_inc(s["obn_s"], 1)
                dve.wait_ge(s["obn_s"], m + 1)
                alone(dve)
                dve.bn_aggr(oag[:, :], obn[:, :]).then_inc(s["oag_s"], 1)
                dve.wait_ge(s["oag_s"], m + 1)
                ts_(orv[:, 0:1], oag[:, 1:2], EPS_LN, None, ALU.add).then_inc(s["orv_s"], 1)

            def offset_norm(m):
                dve.wait_ge(s["orr_s"], m + 1)
                dve.wait_ge(s["dots"], HEAD + m * 2)
                ts_(LN[:, :], bank[7][0:TK, 0:C], oag[:, 0:1], orv[:, 1:2], ALU.subtract, ALU.mult).then_inc(s["ln1"], 1)
                dve.wait_ge(s["ln1"], m + 1)
                tt(LN[:, :], LN[:, :], olng[:, :], ALU.mult).then_inc(s["ln2"], 1)
                dve.wait_ge(s["ln2"], m + 1)
                tt(LN[:, :], LN[:, :], olnb[:, :], ALU.add).then_inc(s["ln_s"], 1)

            def offset_dots(t, m):
                dve.wait_ge(s["gelu"], m + 1)
                dve.wait_ge(s["off_put"], HEAD + m)
                for p in range(2):
                    dve.wait_ge(s["dots"], HEAD + m * 2 + p - 1)
                    dve.tensor_tensor_reduce(out=prod[:, p, :], in0=LN[:, :], in1=woff2[:, p, :], scale=1.0, scalar=0.0,
                                             op0=ALU.mult, op1=ALU.add, accum_out=dot[:, p:p + 1]).then_inc(s["dots"], 1)
                dve.wait_ge(s["dots"], HEAD + m * 2 + 2)
                cp(OFF[:, bass.ds(t, 1), :].rearrange("p a c -> p (a c)"), dot[:, :]).then_inc(s["off_put"], 1)

            def sampling_points(g):
                steps = 9

                def after(i):
                    dve.wait_ge(s["point"], g * steps + i)

                dve.wait_ge(s["off_put"], HEAD + (g + 1) * STRIPS)
                tt(OFF[:, :, :], OFF[:, :, :], refp[:, :, :], ALU.add).then_inc(s["offr"], 1)
                dve.wait_ge(s["tanh_s"], g + 1)
                ts_(POS[:, :, :], POS[:, :, :], 1.0, 0.5 * (W - 1), ALU.add, ALU.mult).then_inc(s["point"], 1)
                after(1)
                cp(FI[:, :, :], POS[:, :, :]).then_inc(s["point"], 1)
                after(2)
                cp(FF[:, :, :], FI[:, :, :]).then_inc(s["point"], 1)
                after(3)
                tt(FG[:, :, :], FF[:, :, :], POS[:, :, :], ALU.is_gt).then_inc(s["point"], 1)
                after(4)
                tt(FF[:, :, :], FF[:, :, :], FG[:, :, :], ALU.subtract).then_inc(s["point"], 1)
                after(5)
                ts_(FF[:, :, :], FF[:, :, :], 0.0, float(W - 2), ALU.max, ALU.min).then_inc(s["point"], 1)
                after(6)
                tt(WG[:, :, :], POS[:, :, :], FF[:, :, :], ALU.subtract)
                ts_(IXF[:, 0, :], FF[:, :, 0], float(W), 1.0, ALU.mult, ALU.add).then_inc(s["point"], 1)
                after(7)
                tt(IXF[:, 0, :], IXF[:, 0, :], FF[:, :, 1], ALU.add)
                ts_(WN[:, :, :], WG[:, :, :], -1.0, 1.0, ALU.mult, ALU.add).then_inc(s["point"], 1)
                after(8)
                ts_(IXF[:, 1, :], IXF[:, 0, :], float(W), None, ALU.add).then_inc(s["point"], 1)
                for c, (wy, wx) in enumerate(((WN, WN), (WN, WG), (WG, WN), (WG, WG))):
                    last = tt(W4[:, :, c], wy[:, :, 0], wx[:, :, 1], ALU.mult)
                last.then_inc(s["w4s"], 1)
                after(9)
                cp(IX[:, :, :], IXF[:, :, :]).then_inc(s["ixi"], 1)

            dve.wait_ge(s["off_ld"], 48)
            alone(dve)
            with dve.Fori(0, STRIPS) as t:
                edges(t, t, 1)
                offset_taps(t, 0, 24)
                key_taps(t, 0, 12)
                offset_stats(t)
                key_taps(t, 12, 6)
                offset_norm(t)
                key_taps(t, 18, 6)
                offset_dots(t, t)
            stage_end(dve, 1)
            sampling_points(0)
            with dve.Fori(0, STRIPS) as t:
                edges(t, t, 2)
                value_taps(t, 0, 24)
                query_taps(t, 0, 24)
            stage_end(dve, 2)

            def image(b, nxt):
                dve.wait_ge(s["w4s"], b + 1)
                for t in range(STRIPS):
                    dve.wait_ge(s[f"gath{t}"], b * 32 + 32)
                    if t >= 2:
                        dve.wait_ge(s["mt_mm"], b * STRIPS + t - 1)
                    ts_(VS[:, t % 2, :], G7[:, t, 0, 0, :], W4[:, t, 0:1], None, ALU.mult).then_inc(s["vs_ch"], 1)
                    for c in range(1, 4):
                        dve.wait_ge(s["vs_ch"], b * (3 * STRIPS) + 3 * t + c)
                        last = stt(VS[:, t % 2, :], G7[:, t, c // 2, c % 2, :], W4[:, t, c:c + 1], VS[:, t % 2, :], ALU.mult, ALU.add)
                        last.then_inc(s["vs_ch"] if c < 3 else s["vs_s"], 1)
                dve.wait_ge(s["mt_mm"], b * STRIPS + STRIPS)
                for k in range(KC):
                    last = tt(MT[:, k, :], head0[:, :], bank[k][:, 0:P], ALU.mult)
                last.then_inc(s["mt_ev"], 1)
                dve.wait_ge(s["w2_mm"], b + 1)
                for k in range(KC):
                    last = cp(W2TH[:, k, :], bank[3 + k][:, 0:C])
                last.then_inc(s["w2_ev"], 1)
                dve.wait_ge(s["w2_ev"], b + 1)
                for k in range(KC):
                    tt(W2TL[:, k, :], bank[3 + k][:, 0:C], f(W2TH[:, k, :]), ALU.subtract)
                stage_end(dve, stage(b, 0))

                for t in range(STRIPS + 1):
                    if t < STRIPS:
                        dve.wait_ge(s["ch"], b * STRIPS + t + 1)
                        tt(CL[:, :, :], CQ[:, t % 2, :, :], f(CH[:, :, :]), ALU.subtract).then_inc(s["cl"], 1)
                    if t >= 1:
                        u = t - 1
                        dve.wait_ge(s[f"cx_ld{u % 2}"], slot_at(b, u, 2, 16))
                        for o in range(KC):
                            dve.wait_ge(s["y0"], (b * STRIPS + u) * KC + o + 1)
                            tt(CX[:, u % 2, o, :], CX[:, u % 2, o, :], bank[2 + 3 * (u % 2) + o][:, 0:T], ALU.add).then_inc(s["x1a"], 1)
                        for o in range(KC):
                            dve.wait_ge(s["x1a"], (b * STRIPS + u) * KC + o + 1)
                            last = dve.bn_stats(bst[:, o, 1, u, :], CX[:, u % 2, o, :])
                        last.then_inc(s["x1bn"], 1)
                        if nxt:
                            strip_stats(b + 1, u)
                dve.wait_ge(s["x1bn"], b * STRIPS + STRIPS)
                if nxt:
                    dve.wait_ge(s["x0bn"], (b + 2) * STRIPS)
                alone(dve)
                gn_coefs(b + 1)
                stage_end(dve, stage(b, 1))

                n0 = b * STRIPS

                def kv_split(n, first):
                    dve.wait_ge(s["kxs"], n * KC + KC)
                    if not first:
                        dve.wait_ge(s["v_mm"], n * SUB)
                    cp(XH[:, :, :], X[:, :, :]).then_inc(s["kxh"], 1)
                    dve.wait_ge(s["kxh"], n + 1)
                    tt(XL[:, :, :], X[:, :, :], f(XH[:, :, :]), ALU.subtract).then_inc(s["kxl"], 1)

                def key_norm(n, h, lo, hi):
                    dve.wait_ge(s["k_sq"], n * SUB + hi)
                    dve.tensor_reduce(kn[:, lo * NH1:hi * NH1],
                                      KS[:, lo:hi, :].rearrange("p s (h c) -> p (s h) c", c=HD), AX.X, ALU.add).then_inc(s["k_red"], 1)

                def key_scale(n, h, lo, hi):
                    dve.wait_ge(s["k_rs"], n * 2 + h + 1)
                    dve.wait_ge(s["k_ev"], HEAD + n * SUB + hi)
                    v = K1[:, lo:hi, :].rearrange("p s (h c) -> p (s h) c", c=HD)
                    r = rk[:, lo * NH1:hi * NH1].unsqueeze(2).to_broadcast([TS, (hi - lo) * NH1, HD])
                    tt(v, v, r, ALU.mult).then_inc(s["k_hat"], 1)

                kv_split(n0, True)
                if nxt:
                    dve.wait_ge(s["off_ld"], (b + 2) * 48)
                    alone(dve)
                with dve.Fori(0, STRIPS) as t:
                    n = b * STRIPS + t
                    m = n + STRIPS
                    if nxt:
                        edges(t, m, 1)
                        offset_taps(m, 0, 12)
                    key_norm(n, 0, 0, 3)
                    if nxt:
                        offset_taps(m, 12, 12)
                    key_norm(n, 1, 3, 4)
                    if nxt:
                        key_taps(m, 0, 3)
                    with dve.If(t < STRIPS - 1):
                        kv_split(n + 1, False)
                    with dve.Else():
                        dve.nop()
                    if nxt:
                        offset_stats(m)
                        key_taps(m, 3, 12)
                        offset_norm(m)
                        key_taps(m, 15, 9)
                    key_scale(n, 0, 0, 3)
                    key_scale(n, 1, 3, 4)
                    if nxt:
                        offset_dots(t, m)
                stage_end(dve, stage(b, 2))
                tt(AB[:, :], head1[:, :], bank[6][:, 0:WTOT], ALU.mult).then_inc(s["ab_s"], 1)
                dve.memset(f(o1r[:, :]), 1.0)
                if nxt:
                    sampling_points(b + 1)
                stage_end(dve, stage(b, 3))

                def split_x(n):
                    dve.wait_ge(s["xs"], n * KC + KC)
                    cp(XH[:, :, :], X[:, :, :]).then_inc(s["xh"], 1)
                    dve.wait_ge(s["xh"], n + 1)
                    tt(XL[:, :, :], X[:, :, :], f(XH[:, :, :]), ALU.subtract).then_inc(s["xl"], 1)

                def token_stats(n, u):
                    dve.wait_ge(s["xt_mm"], n * SUB + u + 1)
                    dve.bn_stats(xbn[:, u, :], bank[(5, 6, 7, 5)[u]][0:TS, 0:C]).then_inc(s["bn_s"], 1)

                def token_var(n):
                    dve.wait_ge(s["bn_s"], n * SUB + SUB)
                    alone(dve)
                    for u in range(SUB):
                        last = dve.bn_aggr(xag[:, u, :], xbn[:, u, :])
                    last.then_inc(s["ag_s"], 1)
                    dve.wait_ge(s["ag_s"], n + 1)
                    ts_(rve[:, :], xag[:, :, 1], EPS_LN, None, ALU.add).then_inc(s["rve_s"], 1)

                def token_diag(n):
                    dve.wait_ge(s["rr_s"], n + 1)
                    cp(rh[:, :], rr[:, :]).then_inc(s["rh_s"], 1)
                    dve.wait_ge(s["rh_s"], n + 1)
                    tt(rl[:, :], rr[:, :], f(rh[:, :]), ALU.subtract).then_inc(s["rl_s"], 1)
                    dve.wait_ge(s["rl_s"], n + 1)
                    idb = ident[0:TS, 0:TS].unsqueeze(1).to_broadcast([TS, SUB, TS])
                    tt(DH[:, :, :], idb, f(rh[:, :]).unsqueeze(2).to_broadcast([TS, SUB, TS]), ALU.mult).then_inc(s["dg"], 1)
                    tt(DL[:, :, :], idb, rl[:, :].unsqueeze(2).to_broadcast([TS, SUB, TS]), ALU.mult).then_inc(s["dg"], 1)

                def scale_x(n):
                    dve.wait_ge(s["rb_mm"], n + 1)
                    tt(X[:, :, :], X[:, :, :], bank[6][:, 0:T].unsqueeze(1).to_broadcast([P, KC, T]), ALU.mult).then_inc(s["xsr"], 1)

                def query_norm(n):
                    dve.wait_ge(s["qs_mm"], n + 1)
                    cp(qn[:, :], bank[7][0:TS, 0:SUB * NH1]).then_inc(s["qn_s"], 1)

                def heads(ap):
                    return ap.rearrange("p (h c) -> p h c", c=HD)

                def o_scale(n, u):
                    if u == 0:
                        dve.wait_ge(s["rq_s"], n + 1)
                    dve.wait_ge(s["qa_mm"], n * SUB + u + 1)
                    r = rq[:, u * NH1:(u + 1) * NH1].unsqueeze(2).to_broadcast([TS, NH1, HD])
                    tt(heads(OS[:, u * C:(u + 1) * C]), heads(bank[(5, 6, 7, 5)[u]][0:TS, 0:C]), r, ALU.mult).then_inc(s["o_sc"], 1)

                def o_mix(n):
                    dve.wait_ge(s["o_sc"], n * SUB + SUB)
                    dve.wait_ge(s["v_ld"], n * 16 + 16)
                    vf = V[:, :, :].rearrange("p s c -> p (s c)")
                    stt(vf, vf, 0.5, OS, ALU.mult, ALU.add).then_inc(s["o_mx"], 1)

                def o_norm(n):
                    dve.wait_ge(s["o_sq"], n + 1)
                    dve.tensor_reduce(on[:, :], heads(OS), AX.X, ALU.add).then_inc(s["o_red"], 1)

                def o_final(n):
                    dve.wait_ge(s["ro_s"], n + 1)
                    v = heads(V[:, :, :].rearrange("p s c -> p (s c)"))
                    tt(v, v, ro[:, :].unsqueeze(2).to_broadcast([TS, SUB * NH1, HD]), ALU.mult).then_inc(s["o_fin"], 1)

                def split_xr(n, first):
                    dve.wait_ge(s["xsr"], n + 1)
                    if not first:
                        dve.wait_ge(s["f1"], n * JC)
                    cp(XRH[:, :, :], X[:, :, :]).then_inc(s["xrh"], 1)
                    dve.wait_ge(s["xrh"], n + 1)
                    tt(XRL[:, :, :], X[:, :, :], f(XRH[:, :, :]), ALU.subtract).then_inc(s["xrl"], 1)

                def split_s(n, j):
                    dve.wait_ge(s["sh"], n * JC + j + 1)
                    tt(SL[:, j % 3, :], S[:, j % 2, :], f(SH[:, j % 3, :]), ALU.subtract).then_inc(s["sl"], 1)

                def middle(n):
                    dve.wait_ge(s["ot_ev"], n * KC + KC)
                    dve.wait_ge(s["f2"], HEAD + n * JC + JC)
                    for k in range(KC):
                        stt(OT[:, k, :], bank[2 + k][:, 0:T], b2[:, k:k + 1], OT[:, k, :], ALU.add, ALU.add).then_inc(s["mid"], 1)
                    dve.wait_ge(s["mh"], n + 1)
                    tt(ML[:, :, :], OT[:, :, :], f(MH[:, :, :]), ALU.subtract).then_inc(s["ml"], 1)

                def output(n):
                    dve.wait_ge(s["y_ld"], n * 16 + 16)
                    for k in range(KC):
                        dve.wait_ge(s["pj"], n * KC + k + 1)
                        stt(Y[:, k, :], bank[5 + k][:, 0:T], bp[:, k:k + 1], Y[:, k, :], ALU.add, ALU.add).then_inc(s["y_s"], 1)

                def tile(t, n, first, last):
                    m = n + STRIPS
                    if not first:
                        middle(n - 1)
                    split_s(n, 0)
                    o_final(n)
                    if nxt:
                        edges(t, m, 2)
                    split_s(n, 1)
                    if nxt:
                        value_taps(m, 0, 3)
                    split_s(n, 2)
                    if not first:
                        output(n - 1)
                    if nxt:
                        value_taps(m, 3, 3)
                    split_s(n, 3)
                    if not last:
                        split_x(n + 1)
                    if nxt:
                        value_taps(m, 6, 4)
                    split_s(n, 4)
                    if not last:
                        token_stats(n + 1, 0)
                        token_stats(n + 1, 1)
                        token_stats(n + 1, 2)
                    if nxt:
                        value_taps(m, 10, 5)
                    split_s(n, 5)
                    if not last:
                        token_stats(n + 1, 3)
                        token_var(n + 1)
                    if nxt:
                        value_taps(m, 15, 4)
                    split_s(n, 6)
                    if not last:
                        token_diag(n + 1)
                    if nxt:
                        value_taps(m, 19, 5)
                    split_s(n, 7)
                    if not last:
                        scale_x(n + 1)
                        query_norm(n + 1)
                    if nxt:
                        query_taps(m, 0, 4)
                    split_s(n, 8)
                    if nxt:
                        query_taps(m, 4, 5)
                    split_s(n, 9)
                    if not last:
                        o_scale(n + 1, 0)
                        o_scale(n + 1, 1)
                    if nxt:
                        query_taps(m, 9, 5)
                    split_s(n, 10)
                    if not last:
                        o_scale(n + 1, 2)
                        o_scale(n + 1, 3)
                    if nxt:
                        query_taps(m, 14, 5)
                    split_s(n, 11)
                    if nxt:
                        query_taps(m, 19, 5)
                    if not last:
                        split_xr(n + 1, False)
                        o_mix(n + 1)
                        o_norm(n + 1)

                split_x(n0)
                for u in range(SUB):
                    token_stats(n0, u)
                token_var(n0)
                token_diag(n0)
                scale_x(n0)
                query_norm(n0)
                split_xr(n0, True)
                for u in range(SUB):
                    o_scale(n0, u)
                o_mix(n0)
                o_norm(n0)
                tile(0, n0, True, False)
                with dve.Fori(1, STRIPS - 1) as t:
                    tile(t, b * STRIPS + t, False, False)
                tile(STRIPS - 1, n0 + STRIPS - 1, False, True)
                middle(n0 + STRIPS - 1)
                output(n0 + STRIPS - 1)
                stage_end(dve, stage(b, 4))

            with dve.Fori(0, B - 1) as b:
                image(b, True)
            image(B - 1, False)


def kernel(**inputs):
    import numpy as _np
    import concourse.bacc as _bacc
    from concourse import mybir as _mybir
    from concourse.bass_utils import run_bass_kernel_spmd as _run

    def a(name):
        return _np.asarray(inputs[name])

    def rows(w):
        k = w.shape[0] // P
        return w.reshape(k, P, -1).transpose(1, 0, 2).reshape(P, -1)

    def cols(v):
        return v.reshape(-1, P).T

    def chunks(w):
        return w.reshape(-1, P, w.shape[-1]).transpose(1, 0, 2)

    x = a("x")
    arrays = dict(constants())
    arrays.update({
        "x": _np.pad(x, ((0, 0), (0, 0), (1, 1), (0, 0))),
        "fc1_w": rows(a("L1_conv_fc1_w")), "fc2_w": rows(a("L1_conv_fc2_w")),
        "qkv_w": rows(a("L1_conv_qkv_w")), "proj_w": rows(a("L1_conv_proj_w")),
        "fc1_b": cols(a("L1_conv_fc1_b")), "fc2_b": cols(a("L1_conv_fc2_b")), "proj_b": cols(a("L1_conv_proj_b")),
        "ln_g": cols(a("L1_conv_ln_g")), "ln_b": cols(a("L1_conv_ln_b")),
        "w_conv": _np.stack([chunks(a("L0_conv_w_" + n).reshape(C, 9)) for n in ("v", "q", "k", "off1")], 1),
        "b_conv": _np.stack([cols(a("L0_conv_b_" + n)) for n in ("v", "q", "k", "off1")], 1),
        "off_g": _np.tile(a("L0_conv_ln_g"), (TK, 1)), "off_b": _np.tile(a("L0_conv_ln_b"), (TK, 1)),
        "w_off2": _np.tile(a("L0_conv_w_off2")[None], (TK, 1, 1)),
        "w_outT": chunks(a("L0_conv_w_out").T),
    })
    nc = _bacc.Bacc("TRN2", target_bir_lowering=False, num_devices=1)
    feed, d = {}, {}
    for name, v in arrays.items():
        v = _np.ascontiguousarray(v)
        feed[f"in_{name}"] = v
        d[name] = nc.dram_tensor(f"in_{name}", v.shape, _mybir.dt.from_np(v.dtype), kind="ExternalInput").ap()
    out = nc.dram_tensor("out_0", x.shape, F32, kind="ExternalOutput").ap()
    build(nc, d, out)
    r = _run(nc, [feed], core_ids=[0])
    return r.results[0]["out_0"]
```

```python
import numpy as np
import concourse.bass as bass
from concourse import mybir
from contextlib import ExitStack

F32 = mybir.dt.float32
F32R = mybir.dt.float32r
I32 = mybir.dt.int32
ALU = mybir.AluOpType
ACT = mybir.ActivationFunctionType
AX = mybir.AxisListType

P = 128
C, H, W = 384, 56, 56
KC = C // P
L = H * W
STRIPS = 7
RS = H // STRIPS
T = RS * W
SUB = 4
TS = T // SUB
HK = WK = 28
SR = HK // STRIPS
TK = SR * WK
GROUPS = 32
CG = C // GROUPS
HC0 = 32
NH1, HD = 8, 48
HID = 4 * C
JC = HID // P
WIN = ((0, 144), (96, 288), (240, 384))
WOFF = (0, 144, 336)
WTOT = 480
TAPS = [(1, 1)] + [(ky, kx) for ky in range(3) for kx in range(3) if (ky, kx) != (1, 1)]
EPS_GN = 1e-5
EPS_LN = 1e-5


def constants():
    f = np.float32
    ch = np.arange(C)
    grp = (ch[:, None] // CG == ch[None, :] // CG).astype(f) / f(CG)
    head0 = (np.arange(P)[:, None] // HC0 == np.arange(P)[None, :] // HC0).astype(f) * f(HC0 ** -0.5)
    head1 = np.zeros((P, WTOT), f)
    for k, (lo, hi) in enumerate(WIN):
        same = (P * k + np.arange(P))[:, None] // HD == np.arange(lo, hi)[None, :] // HD
        head1[:, WOFF[k]:WOFF[k] + hi - lo] = same * f(1.0 / np.pi)
    hsel = (ch[:, None] // HD == np.arange(NH1)[None, :]).astype(f).reshape(KC, P, NH1).transpose(1, 0, 2)
    ref = (np.linspace(0.5, HK - 0.5, HK, dtype=f) / f(HK) * f(2) - f(1)).astype(f)
    ry, rx = np.meshgrid(ref, ref, indexing="ij")
    refp = np.stack([ry, rx], -1).reshape(STRIPS, TK, 2).transpose(1, 0, 2)
    edge = np.ones((P, 2, STRIPS), f)
    edge[:, 0, 0] = 0
    edge[:, 1, STRIPS - 1] = 0
    return {
        "ident": np.eye(P, dtype=f),
        "grp": grp.reshape(KC, P, C).transpose(1, 0, 2),
        "head0": head0, "head1": head1, "hsel": hsel, "refp": refp, "edge": edge,
    }


def build(nc, d, out):
    B = d["x"].shape[0]

    def scratch(name, shape):
        return nc.dram_tensor(name, shape, F32, kind="Internal").ap()

    x1_d = scratch("x1_scr", (B, C, L))
    q_d = scratch("q_scr", (C, L))
    pair_d = scratch("pair_scr", (L + 1, 2 * C))
    kt_d = scratch("kt_scr", (HK * WK, C))
    wkv_d = nc.dram_tensor("wkv_scr", (2, P, KC, 2 * C), F32, kind="Internal").ap()
    v1_d = scratch("v1_scr", (L, C))
    x1_v = x1_d.rearrange("b (k p) l -> b p k l", p=P)
    q_v = q_d.rearrange("(k p) l -> p k l", p=P)
    out_v = out.rearrange("b (k p) h w -> b p k (h w)", p=P)
    xin_v = d["x"].rearrange("b (k p) h w -> b p k h w", p=P)

    ctx = ExitStack()
    with ctx:
        def sem(name):
            return ctx.enter_context(nc.semaphore(name))

        top = [(nc.sbuf_base + 31) // 32 * 32]
        limit = nc.sbuf_usable_end

        def sb(name, shape, dt=F32, at=top):
            size = int(np.prod(shape[1:])) * 4
            t = nc.alloc_sbuf_tensor_at(name, shape, dt, offset=at[0])
            at[0] += (size + 31) // 32 * 32
            assert at[0] <= limit, (name, at[0], limit)
            return t

        W1H, W1L = sb("W1H", [P, KC, HID], F32R), sb("W1L", [P, KC, HID], F32R)
        W2H, W2L = sb("W2H", [P, JC, C], F32R), sb("W2L", [P, JC, C], F32R)
        WQH, WQL = sb("WQH", [P, KC, C], F32R), sb("WQL", [P, KC, C], F32R)
        WPH, WPL = sb("WPH", [P, KC, C], F32R), sb("WPL", [P, KC, C], F32R)
        ident = sb("ident_s", [P, P])
        head1 = sb("head1_s", [P, WTOT])
        hsel = sb("hsel_s", [P, KC, NH1])
        edge = sb("edge_s", [P, 2, STRIPS])
        wconv = sb("wconv", [P, 4, KC, 9])
        bconv = sb("bconv", [P, 4, KC])
        b1p, b1 = sb("b1p", [P, JC]), sb("b1", [P, JC])
        b2, bp = sb("b2", [P, KC]), sb("bp", [P, KC])
        lng, lnb = sb("lng", [P, KC]), sb("lnb", [P, KC])
        nhalf = sb("nhalf", [P, 32])
        gst, gmv = sb("gst", [P, KC, 2, 2]), sb("gmv", [P, KC, 2, 2])
        gdev, gvar, gmean = sb("gdev", [P, KC, 2, 2]), sb("gvar", [P, KC, 2]), sb("gmean", [P, KC, 2])
        coefA, coefB = sb("coefA", [P, KC, 2]), sb("coefB", [P, KC, 2])
        bst = sb("bst", [P, KC, 2, STRIPS, 6])
        refp, OFF, POS = sb("refp_s", [TK, STRIPS, 2]), sb("OFF", [TK, STRIPS, 2]), sb("POS", [TK, STRIPS, 2])
        FI, FF, FG = sb("FI", [TK, STRIPS, 2], I32), sb("FF", [TK, STRIPS, 2]), sb("FG", [TK, STRIPS, 2])
        WG, WN, W4 = sb("WG", [TK, STRIPS, 2]), sb("WN", [TK, STRIPS, 2]), sb("W4", [TK, STRIPS, 4])
        IXF, IX = sb("IXF", [TK, 2, STRIPS]), sb("IX", [TK, 2, STRIPS], I32)
        AB = sb("AB", [P, WTOT])
        shared = top[0]

        at = [shared]
        W2TH, W2TL = sb("W2TH", [P, KC, C], F32R, at=at), sb("W2TL", [P, KC, C], F32R, at=at)
        after_w2t = at[0]
        KT7 = sb("KT7", [TK, STRIPS, C], at=at)
        G7 = sb("G7", [TK, STRIPS, 2, 2, C], at=at)
        VS = sb("VS", [TK, 2, C], at=at)
        MT = sb("MT", [P, KC, P], at=at)
        woT, head0 = sb("woT", [P, KC, C], at=at), sb("head0_s", [P, P], at=at)

        at = [after_w2t]
        CH, CL = sb("CH", [P, 2, KC, T], F32R, at=at), sb("CL", [P, 2, KC, T], F32R, at=at)
        at = [max(at[0], shared + 2 * KC * HID * 4)]
        X0S = sb("X0S", [P, 3, KC, T], at=at)
        grp = sb("grp_s", [P, KC, C], at=at)
        ones = sb("ones", [P, P], at=at)
        front_end = at[0]

        at = [shared]
        stg = [sb("stg0", [P, KC * HID], at=at), sb("stg1", [P, KC * HID], at=at)]

        at = [shared]
        X = sb("X", [P, KC, T], at=at)
        XH, XL = sb("XH", [P, KC, T], F32R, at=at), sb("XL", [P, KC, T], F32R, at=at)
        base1 = at[0]
        K1, V1 = sb("K1", [TS, 2, SUB, C], at=at), sb("V1", [TS, 2, SUB, C], at=at)
        KS = sb("KS", [TS, SUB, C], at=at)
        kn, rk = sb("kn", [TS, SUB * NH1], at=at), sb("rk", [TS, SUB * NH1], at=at)

        KA, OA = sb("KA", [P, KC, TK], at=at), sb("OA", [P, KC, TK], at=at)
        KT, LN = sb("KT", [TK, C], at=at), sb("LN", [TK, C], at=at)
        olng, olnb = sb("olng", [TK, C], at=at), sb("olnb", [TK, C], at=at)
        woff2, prod = sb("woff2", [TK, 2, C], at=at), sb("prod", [TK, 2, C], at=at)
        obn, oag, orv = sb("obn", [TK, 6], at=at), sb("oag", [TK, 2], at=at), sb("orv", [TK, 2], at=at)
        dot = sb("dot", [TK, 2], at=at)

        at = [max(at[0], front_end)]
        wkv_at = at[0]
        WKVH, WKVL = sb("WKVH", [P, KC, 2 * C], F32R, at=at), sb("WKVL", [P, KC, 2 * C], F32R, at=at)
        zero = sb("zero", [P, P], at=at)
        CQ, CX = sb("CQ", [P, 2, KC, T], at=at), sb("CX", [P, 3, KC, T], at=at)
        after_wkv = at[0] - 5 * KC * T * 4

        at = [base1]
        XRH, XRL = sb("XRH", [P, KC, T], F32R, at=at), sb("XRL", [P, KC, T], F32R, at=at)
        Q = sb("Q", [P, KC, T], at=at)
        QQ = sb("QQ", [P, SUB * C], at=at)
        V = sb("V", [TS, SUB, C], at=at)
        OT = sb("OT", [P, KC, T], at=at)
        S = sb("S", [P, 2, T], at=at)
        SH, SL = sb("SH", [P, 3, T], F32R, at=at), sb("SL", [P, 3, T], F32R, at=at)
        MH = sb("MH", [P, KC, T], F32R, at=at)
        ML = sb("ML", [P, KC, T], F32R, at=at)
        Y = sb("Y", [P, KC, T], at=at)
        DH, DL = sb("DH", [TS, SUB, TS], F32R, at=at), sb("DL", [TS, SUB, TS], F32R, at=at)
        o1r = sb("o1r", [TS, P], F32R, at=at)
        xbn, xag = sb("xbn", [TS, SUB, 6], at=at), sb("xag", [TS, SUB, 2], at=at)
        rve, rr = sb("rve", [TS, SUB], at=at), sb("rr", [TS, SUB], at=at)
        rh, rl = sb("rh", [TS, SUB], F32R, at=at), sb("rl", [TS, SUB], at=at)
        qn, rq = sb("qn", [TS, SUB * NH1], at=at), sb("rq", [TS, SUB * NH1], at=at)
        on, ro = sb("on", [TS, SUB * NH1], at=at), sb("ro", [TS, SUB * NH1], at=at)
        OS = QQ[0:TS, :]

        assert at[0] >= after_wkv
        xr_at = at[0]
        XR = sb("XR", [P, KC, RS + 2, W], at=at)
        XG = sb("XG", [P, KC, RS + 2, W + 2], at=at)
        XG3 = sb("XG3", [P, KC, RS + 2, W + 2], at=list(at))
        VA, QA = sb("VA", [P, KC, T], at=at), sb("QA", [P, KC, T], at=at)
        VT = sb("VT", [TS, 2, C], at=at)

        at = [wkv_at]
        diag = sb("diag", [P, KC, 9, P], at=at)
        XG2 = sb("XG2", [P, KC, RS + 2, W + 2], at=at)
        assert at[0] <= xr_at

        bank = [ctx.enter_context(nc.psum_tensor(f"bank{i}", [P, 512], F32)) for i in range(8)]

        stage_done = sem("stage_done")
        held = sem("held")
        names = """const_ld stg_ld0 stg_ld1 stg_h stg_used set_sum set_ctr set_ones set_ps pair_z wkv_st
            x0_ld0 x0_ld1 x0_ld2 x0bn grp_ld gn_st gn_mm gn_s1 gn_d gn_dev gn_mm2 gn_v1 gn_v2 gn_rstd gn_nb
            off_ld xr1_ld xg1 edged1 o0 k0 oa ka otp ktp kt_ev kt_st obn_s oag_s orv_s orr_s ln1 ln2 ln_s gelu dots off_put
            diag_s xr2_ld xg2 edged2 v0 q0 va qa vtp vt_ev q_st pair_st0 pair_st1
            offr tanh_s point w4s ixi
            b_ld vs_ch vs_s mt_mm mt_ev w2_mm w2_ev
            cq_ld0 cq_ld1 cx_ld0 cx_ld1 cx_ld2 ch cl y0 x1a x1bn x1_st0 x1_st1 x1_st2 wkv_ld
            kv_ld kxs kxh kxl k_mm v_mm k_sq k_ev v_ev k_red k_rs k_hat v1_st0 v1_st1 at_mm ab_s
            x_ld v_ld y_ld y_st xs xh xl xt_mm bn_s ag_s rve_s rr_s rh_s rl_s dg rb_mm xsr xrh xrl
            q_mm q_ev qq qs_mm qn_s rq_s qa_mm o_sc o_mx o_sq o_red ro_s o_fin ot_mm ot_ev
            f1 s_s sh sl f2 mid mh ml pj y_s""".split()
        names += [f"gath{t}" for t in range(STRIPS)]
        s = {n: sem("s_" + n) for n in names}

        def slot_uses(t, slots):
            return len(range(t % slots, STRIPS, slots)), t // slots + 1

        def slot_at(b, t, slots, each):
            per, upto = slot_uses(t, slots)
            return b * (per * each) + upto * each

        HEAD = 32
        ahead = """otp ktp oa ka kt_ev kt_st dots off_put va qa vtp vt_ev q_st pair_st0 pair_st1
            at_mm k_red k_hat v1_st0 v1_st1 k_ev v_ev s_s sl f2""".split()

        block = ctx.enter_context(nc.Block())

        def alone(eng):
            eng.sem_inc(held, 1)

        def stage_end(eng, n):
            alone(eng)
            eng.drain().then_inc(stage_done, 1)
            eng.wait_ge(stage_done, n * 5 + 5)
            alone(eng)

        STAGES = 4

        def stage(b, i):
            return b * STAGES + 2 + i

        def load_x0(eng, g, t):
            if t >= 3:
                eng.wait_ge(s["x0bn"], g * STRIPS + t - 2)
            eng.dma_start(X0S[:, t % 3, :, :].rearrange("p k (r w) -> p k r w", w=W),
                          xin_v[g, :, :, 1 + t * RS:1 + (t + 1) * RS, :]).then_inc(s[f"x0_ld{t % 3}"], 16)

        def strip_px(t):
            return bass.ts(t, T)

        CONSTS = 12

        @block.sync
        def _(sp):
            for dst, src in [
                (ident, d["ident"]), (head1, d["head1"]), (hsel, d["hsel"]), (edge, d["edge"]),
                (b1, d["fc1_b"]), (b2, d["fc2_b"]), (bp, d["proj_b"]), (lng, d["ln_g"]), (lnb, d["ln_b"]),
                (wconv, d["w_conv"]), (bconv, d["b_conv"]), (refp, d["refp"]),
            ]:
                sp.dma_start(dst.ap(), src).then_inc(s["const_ld"], 16)
            sp.dma_start(stg[0][:, :], d["fc1_w"]).then_inc(s["stg_ld0"], 16)
            sp.dma_start(stg[1][:, :], d["fc2_w"]).then_inc(s["stg_ld1"], 16)

            load_x0(sp, 0, 0)
            load_x0(sp, 0, 1)
            load_x0(sp, 0, 2)
            sp.dma_start(grp[:, :, :], d["grp"]).then_inc(s["grp_ld"], 16)
            sp.wait_ge(s["set_ones"], 1)
            sp.dma_start(pair_d[0, 0:C].rearrange("(a c) -> a c", a=3), zero[0:3, :]).then_inc(s["pair_z"], 16)
            sp.dma_start(pair_d[L, C:2 * C].rearrange("(a c) -> a c", a=3), zero[0:3, :]).then_inc(s["pair_z"], 16)
            sp.wait_ge(s["stg_used"], 1)
            sp.dma_start(stg[1][:, 0:KC * 3 * C], d["qkv_w"]).then_inc(s["stg_ld1"], 16)
            sp.dma_start(stg[1][:, KC * 3 * C:KC * 4 * C], d["proj_w"]).then_inc(s["stg_ld1"], 16)
            for t in range(3, STRIPS):
                load_x0(sp, 0, t)
            sp.wait_ge(s["stg_used"], 2)
            sp.dma_start(wkv_d[0], WKVH[:, :, :].bitcast(F32)).then_inc(s["wkv_st"], 16)
            sp.dma_start(wkv_d[1], WKVL[:, :, :].bitcast(F32)).then_inc(s["wkv_st"], 16)
            sp.wait_ge(s["wkv_st"], 32)
            sp.wait_ge(s["pair_z"], 32)
            stage_end(sp, 0)

            def load_offset_tables():
                for dst, src in ((olng[:, :], d["off_g"]), (olnb[:, :], d["off_b"]), (woff2[:, :, :], d["w_off2"])):
                    sp.dma_start(dst, src).then_inc(s["off_ld"], 16)

            def load_strip(g, t, which):
                sp.dma_start(XR[:, :, :, :], xin_v[g, :, :, bass.ds(t * RS, RS + 2), :]).then_inc(s[f"xr{which}_ld"], 16)

            def strip_read(m, which):
                sp.wait_ge(s[f"xg{which}"], m * KC + KC)

            def store_keys(t, m):
                sp.wait_ge(s["kt_ev"], HEAD + m + 1)
                sp.dma_start(kt_d[bass.ts(t, TK), :], KT[:, :]).then_inc(s["kt_st"], 16)

            def store_values(t, m):
                for u in range(SUB):
                    sp.wait_ge(s["vt_ev"], HEAD + m * SUB + u + 1)
                    for half in range(2):
                        sp.dma_start(pair_d[bass.ds(t * T + (u * TS + 1 - half), TS), half * C:(half + 1) * C],
                                     VT[:, u % 2, :]).then_inc(s[f"pair_st{u % 2}"], 16)

            def store_queries(t, m):
                sp.wait_ge(s["qa"], HEAD + m * 24 + 24)
                alone(sp)
                sp.dma_start(q_v[:, :, strip_px(t)], QA[:, :, :]).then_inc(s["q_st"], 16)

            load_offset_tables()
            load_strip(0, 0, 2)
            with sp.Fori(0, STRIPS - 1) as t:
                strip_read(t, 2)
                load_strip(0, t + 1, 2)
                store_queries(t, t)
                store_values(t, t)
                store_keys(t, t)
            store_queries(STRIPS - 1, STRIPS - 1)
            store_values(STRIPS - 1, STRIPS - 1)
            store_keys(STRIPS - 1, STRIPS - 1)
            sp.wait_ge(s["kt_st"], HEAD + 16 * STRIPS)
            for _ in range(STRIPS):
                sp.sem_inc(s["xr1_ld"], 16)

            def front_stored(g):
                sp.wait_ge(s["q_st"], HEAD + (g + 1) * (16 * STRIPS))
                sp.wait_ge(s["pair_st0"], HEAD + (g + 1) * (64 * STRIPS))
                sp.wait_ge(s["pair_st1"], HEAD + (g + 1) * (64 * STRIPS))

            front_stored(0)
            stage_end(sp, 1)

            def image(b, nxt):
                for dst, src in [(KT7[:, :, :], kt_d.rearrange("(t p) c -> p t c", p=TK)), (woT[:, :, :], d["w_outT"]),
                                 (head0[:, :], d["head0"])]:
                    sp.dma_start(dst, src).then_inc(s["b_ld"], 16)

                def load_queries(t):
                    sp.dma_start(CQ[:, t % 2, :, :], q_v[:, :, t * T:(t + 1) * T]).then_inc(s[f"cq_ld{t % 2}"], 16)

                def load_residual(t):
                    sp.dma_start(CX[:, t % 3, :, :].rearrange("p k (r w) -> p k r w", w=W),
                                 xin_v[b, :, :, 1 + t * RS:1 + (t + 1) * RS, :]).then_inc(s[f"cx_ld{t % 3}"], 16)

                sp.wait_ge(s["gath1"], b * 32 + 32)
                alone(sp)
                for t in range(2):
                    load_queries(t)
                    load_residual(t)
                stage_end(sp, stage(b, 0))
                sp.dma_start(grp[:, :, :], d["grp"]).then_inc(s["grp_ld"], 16)
                load_residual(2)
                for t in range(STRIPS):
                    if t + 2 < STRIPS:
                        sp.wait_ge(s["cl"], b * STRIPS + t + 1)
                        load_queries(t + 2)
                    if 1 <= t and t + 2 < STRIPS:
                        sp.wait_ge(s["x1bn"], b * STRIPS + t)
                        alone(sp)
                        sp.wait_ge(s[f"x1_st{(t - 1) % 3}"], slot_at(b, t - 1, 3, 16))
                        load_residual(t + 2)
                    sp.wait_ge(s["x1a"], (b * STRIPS + t + 1) * KC)
                    sp.dma_start(x1_v[b, :, :, t * T:(t + 1) * T], CX[:, t % 3, :, :]).then_inc(s[f"x1_st{t % 3}"], 16)
                for t in range(STRIPS - 3, STRIPS):
                    sp.wait_ge(s[f"x1_st{t % 3}"], slot_at(b, t, 3, 16))
                    alone(sp)
                stage_end(sp, stage(b, 1))
                n0 = b * STRIPS
                sp.dma_start(X[:, :, :], x1_v[b, :, :, 0:T]).then_inc(s["kv_ld"], 16)
                if nxt:
                    load_strip(b + 1, 0, 1)
                    load_offset_tables()

                for t in range(STRIPS):
                    n, m = n0 + t, n0 + STRIPS + t
                    if t < STRIPS - 1:
                        sp.wait_ge(s["kxl"], n + 1)
                        sp.dma_start(X[:, :, :], x1_v[b, :, :, (t + 1) * T:(t + 2) * T]).then_inc(s["kv_ld"], 16)
                        if nxt:
                            strip_read(m, 1)
                            load_strip(b + 1, t + 1, 1)
                    if nxt and t >= 1:
                        store_keys(t - 1, m - 1)
                    sp.wait_ge(s["v_ev"], HEAD + n * SUB + SUB)
                    sp.dma_start(v1_d[t * T:(t + 1) * T, :].rearrange("(s p) c -> p s c", p=TS),
                                 V1[:, t % 2, :, :]).then_inc(s[f"v1_st{t % 2}"], 16)
                for t in range(STRIPS - 2, STRIPS):
                    sp.wait_ge(s[f"v1_st{t % 2}"], HEAD + slot_at(b, t, 2, 16))
                    alone(sp)
                if nxt:
                    store_keys(STRIPS - 1, n0 + (2 * STRIPS - 1))
                    sp.wait_ge(s["kt_st"], HEAD + (b + 2) * (16 * STRIPS))
                stage_end(sp, stage(b, 2))

                def load_pre(t):
                    sp.dma_start(X[:, :, :], x1_v[b, :, :, strip_px(t)]).then_inc(s["x_ld"], 16)

                def load_v(t):
                    sp.dma_start(V[:, :, :], v1_d[bass.ts(t, T), :].rearrange("(s p) c -> p s c", p=TS)).then_inc(s["v_ld"], 16)

                def load_res(t):
                    sp.dma_start(Y[:, :, :], x1_v[b, :, :, strip_px(t)]).then_inc(s["y_ld"], 16)

                def store_out(t, n):
                    sp.wait_ge(s["y_s"], n * KC + KC)
                    sp.dma_start(out_v[b, :, :, strip_px(t)], Y[:, :, :]).then_inc(s["y_st"], 16)

                load_pre(0)
                load_v(0)
                load_res(0)
                if nxt:
                    load_strip(b + 1, 0, 2)
                sp.wait_ge(s["xrl"], n0 + 1)
                load_pre(1)
                if nxt:
                    strip_read(n0 + STRIPS, 2)
                    load_strip(b + 1, 1, 2)
                sp.wait_ge(s["ot_mm"], n0 * KC + KC)
                load_v(1)
                with sp.Fori(1, STRIPS - 1) as t:
                    n = b * STRIPS + t
                    sp.wait_ge(s["xrl"], n + 1)
                    load_pre(t + 1)
                    if nxt:
                        store_values(t - 1, n + (STRIPS - 1))
                        store_queries(t - 1, n + (STRIPS - 1))
                        strip_read(n + STRIPS, 2)
                        load_strip(b + 1, t + 1, 2)
                    store_out(t - 1, n - 1)
                    sp.wait_ge(s["y_st"], n * 16)
                    load_res(t)
                    sp.wait_ge(s["ot_mm"], n * KC + KC)
                    load_v(t + 1)
                nl = n0 + STRIPS - 1
                if nxt:
                    store_values(STRIPS - 2, nl + STRIPS - 1)
                    store_queries(STRIPS - 2, nl + STRIPS - 1)
                store_out(STRIPS - 2, nl - 1)
                sp.wait_ge(s["y_st"], nl * 16)
                load_res(STRIPS - 1)
                if nxt:
                    store_values(STRIPS - 1, nl + STRIPS)
                    store_queries(STRIPS - 1, nl + STRIPS)
                store_out(STRIPS - 1, nl)
                sp.wait_ge(s["y_st"], nl * 16 + 16)
                if nxt:
                    front_stored(b + 1)
                stage_end(sp, stage(b, 3))

            with sp.Fori(0, B - 1) as b:
                image(b, True)
            image(B - 1, False)

        @block.gpsimd
        def _(pool):
            for name in ahead:
                pool.sem_inc(s[name], HEAD)
            pool.memset(nhalf[:, :], -0.5)
            pool.memset(ones[:, :], 1.0 / C)
            pool.memset(zero[:, :], 0.0).then_inc(s["set_ones"], 1)

            def gn_rstd(g):
                pool.wait_ge(s["gn_v2"], g + 1)
                pool.tensor_tensor(gvar[:, :, :].rearrange("p k s -> p (k s)"), gvar[:, :, :].rearrange("p k s -> p (k s)"),
                                   nhalf[:, 0:2 * KC], ALU.pow).then_inc(s["gn_rstd"], 1)

            def offset_rstd(m):
                pool.wait_ge(s["orv_s"], m + 1)
                pool.tensor_tensor(orv[:, 1:2], orv[:, 0:1], nhalf[0:TK, 0:1], ALU.pow).then_inc(s["orr_s"], 1)

            def gather(g):
                pool.wait_ge(s["ixi"], g + 1)
                alone(pool)
                for t in range(STRIPS):
                    for r in range(2):
                        pool.indirect_dma_start(
                            out=G7[:, t, r, :, :].rearrange("p a c -> p (a c)"), out_offset=None,
                            in_=pair_d, in_offset=bass.IndirectOffsetOnAxis(ap=IX[:, r, t:t + 1], axis=0),
                        ).then_inc(s[f"gath{t}"], 16)
                for t in range(STRIPS):
                    pool.wait_ge(s[f"gath{t}"], g * 32 + 32)
                    alone(pool)

            gn_rstd(0)
            stage_end(pool, 0)
            with pool.Fori(0, STRIPS) as t:
                offset_rstd(t)
            stage_end(pool, 1)

            def image(b, nxt):
                gather(b)
                stage_end(pool, stage(b, 0))
                pool.memset(zero[:, :], 0.0)
                gn_rstd(b + 1)
                stage_end(pool, stage(b, 1))
                with pool.Fori(0, STRIPS) as t:
                    n = b * STRIPS + t
                    if nxt:
                        offset_rstd(n + STRIPS)
                    for h, (lo, hi) in enumerate(((0, 24), (24, 32))):
                        pool.wait_ge(s["k_red"], HEAD + n * 2 + h + 1)
                        pool.tensor_tensor(rk[:, lo:hi], kn[:, lo:hi], nhalf[0:TS, lo:hi], ALU.pow).then_inc(s["k_rs"], 1)
                stage_end(pool, stage(b, 2))
                with pool.Fori(0, STRIPS) as t:
                    n = b * STRIPS + t
                    pool.wait_ge(s["rve_s"], n + 1)
                    pool.tensor_tensor(rr[:, :], rve[:, :], nhalf[0:TS, 0:SUB], ALU.pow).then_inc(s["rr_s"], 1)
                    pool.wait_ge(s["qn_s"], n + 1)
                    pool.tensor_tensor(rq[:, :], qn[:, :], nhalf[0:TS, :], ALU.pow).then_inc(s["rq_s"], 1)
                    pool.wait_ge(s["o_red"], n + 1)
                    pool.tensor_tensor(ro[:, :], on[:, :], nhalf[0:TS, :], ALU.pow).then_inc(s["ro_s"], 1)
                stage_end(pool, stage(b, 3))

            with pool.Fori(0, B - 1) as b:
                image(b, True)
            image(B - 1, False)

        @block.tensor
        def _(pe):
            mm, tr = pe.matmul, pe.transpose

            pe.wait_ge(s["const_ld"], CONSTS * 16)
            pe.wait_ge(s["stg_ld0"], 16)
            pe.wait_ge(s["set_ones"], 1)
            for j in range(JC):
                for k in range(KC):
                    last = mm(bank[0][:, j:j + 1], stg[0][:, k * HID + j * P:k * HID + (j + 1) * P], lnb[:, k:k + 1],
                              start=(k == 0), stop=(k == KC - 1))
            last.then_inc(s["set_ps"], 1)
            def gn_groups(g):
                pe.wait_ge(s["grp_ld"], g * 16 + 16)
                pe.wait_ge(s["gn_st"], g + 1)
                for ko in range(KC):
                    for ki in range(KC):
                        last = mm(bank[4][:, 4 * ko:4 * ko + 4], grp[:, ki, ko * P:(ko + 1) * P],
                                  gst[:, ki, :, :].rearrange("p s c -> p (s c)"), start=(ki == 0), stop=(ki == KC - 1))
                last.then_inc(s["gn_mm"], 1)
                pe.wait_ge(s["gn_dev"], g + 1)
                for ko in range(KC):
                    for ki in range(KC):
                        last = mm(bank[0][:, 4 * ko:4 * ko + 4], grp[:, ki, ko * P:(ko + 1) * P],
                                  gdev[:, ki, :, :].rearrange("p s c -> p (s c)"), start=(ki == 0), stop=(ki == KC - 1))
                last.then_inc(s["gn_mm2"], 1)

            def three_pass(o, wh, wl, xh, xl, first, stop):
                mm(o, wh, xh, start=first, stop=False)
                mm(o, wh, xl, start=False, stop=False)
                return mm(o, wl, xh, start=False, stop=stop)

            def turn_offset(m):
                pe.wait_ge(s["oa"], HEAD + m * 24 + 24)
                pe.wait_ge(s["kt_ev"], HEAD + m)
                for k in range(KC):
                    last = tr(bank[7][0:TK, k * P:(k + 1) * P], OA[:, k, :], ident[:, :])
                last.then_inc(s["otp"], 1)

            def turn_keys(m):
                pe.wait_ge(s["ka"], HEAD + m * 24 + 24)
                pe.wait_ge(s["ln1"], m + 1)
                for k in range(KC):
                    last = tr(bank[7][0:TK, k * P:(k + 1) * P], KA[:, k, :], ident[:, :])
                last.then_inc(s["ktp"], 1)

            VTB = (6, 7, 5, 6)

            def turn_values(m, u):
                if u == 0:
                    pe.wait_ge(s["va"], HEAD + m * 24 + 24)
                if u == 3:
                    pe.wait_ge(s["vt_ev"], HEAD + m * SUB + 1)
                for k in range(KC):
                    last = tr(bank[VTB[u]][0:TS, k * P:(k + 1) * P], VA[:, k, u * TS:(u + 1) * TS], ident[:, :])
                last.then_inc(s["vtp"], 1)

            pe.wait_ge(s["set_sum"], 1)
            for q in range(3):
                for k in range(KC):
                    last = mm(bank[1 + q][:, :], ones[:, :], stg[0][:, k * HID + q * 512:k * HID + (q + 1) * 512],
                              start=(k == 0), stop=(k == KC - 1))
            last.then_inc(s["set_ps"], 1)
            gn_groups(0)
            stage_end(pe, 0)
            def query_conv(m, xg, k):
                if k == 0:
                    pe.wait_ge(s["edged2"], m + 1)
                    pe.wait_ge(s["qa"], HEAD + m * 24)
                for i, (ky, kx) in enumerate(TAPS):
                    last = mm(bank[k][:, 0:T].rearrange("p (r w) -> p r w", w=W), diag[:, k, i, :],
                              xg[:, k, ky:ky + RS, kx:kx + W], start=(i == 0), stop=(i == 8))
                last.then_inc(s["q0"], 1)

            def front(m, xg):
                query_conv(m, xg, 0)
                turn_offset(m)
                query_conv(m, xg, 1)
                query_conv(m, xg, 2)
                pe.wait_ge(s["vt_ev"], HEAD + m * SUB)
                pe.wait_ge(s["ln1"], m + 1)
                for u in range(SUB):
                    turn_values(m, u)
                pe.wait_ge(s["vt_ev"], HEAD + m * SUB + 2)
                turn_keys(m)

            pe.wait_ge(s["diag_s"], KC)
            with pe.Fori(0, STRIPS // 2) as h:
                front(h * 2, XG)
                front(h * 2 + 1, XG2)
            front(STRIPS - 1, XG)
            stage_end(pe, 1)

            def image(b, nxt):
                pe.wait_ge(s["b_ld"], b * 48 + 48)
                for t in range(STRIPS):
                    pe.wait_ge(s["vs_s"], b * STRIPS + t + 1)
                    for k in range(KC):
                        last = mm(bank[k][:, 0:P], VS[:, t % 2, k * P:(k + 1) * P], KT7[:, t, k * P:(k + 1) * P],
                                  start=(t == 0), stop=(t == STRIPS - 1))
                    last.then_inc(s["mt_mm"], 1)
                pe.wait_ge(s["mt_ev"], b + 1)
                for k in range(KC):
                    last = mm(bank[3 + k][:, 0:C], MT[:, k, :], woT[:, k, :], start=True, stop=True)
                last.then_inc(s["w2_mm"], 1)
                stage_end(pe, stage(b, 0))
                for t in range(STRIPS):
                    pe.wait_ge(s["cl"], b * STRIPS + t + 1)
                    pe.wait_ge(s["ch"], b * STRIPS + t + 1)
                    for o in range(KC):
                        if t >= 2:
                            pe.wait_ge(s["x1a"], (b * STRIPS + t - 2) * KC + o + 1)
                        p = bank[2 + 3 * (t % 2) + o][:, 0:T]
                        for k in range(KC):
                            last = three_pass(p, W2TH[:, k, o * P:(o + 1) * P], W2TL[:, k, o * P:(o + 1) * P],
                                              CH[:, t % 2, k, :], CL[:, t % 2, k, :], k == 0, k == KC - 1)
                        last.then_inc(s["y0"], 1)
                gn_groups(b + 1)
                stage_end(pe, stage(b, 1))

                KB, VB, ATB = (0, 1, 2), (3, 4, 5), 6
                mm(bank[ATB][:, 0:WTOT], zero[:, :], head1[:, :], start=True, stop=False, skip_group_check=True)

                def kv(n, u):
                    if u == 0:
                        pe.wait_ge(s["kxl"], n + 1)
                        pe.wait_ge(s["kxh"], n + 1)
                    for bk, c0, free, sg in ((KB, 0, "k_ev", "k_mm"), (VB, C, "v_ev", "v_mm")):
                        if u == 3:
                            pe.wait_ge(s[free], HEAD + n * SUB + 1)
                        elif u == 0:
                            pe.wait_ge(s[free], HEAD + n * SUB)
                        p = bank[bk[u % 3]][0:TS, 0:C]
                        for k in range(KC):
                            xh, xl = XH[:, k, u * TS:(u + 1) * TS], XL[:, k, u * TS:(u + 1) * TS]
                            mm(p, xh, WKVH[:, k, c0:c0 + C], start=(k == 0), stop=False)
                            mm(p, xh, WKVL[:, k, c0:c0 + C], start=False, stop=False)
                            last = mm(p, xl, WKVH[:, k, c0:c0 + C], start=False, stop=(k == KC - 1))
                        last.then_inc(s[sg], 1)

                def state(n, slot):
                    pe.wait_ge(s["k_hat"], HEAD + n * 2 + 2)
                    pe.wait_ge(s["v_ev"], HEAD + n * SUB + SUB)
                    for u in range(SUB):
                        for k, (lo, hi) in enumerate(WIN):
                            last = mm(bank[ATB][:, WOFF[k]:WOFF[k] + hi - lo], K1[:, slot, u, k * P:(k + 1) * P], V1[:, slot, u, lo:hi],
                                      start=False, stop=False, skip_group_check=True)
                    last.then_inc(s["at_mm"], 1)

                n0 = b * STRIPS

                def kv_tile(n, slot, first):
                    kv(n, 0)
                    if nxt and not first:
                        turn_keys(n + (STRIPS - 1))
                    kv(n, 1)
                    kv(n, 2)
                    if nxt:
                        turn_offset(n + STRIPS)
                    kv(n, 3)
                    if not first:
                        state(n - 1, 1 - slot)

                pe.wait_ge(s["wkv_ld"], b * 32 + 32)
                kv_tile(n0, 0, True)
                with pe.Fori(0, STRIPS // 2) as h:
                    kv_tile(b * STRIPS + h * 2 + 1, 1, False)
                    kv_tile(b * STRIPS + h * 2 + 2, 0, False)
                if nxt:
                    turn_keys(n0 + 2 * STRIPS - 1)
                state(n0 + STRIPS - 1, 0)
                stage_end(pe, stage(b, 2))
                pe.wait_ge(s["ab_s"], b + 1)

                CB = (5, 6, 7)

                def turn_x(n, u):
                    if u == 0:
                        pe.wait_ge(s["xs"], n * KC + KC)
                    if u == 3:
                        pe.wait_ge(s["bn_s"], n * SUB + 1)
                    for k in range(KC):
                        last = tr(bank[CB[u % 3]][0:TS, k * P:(k + 1) * P], X[:, k, u * TS:(u + 1) * TS], ident[:, :])
                    last.then_inc(s["xt_mm"], 1)

                def query(n, o):
                    if o == 0:
                        pe.wait_ge(s["xl"], n + 1)
                        pe.wait_ge(s["xh"], n + 1)
                        pe.wait_ge(s["bn_s"], n * SUB + 2)
                    if o == 1:
                        pe.wait_ge(s["bn_s"], n * SUB + 3)
                    if o == 2:
                        pe.wait_ge(s["bn_s"], n * SUB + 4)
                    p = bank[(6, 7, 5)[o]][:, 0:T]
                    for k in range(KC):
                        last = three_pass(p, WQH[:, k, o * P:(o + 1) * P], WQL[:, k, o * P:(o + 1) * P],
                                          XH[:, k, :], XL[:, k, :], k == 0, k == KC - 1)
                    last.then_inc(s["q_mm"], 1)

                def spread_r(n):
                    pe.wait_ge(s["dg"], n * 2 + 2)
                    pe.wait_ge(s["q_ev"], n * KC + 1)
                    pe.wait_ge(s["qq"], n * KC + 1)
                    for u in range(SUB):
                        mm(bank[6][:, u * TS:(u + 1) * TS], o1r[:, :], DH[:, u, :], start=True, stop=False)
                        last = mm(bank[6][:, u * TS:(u + 1) * TS], o1r[:, :], DL[:, u, :], start=False, stop=True)
                    last.then_inc(s["rb_mm"], 1)

                def query_norms(n):
                    pe.wait_ge(s["q_ev"], n * KC + 2)
                    pe.wait_ge(s["qq"], n * KC + KC)
                    for u in range(SUB):
                        for k in range(KC):
                            last = mm(bank[7][0:TS, u * NH1:(u + 1) * NH1], QQ[:, k * T + u * TS:k * T + (u + 1) * TS],
                                      hsel[:, k, :], start=(k == 0), stop=(k == KC - 1))
                    last.then_inc(s["qs_mm"], 1)

                def attend(n, u):
                    if u == 0:
                        pe.wait_ge(s["q_ev"], n * KC + KC)
                    if u == 1:
                        pe.wait_ge(s["xsr"], n + 1)
                    if u == 2:
                        pe.wait_ge(s["qn_s"], n + 1)
                    if u == 3:
                        pe.wait_ge(s["o_sc"], n * SUB + 1)
                    p = bank[(5, 6, 7, 5)[u]]
                    for k, (lo, hi) in enumerate(WIN):
                        last = mm(p[0:TS, lo:hi], Q[:, k, u * TS:(u + 1) * TS], AB[:, WOFF[k]:WOFF[k] + hi - lo],
                                  start=(k == 0), stop=(k == KC - 1), skip_group_check=True)
                    last.then_inc(s["qa_mm"], 1)

                def fc1(n, j):
                    if j == 0:
                        pe.wait_ge(s["xrl"], n + 1)
                        pe.wait_ge(s["xrh"], n + 1)
                    pe.wait_ge(s["s_s"], HEAD + n * JC + (j - 1))
                    p = bank[j % 2][:, 0:T]
                    for k in range(KC):
                        last = three_pass(p, W1H[:, k, j * P:(j + 1) * P], W1L[:, k, j * P:(j + 1) * P],
                                          XRH[:, k, :], XRL[:, k, :], k == 0, k == KC - 1)
                    last.then_inc(s["f1"], 1)

                def fc2(n, j, first):
                    pe.wait_ge(s["sl"], HEAD + n * JC + j + 1)
                    pe.wait_ge(s["sh"], n * JC + j + 1)
                    if j == 0 and not first:
                        pe.wait_ge(s["mid"], n * KC)
                    for o in range(KC):
                        last = three_pass(bank[2 + o][:, 0:T], W2H[:, j, o * P:(o + 1) * P], W2L[:, j, o * P:(o + 1) * P],
                                          SH[:, j % 3, :], SL[:, j % 3, :], j == 0, j == JC - 1)
                    last.then_inc(s["f2"], 1)

                def proj(n):
                    pe.wait_ge(s["mh"], n + 1)
                    pe.wait_ge(s["ml"], n + 1)
                    for o in range(KC):
                        p = bank[CB[o]][:, 0:T]
                        for k in range(KC):
                            last = three_pass(p, WPH[:, k, o * P:(o + 1) * P], WPL[:, k, o * P:(o + 1) * P],
                                              MH[:, k, :], ML[:, k, :], k == 0, k == KC - 1)
                        last.then_inc(s["pj"], 1)

                def turn_o(n, prev):
                    pe.wait_ge(s["o_fin"], n + 1)
                    for k in range(KC):
                        if prev:
                            pe.wait_ge(s["y_s"], (n - 1) * KC + k + 1)
                        for u in range(SUB):
                            last = tr(bank[CB[k]][:, u * TS:(u + 1) * TS], V[:, u, k * P:(k + 1) * P], ident[0:TS, 0:TS])
                        last.then_inc(s["ot_mm"], 1)

                def pre(n, step):
                    if step == 1:
                        pe.wait_ge(s["xs"], n * KC + KC)
                        turn_x(n, 0)
                        turn_x(n, 1)
                        turn_x(n, 2)
                    elif step == 2:
                        turn_x(n, 3)
                        query(n, 0)
                    elif step == 3:
                        query(n, 1)
                        query(n, 2)
                    elif step == 4:
                        spread_r(n)
                        query_norms(n)
                    elif step == 5:
                        attend(n, 0)
                        attend(n, 1)
                    elif step == 6:
                        attend(n, 2)
                    elif step == 7:
                        attend(n, 3)

                def tile(n, first, last):
                    fc1(n, 0)
                    fc1(n, 1)
                    fc1(n, 2)
                    fc2(n, 0, first)
                    if not first:
                        pe.wait_ge(s["o_sc"], n * SUB + SUB)
                        if nxt:
                            pe.wait_ge(s["vt_ev"], HEAD + (n + (STRIPS - 1)) * SUB + SUB)
                        proj(n - 1)
                    fc1(n, 3)
                    if first:
                        pe.wait_ge(s["o_sc"], n * SUB + SUB)
                    turn_o(n, not first)
                    fc2(n, 1, first)
                    fc1(n, 4)
                    if not last:
                        pe.wait_ge(s["ot_ev"], n * KC + KC)
                        pre(n + 1, 1)
                    fc2(n, 2, first)
                    fc1(n, 5)
                    for i in range(3, JC):
                        if not last and 2 <= i - 1 <= 7:
                            pre(n + 1, i - 1)
                        fc2(n, i, first)
                        if i + 3 < JC:
                            fc1(n, i + 3)
                        if nxt and i == 9:
                            if last:
                                pe.wait_ge(s["ot_ev"], n * KC + KC)
                            else:
                                pe.wait_ge(s["o_sc"], (n + 1) * SUB + SUB)
                            for u in range(3):
                                turn_values(n + STRIPS, u)
                        if nxt and i == 10:
                            turn_values(n + STRIPS, 3)

                for step in range(1, 8):
                    pre(n0, step)
                tile(n0, True, False)
                with pe.Fori(1, STRIPS - 1) as t:
                    tile(b * STRIPS + t, False, False)
                tile(n0 + STRIPS - 1, False, True)
                pe.wait_ge(s["ot_ev"], (n0 + STRIPS) * KC)
                if nxt:
                    pe.wait_ge(s["vt_ev"], HEAD + (n0 + 2 * STRIPS) * SUB)
                proj(n0 + STRIPS - 1)
                stage_end(pe, stage(b, 3))

            with pe.Fori(0, B - 1) as b:
                image(b, True)
            image(B - 1, False)

        @block.scalar
        def _(act):
            fn = act.activation
            act.wait_ge(s["const_ld"], CONSTS * 16)

            def lead(dst, src):
                fn(dst, src, ACT.Copy).then_inc(s["stg_h"], 1)

            act.wait_ge(s["stg_ld1"], 16)
            lead(W2H[:, :, :], stg[1][:, :].rearrange("p (k n) -> p k n", k=JC))
            act.wait_ge(s["stg_ld1"], 48)
            qkv = stg[1][:, 0:KC * 3 * C].rearrange("p (k n) -> p k n", k=KC)
            lead(WQH[:, :, :], qkv[:, :, 0:C])
            lead(WKVH[:, :, :], qkv[:, :, C:3 * C])
            lead(WPH[:, :, :], stg[1][:, KC * 3 * C:KC * 4 * C].rearrange("p (k n) -> p k n", k=KC))
            act.wait_ge(s["set_ctr"], 1)
            lead(W1H[:, :, :], stg[0][:, :].rearrange("p (k n) -> p k n", k=KC))
            stage_end(act, 0)

            def normalise(m, which, accs, xg=XG, slots=1):
                act.wait_ge(s[f"xr{which}_ld"], m * 16 + 16)
                for acc in accs:
                    act.wait_ge(s[acc], HEAD + m * 24 - (slots - 1) * 24)
                for k in range(KC):
                    fn(xg[:, k, :, 1:W + 1], XR[:, k, :, :], ACT.Identity, bias=coefB[:, k, 0:1],
                       scale=coefA[:, k, 0:1]).then_inc(s[f"xg{which}"], 1)

            def centre_tap(m, acc, conv, st, which, used, value, sg, xg=XG):
                rows, cols = (RS, W) if st == 1 else (SR, WK)
                act.wait_ge(s[used], value)
                for k in range(KC):
                    act.wait_ge(s[f"xg{which}"], m * KC + k + 1)
                    fn(acc[:, k, :].rearrange("p (r w) -> p r w", w=cols),
                       xg[:, k, 1:2 + st * (rows - 1):st, 1:2 + st * (cols - 1):st],
                       ACT.Identity, bias=bconv[:, conv, k:k + 1], scale=wconv[:, conv, k, 4:5]).then_inc(s[sg], 1)

            def offset_start(m, xg):
                centre_tap(m, OA, 3, 2, 1, "otp", HEAD + m, "o0", xg)

            def keys_start(m, xg):
                centre_tap(m, KA, 2, 2, 1, "ktp", HEAD + m, "k0", xg)

            def offset_gelu(m):
                act.wait_ge(s["ln_s"], m + 1)
                fn(LN[:, :], LN[:, :], ACT.Gelu).then_inc(s["gelu"], 1)

            def keys_out(m):
                act.wait_ge(s["ktp"], HEAD + m + 1)
                act.wait_ge(s["kt_st"], HEAD + m * 16)
                fn(KT[:, :], bank[7][0:TK, 0:C], ACT.Copy).then_inc(s["kt_ev"], 1)

            def values_start(m):
                centre_tap(m, VA, 0, 1, 2, "vtp", HEAD + m * SUB, "v0")

            def queries_start(m):
                centre_tap(m, QA, 1, 1, 2, "q_st", HEAD + m * 16, "q0")

            def values_out(m, u):
                act.wait_ge(s["vtp"], HEAD + m * SUB + u + 1)
                act.wait_ge(s[f"pair_st{u % 2}"], HEAD + m * 64 + (u // 2) * 32)
                fn(VT[:, u % 2, :], bank[(6, 7, 5, 6)[u]][0:TS, 0:C], ACT.Copy).then_inc(s["vt_ev"], 1)

            def tanh(g):
                act.wait_ge(s["offr"], g + 1)
                fn(POS[:, :, :], OFF[:, :, :], ACT.Tanh).then_inc(s["tanh_s"], 1)

            def front(m, xg, other, more):
                centre_tap(m, OA, 3, 2, 2, "otp", HEAD + m, "o0", xg)
                centre_tap(m, VA, 0, 1, 2, "vtp", HEAD + m * SUB, "v0", xg)
                centre_tap(m, KA, 2, 2, 2, "ktp", HEAD + m, "k0", xg)
                if more:
                    normalise(m + 1, 2, ("oa", "ka", "va", "qa"), other, 2)
                offset_gelu(m)
                act.wait_ge(s["q_st"], HEAD + m * 16)
                for k in range(KC):
                    act.wait_ge(s["q0"], m * KC + k + 1)
                    fn(QA[:, k, :], bank[k][:, 0:T], ACT.Identity, bias=bconv[:, 1, k:k + 1]).then_inc(s["qa"], 8)
                for u in range(SUB):
                    values_out(m, u)
                keys_out(m)

            normalise(0, 2, ("oa", "ka", "va", "qa"), XG, 2)
            for k in range(KC):
                for i, (ky, kx) in enumerate(TAPS):
                    w = 3 * ky + kx
                    last = fn(diag[:, k, i, :], ident[:, :], ACT.Copy, scale=wconv[:, 1, k, w:w + 1])
                last.then_inc(s["diag_s"], 1)
            with act.Fori(0, STRIPS // 2) as h:
                front(h * 2, XG, XG2, True)
                front(h * 2 + 1, XG2, XG, True)
            front(STRIPS - 1, XG, XG2, False)
            for _ in range(STRIPS):
                act.sem_inc(s["xg1"], KC)
            tanh(0)
            stage_end(act, 1)

            def image(b, nxt):
                stage_end(act, stage(b, 0))
                if nxt:
                    load_x0(act, b + 1, 0)
                    load_x0(act, b + 1, 1)
                    load_x0(act, b + 1, 2)
                for t in range(STRIPS):
                    if nxt and 3 <= t + 1 < STRIPS:
                        load_x0(act, b + 1, t + 1)
                    if t in (1, 2):
                        dst, src = ((WKVH, wkv_d[0]), (WKVL, wkv_d[1]))[t - 1]
                        act.dma_start(dst[:, :, :].bitcast(F32), src).then_inc(s["wkv_ld"], 16)
                    act.wait_ge(s[f"cq_ld{t % 2}"], slot_at(b, t, 2, 16))
                    if t >= 2:
                        act.wait_ge(s["y0"], (b * STRIPS + t - 1) * KC)
                    fn(CH[:, t % 2, :, :], CQ[:, t % 2, :, :], ACT.Copy).then_inc(s["ch"], 1)
                stage_end(act, stage(b, 1))

                def norm_in(n, ld, sg):
                    act.wait_ge(s[ld], n * 16 + 16)
                    for k in range(KC):
                        fn(X[:, k, :], X[:, k, :], ACT.Identity, bias=coefB[:, k, 1:2],
                           scale=coefA[:, k, 1:2]).then_inc(s[sg], 1)

                def kv_out(n, slot, u):
                    act.wait_ge(s["k_mm"], n * SUB + u + 1)
                    fn(KS[:, u, :], bank[u % 3][0:TS, 0:C], ACT.Square).then_inc(s["k_sq"], 1)
                    fn(K1[:, slot, u, :], bank[u % 3][0:TS, 0:C], ACT.Copy).then_inc(s["k_ev"], 1)
                    act.wait_ge(s["v_mm"], n * SUB + u + 1)
                    fn(V1[:, slot, u, :], bank[3 + u % 3][0:TS, 0:C], ACT.Copy).then_inc(s["v_ev"], 1)

                def kv_tile(n, slot, used, first):
                    m = n + STRIPS
                    xg = (XG, XG3)[slot]
                    if nxt:
                        offset_start(m, xg)
                    act.wait_ge(s["at_mm"], HEAD + n - 1)
                    act.wait_ge(s["k_red"], HEAD + n * 2)
                    act.wait_ge(s[f"v1_st{slot}"], HEAD + b * (slot_uses(slot, 2)[0] * 16) + used * 16)
                    kv_out(n, slot, 0)
                    if nxt:
                        if not first:
                            offset_gelu(m - 1)
                            keys_out(m - 1)
                        keys_start(m, xg)
                    kv_out(n, slot, 1)
                    kv_out(n, slot, 2)

                def next_in(n, slot):
                    norm_in(n, "kv_ld", "kxs")
                    if nxt:
                        normalise(n + STRIPS, 1, ("oa", "ka"), (XG, XG3)[slot], 2)

                def lead_in(n, first):
                    act.wait_ge(s["kxs"], n * KC + KC)
                    if not first:
                        act.wait_ge(s["v_mm"], n * SUB)
                        act.wait_ge(s["kxl"], n)
                    fn(XH[:, :, :], X[:, :, :], ACT.Copy).then_inc(s["kxh"], 1)

                n0 = b * STRIPS
                next_in(n0, 0)
                lead_in(n0, True)
                kv_tile(n0, 0, 0, True)
                next_in(n0 + 1, 1)
                kv_out(n0, 0, 3)
                lead_in(n0 + 1, False)
                with act.Fori(0, STRIPS // 2) as h:
                    n = b * STRIPS + h * 2 + 1
                    kv_tile(n, 1, h, False)
                    next_in(n + 1, 0)
                    kv_out(n, 1, 3)
                    lead_in(n + 1, False)
                    kv_tile(n + 1, 0, h + 1, False)
                    with act.If(h < STRIPS // 2 - 1):
                        next_in(n + 2, 1)
                    with act.Else():
                        act.nop()
                    kv_out(n + 1, 0, 3)
                    with act.If(h < STRIPS // 2 - 1):
                        lead_in(n + 2, False)
                    with act.Else():
                        act.nop()
                if nxt:
                    keys_out(n0 + 2 * STRIPS - 1)
                    offset_gelu(n0 + 2 * STRIPS - 1)
                stage_end(act, stage(b, 2))

                def query_out(n, o):
                    act.wait_ge(s["q_mm"], n * KC + o + 1)
                    p = bank[(6, 7, 5)[o]][:, 0:T]
                    fn(Q[:, o, :], p, ACT.Copy).then_inc(s["q_ev"], 1)
                    fn(QQ[:, o * T:(o + 1) * T], p, ACT.Square).then_inc(s["qq"], 1)

                def silu(n, j):
                    act.wait_ge(s["f1"], n * JC + j + 1)
                    act.wait_ge(s["sl"], HEAD + n * JC + j - 1)
                    fn(S[:, j % 2, :], bank[j % 2][:, 0:T], ACT.Silu, bias=b1p[:, j:j + 1]).then_inc(s["s_s"], 1)
                    act.wait_ge(s["f2"], HEAD + n * JC + j - 2)
                    act.wait_ge(s["s_s"], HEAD + n * JC + j + 1)
                    fn(SH[:, j % 3, :], S[:, j % 2, :], ACT.Copy).then_inc(s["sh"], 1)

                def o_square(n):
                    act.wait_ge(s["o_mx"], n + 1)
                    fn(OS, V[:, :, :].rearrange("p s c -> p (s c)"), ACT.Square).then_inc(s["o_sq"], 1)

                def mid_h(n):
                    act.wait_ge(s["mid"], n * KC + KC)
                    fn(MH[:, :, :], OT[:, :, :], ACT.Copy).then_inc(s["mh"], 1)

                def tile(n, first, last):
                    m = n + STRIPS
                    silu(n, 0)
                    if not first:
                        mid_h(n - 1)
                    silu(n, 1)
                    if nxt and not first:
                        values_out(m - 1, 2)
                        values_out(m - 1, 3)
                    silu(n, 2)
                    if not last:
                        norm_in(n + 1, "x_ld", "xs")
                    if nxt:
                        normalise(m, 2, ("va", "qa"))
                    silu(n, 3)
                    if not first:
                        act.wait_ge(s["ml"], n)
                    for k in range(KC):
                        act.wait_ge(s["ot_mm"], n * KC + k + 1)
                        fn(OT[:, k, :], bank[5 + k][:, 0:T], ACT.Copy).then_inc(s["ot_ev"], 1)
                    if nxt:
                        values_start(m)
                    silu(n, 4)
                    if nxt:
                        queries_start(m)
                    silu(n, 5)
                    if not last:
                        query_out(n + 1, 0)
                    silu(n, 6)
                    if not last:
                        query_out(n + 1, 1)
                        query_out(n + 1, 2)
                    for j in range(7, JC - 1):
                        silu(n, j)
                    if not last:
                        o_square(n + 1)
                    silu(n, JC - 1)
                    if nxt:
                        values_out(m, 0)
                        values_out(m, 1)

                norm_in(n0, "x_ld", "xs")
                if nxt:
                    tanh(b + 1)
                for o in range(KC):
                    query_out(n0, o)
                o_square(n0)
                tile(n0, True, False)
                with act.Fori(1, STRIPS - 1) as t:
                    tile(b * STRIPS + t, False, False)
                tile(n0 + STRIPS - 1, False, True)
                mid_h(n0 + STRIPS - 1)
                if nxt:
                    values_out(n0 + 2 * STRIPS - 1, 2)
                    values_out(n0 + 2 * STRIPS - 1, 3)
                stage_end(act, stage(b, 3))

            with act.Fori(0, B - 1) as b:
                image(b, True)
            image(B - 1, False)

        @block.vector
        def _(dve):
            tt, ts_, stt, cp = dve.tensor_tensor, dve.tensor_scalar, dve.scalar_tensor_tensor, dve.tensor_copy

            def f(ap):
                return ap.bitcast(F32)

            dve.wait_ge(s["const_ld"], CONSTS * 16)
            dve.memset(bst[:, :, 1, :, :], 1.0)

            def clear_borders(xg):
                for col in (0, W + 1):
                    dve.memset(xg[:, :, :, col:col + 1], 0.0)

            def strip_stats(g, t):
                dve.wait_ge(s[f"x0_ld{t % 3}"], slot_at(g, t, 3, 16))
                for k in range(KC):
                    last = dve.bn_stats(bst[:, k, 0, t, :], X0S[:, t % 3, k, :])
                last.then_inc(s["x0bn"], 1)

            def gn_coefs(g):
                for k in range(KC):
                    for w in range(2):
                        last = dve.bn_aggr(gst[:, k, w, :], bst[:, k, w, :, :].rearrange("p a c -> p (a c)"))
                last.then_inc(s["gn_st"], 1)
                dve.wait_ge(s["gn_mm"], g + 1)
                cp(gmv[:, :, :, :].rearrange("p k s c -> p (k s c)"), bank[4][:, 0:4 * KC]).then_inc(s["gn_s1"], 1)
                dve.wait_ge(s["gn_s1"], g + 1)
                tt(gdev[:, :, :, 0], gst[:, :, :, 0], gmv[:, :, :, 0], ALU.subtract)
                tt(gdev[:, :, :, 1], gst[:, :, :, 0], gmv[:, :, :, 0], ALU.subtract).then_inc(s["gn_d"], 1)
                dve.wait_ge(s["gn_d"], g + 1)
                tt(gdev[:, :, :, :], gdev[:, :, :, :], gdev[:, :, :, :], ALU.mult).then_inc(s["gn_dev"], 1)
                dve.wait_ge(s["gn_mm2"], g + 1)
                tt(gvar[:, :, :].rearrange("p k s -> p (k s)"), gmv[:, :, :, 1].rearrange("p k s -> p (k s)"),
                   bank[0][:, 0:4 * KC:2], ALU.add).then_inc(s["gn_v1"], 1)
                dve.wait_ge(s["gn_v1"], g + 1)
                ts_(gvar[:, :, :], gvar[:, :, :], EPS_GN, None, ALU.add).then_inc(s["gn_v2"], 1)
                dve.wait_ge(s["gn_rstd"], g + 1)
                cp(coefA[:, :, :], gvar[:, :, :])
                tt(gmean[:, :, :], gmv[:, :, :, 0], gvar[:, :, :], ALU.mult).then_inc(s["gn_nb"], 1)
                dve.wait_ge(s["gn_nb"], g + 1)
                ts_(coefB[:, :, :], gmean[:, :, :], -1.0, None, ALU.mult)

            for t in range(3):
                strip_stats(0, t)
            dve.wait_ge(s["stg_h"], 1)
            tt(W2L[:, :, :], stg[1][:, :].rearrange("p (k n) -> p k n", k=JC), f(W2H[:, :, :]), ALU.subtract).then_inc(s["stg_used"], 1)
            dve.wait_ge(s["set_ps"], 1)
            tt(b1p[:, :], b1[:, :], bank[0][:, 0:JC], ALU.add)
            for k in range(KC):
                last = ts_(stg[0][:, k * HID:(k + 1) * HID], stg[0][:, k * HID:(k + 1) * HID], lng[:, k:k + 1], None, ALU.mult)
            last.then_inc(s["set_sum"], 1)
            for t in range(3, STRIPS):
                strip_stats(0, t)
            dve.wait_ge(s["set_ps"], 2)
            dve.wait_ge(s["set_sum"], 1)
            for k in range(KC):
                for q in range(3):
                    v = stg[0][:, k * HID + q * 512:k * HID + (q + 1) * 512]
                    last = tt(v, v, bank[1 + q][:, :], ALU.subtract)
            last.then_inc(s["set_ctr"], 1)
            qkv = stg[1][:, 0:KC * 3 * C].rearrange("p (k n) -> p k n", k=KC)
            dve.wait_ge(s["stg_h"], 4)
            tt(WQL[:, :, :], qkv[:, :, 0:C], f(WQH[:, :, :]), ALU.subtract)
            tt(WKVL[:, :, :], qkv[:, :, C:3 * C], f(WKVH[:, :, :]), ALU.subtract).then_inc(s["stg_used"], 1)
            tt(WPL[:, :, :], stg[1][:, KC * 3 * C:KC * 4 * C].rearrange("p (k n) -> p k n", k=KC), f(WPH[:, :, :]), ALU.subtract)
            dve.wait_ge(s["x0bn"], STRIPS)
            alone(dve)
            gn_coefs(0)
            dve.wait_ge(s["stg_h"], 5)
            tt(W1L[:, :, :], stg[0][:, :].rearrange("p (k n) -> p k n", k=KC), f(W1H[:, :, :]), ALU.subtract)
            stage_end(dve, 0)

            def edges(t, m, which, xg=XG):
                dve.wait_ge(s[f"xg{which}"], m * KC + KC)
                ts_(xg[:, :, 0, 1:W + 1], xg[:, :, 0, 1:W + 1], edge[:, 0, bass.ds(t, 1)], None, ALU.mult)
                ts_(xg[:, :, RS + 1, 1:W + 1], xg[:, :, RS + 1, 1:W + 1], edge[:, 1, bass.ds(t, 1)], None,
                    ALU.mult).then_inc(s[f"edged{which}"], 1)
                dve.wait_ge(s[f"edged{which}"], m + 1)

            def taps(m, acc, conv, st, start, sg, first, count, xg):
                rows, cols = (RS, W) if st == 1 else (SR, WK)
                for q in range(first, first + count):
                    i, k = 1 + q // KC, q % KC
                    ky, kx = TAPS[i]
                    if i == 1:
                        dve.wait_ge(s[start], m * KC + k + 1)
                    else:
                        dve.wait_ge(s[sg], HEAD + m * 24 + (q - KC + 1))
                    src = xg[:, k, ky:ky + st * (rows - 1) + 1:st, kx:kx + st * (cols - 1) + 1:st]
                    o = acc[:, k, :].rearrange("p (r w) -> p r w", w=cols)
                    stt(o, src, wconv[:, conv, k, 3 * ky + kx:3 * ky + kx + 1], o, ALU.mult, ALU.add).then_inc(s[sg], 1)

            def offset_taps(m, first, count, xg=XG):
                taps(m, OA, 3, 2, "o0", "oa", first, count, xg)

            def key_taps(m, first, count, xg=XG):
                taps(m, KA, 2, 2, "k0", "ka", first, count, xg)

            def value_taps(m, first, count, xg=XG):
                taps(m, VA, 0, 1, "v0", "va", first, count, xg)

            def query_taps(m, first, count, xg=XG):
                taps(m, QA, 1, 1, "q0", "qa", first, count, xg)

            def offset_stats(m):
                dve.wait_ge(s["otp"], HEAD + m + 1)
                dve.bn_stats(obn[:, :], bank[7][0:TK, 0:C]).then_inc(s["obn_s"], 1)
                dve.wait_ge(s["obn_s"], m + 1)
                alone(dve)
                dve.bn_aggr(oag[:, :], obn[:, :]).then_inc(s["oag_s"], 1)
                dve.wait_ge(s["oag_s"], m + 1)
                ts_(orv[:, 0:1], oag[:, 1:2], EPS_LN, None, ALU.add).then_inc(s["orv_s"], 1)

            def offset_norm(m):
                dve.wait_ge(s["orr_s"], m + 1)
                dve.wait_ge(s["dots"], HEAD + m * 2)
                ts_(LN[:, :], bank[7][0:TK, 0:C], oag[:, 0:1], orv[:, 1:2], ALU.subtract, ALU.mult).then_inc(s["ln1"], 1)
                dve.wait_ge(s["ln1"], m + 1)
                tt(LN[:, :], LN[:, :], olng[:, :], ALU.mult).then_inc(s["ln2"], 1)
                dve.wait_ge(s["ln2"], m + 1)
                tt(LN[:, :], LN[:, :], olnb[:, :], ALU.add).then_inc(s["ln_s"], 1)

            def offset_dots(t, m):
                dve.wait_ge(s["gelu"], m + 1)
                dve.wait_ge(s["off_put"], HEAD + m)
                for p in range(2):
                    dve.wait_ge(s["dots"], HEAD + m * 2 + p - 1)
                    dve.tensor_tensor_reduce(out=prod[:, p, :], in0=LN[:, :], in1=woff2[:, p, :], scale=1.0, scalar=0.0,
                                             op0=ALU.mult, op1=ALU.add, accum_out=dot[:, p:p + 1]).then_inc(s["dots"], 1)
                dve.wait_ge(s["dots"], HEAD + m * 2 + 2)
                cp(OFF[:, bass.ds(t, 1), :].rearrange("p a c -> p (a c)"), dot[:, :]).then_inc(s["off_put"], 1)

            def sampling_points(g):
                steps = 9

                def after(i):
                    dve.wait_ge(s["point"], g * steps + i)

                dve.wait_ge(s["off_put"], HEAD + (g + 1) * STRIPS)
                tt(OFF[:, :, :], OFF[:, :, :], refp[:, :, :], ALU.add).then_inc(s["offr"], 1)
                dve.wait_ge(s["tanh_s"], g + 1)
                ts_(POS[:, :, :], POS[:, :, :], 1.0, 0.5 * (W - 1), ALU.add, ALU.mult).then_inc(s["point"], 1)
                after(1)
                cp(FI[:, :, :], POS[:, :, :]).then_inc(s["point"], 1)
                after(2)
                cp(FF[:, :, :], FI[:, :, :]).then_inc(s["point"], 1)
                after(3)
                tt(FG[:, :, :], FF[:, :, :], POS[:, :, :], ALU.is_gt).then_inc(s["point"], 1)
                after(4)
                tt(FF[:, :, :], FF[:, :, :], FG[:, :, :], ALU.subtract).then_inc(s["point"], 1)
                after(5)
                ts_(FF[:, :, :], FF[:, :, :], 0.0, float(W - 2), ALU.max, ALU.min).then_inc(s["point"], 1)
                after(6)
                tt(WG[:, :, :], POS[:, :, :], FF[:, :, :], ALU.subtract)
                ts_(IXF[:, 0, :], FF[:, :, 0], float(W), 1.0, ALU.mult, ALU.add).then_inc(s["point"], 1)
                after(7)
                tt(IXF[:, 0, :], IXF[:, 0, :], FF[:, :, 1], ALU.add)
                ts_(WN[:, :, :], WG[:, :, :], -1.0, 1.0, ALU.mult, ALU.add).then_inc(s["point"], 1)
                after(8)
                ts_(IXF[:, 1, :], IXF[:, 0, :], float(W), None, ALU.add).then_inc(s["point"], 1)
                for c, (wy, wx) in enumerate(((WN, WN), (WN, WG), (WG, WN), (WG, WG))):
                    last = tt(W4[:, :, c], wy[:, :, 0], wx[:, :, 1], ALU.mult)
                last.then_inc(s["w4s"], 1)
                after(9)
                cp(IX[:, :, :], IXF[:, :, :]).then_inc(s["ixi"], 1)

            clear_borders(XG)
            clear_borders(XG2)
            dve.wait_ge(s["off_ld"], 48)
            alone(dve)

            def front(t, m, xg):
                edges(t, m, 2, xg)
                offset_taps(m, 0, 24, xg)
                value_taps(m, 0, 12, xg)
                offset_stats(m)
                value_taps(m, 12, 12, xg)
                offset_norm(m)
                key_taps(m, 0, 24, xg)
                offset_dots(t, m)

            with dve.Fori(0, STRIPS // 2) as h:
                front(h * 2, h * 2, XG)
                front(h * 2 + 1, h * 2 + 1, XG2)
            front(STRIPS - 1, STRIPS - 1, XG)
            dve.sem_inc(s["edged1"], STRIPS)
            sampling_points(0)
            stage_end(dve, 1)

            def sample(b, nxt):
                dve.wait_ge(s["w4s"], b + 1)
                for t in range(STRIPS):
                    dve.wait_ge(s[f"gath{t}"], b * 32 + 32)
                    if t >= 2:
                        dve.wait_ge(s["mt_mm"], b * STRIPS + t - 1)
                    ts_(VS[:, t % 2, :], G7[:, t, 0, 0, :], W4[:, t, 0:1], None, ALU.mult).then_inc(s["vs_ch"], 1)
                    for c in range(1, 4):
                        dve.wait_ge(s["vs_ch"], b * (3 * STRIPS) + 3 * t + c)
                        last = stt(VS[:, t % 2, :], G7[:, t, c // 2, c % 2, :], W4[:, t, c:c + 1], VS[:, t % 2, :], ALU.mult, ALU.add)
                        last.then_inc(s["vs_ch"] if c < 3 else s["vs_s"], 1)
                dve.wait_ge(s["mt_mm"], b * STRIPS + STRIPS)
                for k in range(KC):
                    last = tt(MT[:, k, :], head0[:, :], bank[k][:, 0:P], ALU.mult)
                last.then_inc(s["mt_ev"], 1)
                dve.wait_ge(s["w2_mm"], b + 1)
                for k in range(KC):
                    last = cp(W2TH[:, k, :], bank[3 + k][:, 0:C])
                last.then_inc(s["w2_ev"], 1)
                dve.wait_ge(s["w2_ev"], b + 1)
                for k in range(KC):
                    tt(W2TL[:, k, :], bank[3 + k][:, 0:C], f(W2TH[:, k, :]), ALU.subtract)
                stage_end(dve, stage(b, 0))

            def project(b, nxt):
                for t in range(STRIPS + 1):
                    if t < STRIPS:
                        dve.wait_ge(s["ch"], b * STRIPS + t + 1)
                        tt(CL[:, t % 2, :, :], CQ[:, t % 2, :, :], f(CH[:, t % 2, :, :]), ALU.subtract).then_inc(s["cl"], 1)
                    if t >= 1:
                        u = t - 1
                        dve.wait_ge(s[f"cx_ld{u % 3}"], slot_at(b, u, 3, 16))
                        for o in range(KC):
                            dve.wait_ge(s["y0"], (b * STRIPS + u) * KC + o + 1)
                            tt(CX[:, u % 3, o, :], CX[:, u % 3, o, :], bank[2 + 3 * (u % 2) + o][:, 0:T], ALU.add).then_inc(s["x1a"], 1)
                        for o in range(KC):
                            dve.wait_ge(s["x1a"], (b * STRIPS + u) * KC + o + 1)
                            last = dve.bn_stats(bst[:, o, 1, u, :], CX[:, u % 3, o, :])
                        last.then_inc(s["x1bn"], 1)
                        if nxt:
                            strip_stats(b + 1, u)
                dve.wait_ge(s["x1bn"], b * STRIPS + STRIPS)
                if nxt:
                    dve.wait_ge(s["x0bn"], (b + 2) * STRIPS)
                alone(dve)
                gn_coefs(b + 1)
                stage_end(dve, stage(b, 1))

            def keys_values(b, nxt):
                n0 = b * STRIPS

                def kv_split(n, first):
                    if not first:
                        dve.wait_ge(s["v_mm"], n * SUB)
                    dve.wait_ge(s["kxh"], n + 1)
                    tt(XL[:, :, :], X[:, :, :], f(XH[:, :, :]), ALU.subtract).then_inc(s["kxl"], 1)

                PARTS = ((0, 3), (3, 4))

                def key_norm(n, h):
                    lo, hi = PARTS[h]
                    dve.wait_ge(s["k_sq"], n * SUB + hi)
                    dve.tensor_reduce(kn[:, lo * NH1:hi * NH1],
                                      KS[:, lo:hi, :].rearrange("p s (h c) -> p (s h) c", c=HD), AX.X, ALU.add).then_inc(s["k_red"], 1)

                def key_scale(n, slot, h):
                    lo, hi = PARTS[h]
                    dve.wait_ge(s["k_rs"], n * 2 + h + 1)
                    dve.wait_ge(s["k_ev"], HEAD + n * SUB + hi)
                    v = K1[:, slot, lo:hi, :].rearrange("p s (h c) -> p (s h) c", c=HD)
                    r = rk[:, lo * NH1:hi * NH1].unsqueeze(2).to_broadcast([TS, (hi - lo) * NH1, HD])
                    tt(v, v, r, ALU.mult).then_inc(s["k_hat"], 1)

                def kv_tile(t, n, slot, first):
                    m = n + STRIPS
                    xg = (XG, XG3)[slot]
                    kv_split(n, first)
                    if not first:
                        key_norm(n - 1, 1)
                    if nxt:
                        edges(t, m, 1, xg)
                        offset_taps(m, 0, 12, xg)
                    if not first:
                        key_scale(n - 1, 1 - slot, 0)
                        key_scale(n - 1, 1 - slot, 1)
                    if nxt:
                        offset_taps(m, 12, 12, xg)
                        key_taps(m, 0, 9, xg)
                        if not first:
                            offset_dots(t - 1, m - 1)
                        offset_stats(m)
                    key_norm(n, 0)
                    if nxt:
                        key_taps(m, 9, 9, xg)
                        offset_norm(m)
                        key_taps(m, 18, 6, xg)

                if nxt:
                    clear_borders(XG)
                    clear_borders(XG3)
                    dve.wait_ge(s["off_ld"], (b + 2) * 48)
                    alone(dve)
                kv_tile(0, n0, 0, True)
                with dve.Fori(0, STRIPS // 2) as h:
                    n = b * STRIPS + h * 2 + 1
                    kv_tile(h * 2 + 1, n, 1, False)
                    n = n + 1
                    kv_tile(h * 2 + 2, n, 0, False)
                nl = n0 + STRIPS - 1
                key_norm(nl, 1)
                key_scale(nl, 0, 0)
                key_scale(nl, 0, 1)
                if nxt:
                    offset_dots(STRIPS - 1, nl + STRIPS)
                stage_end(dve, stage(b, 2))

            def rest(b, nxt):
                n0 = b * STRIPS

                tt(AB[:, :], head1[:, :], bank[6][:, 0:WTOT], ALU.mult).then_inc(s["ab_s"], 1)
                dve.memset(f(o1r[:, :]), 1.0)

                def split_x(n):
                    dve.wait_ge(s["xs"], n * KC + KC)
                    cp(XH[:, :, :], X[:, :, :]).then_inc(s["xh"], 1)
                    dve.wait_ge(s["xh"], n + 1)
                    tt(XL[:, :, :], X[:, :, :], f(XH[:, :, :]), ALU.subtract).then_inc(s["xl"], 1)

                def token_stats(n, u):
                    dve.wait_ge(s["xt_mm"], n * SUB + u + 1)
                    dve.bn_stats(xbn[:, u, :], bank[(5, 6, 7, 5)[u]][0:TS, 0:C]).then_inc(s["bn_s"], 1)

                def token_var(n):
                    dve.wait_ge(s["bn_s"], n * SUB + SUB)
                    alone(dve)
                    for u in range(SUB):
                        last = dve.bn_aggr(xag[:, u, :], xbn[:, u, :])
                    last.then_inc(s["ag_s"], 1)
                    dve.wait_ge(s["ag_s"], n + 1)
                    ts_(rve[:, :], xag[:, :, 1], EPS_LN, None, ALU.add).then_inc(s["rve_s"], 1)

                def token_diag(n):
                    dve.wait_ge(s["rr_s"], n + 1)
                    cp(rh[:, :], rr[:, :]).then_inc(s["rh_s"], 1)
                    dve.wait_ge(s["rh_s"], n + 1)
                    tt(rl[:, :], rr[:, :], f(rh[:, :]), ALU.subtract).then_inc(s["rl_s"], 1)
                    dve.wait_ge(s["rl_s"], n + 1)
                    idb = ident[0:TS, 0:TS].unsqueeze(1).to_broadcast([TS, SUB, TS])
                    tt(DH[:, :, :], idb, f(rh[:, :]).unsqueeze(2).to_broadcast([TS, SUB, TS]), ALU.mult).then_inc(s["dg"], 1)
                    tt(DL[:, :, :], idb, rl[:, :].unsqueeze(2).to_broadcast([TS, SUB, TS]), ALU.mult).then_inc(s["dg"], 1)

                def scale_x(n):
                    dve.wait_ge(s["rb_mm"], n + 1)
                    tt(X[:, :, :], X[:, :, :], bank[6][:, 0:T].unsqueeze(1).to_broadcast([P, KC, T]), ALU.mult).then_inc(s["xsr"], 1)

                def query_norm(n):
                    dve.wait_ge(s["qs_mm"], n + 1)
                    cp(qn[:, :], bank[7][0:TS, 0:SUB * NH1]).then_inc(s["qn_s"], 1)

                def heads(ap):
                    return ap.rearrange("p (h c) -> p h c", c=HD)

                def o_scale(n, u):
                    if u == 0:
                        dve.wait_ge(s["rq_s"], n + 1)
                    dve.wait_ge(s["qa_mm"], n * SUB + u + 1)
                    r = rq[:, u * NH1:(u + 1) * NH1].unsqueeze(2).to_broadcast([TS, NH1, HD])
                    tt(heads(OS[:, u * C:(u + 1) * C]), heads(bank[(5, 6, 7, 5)[u]][0:TS, 0:C]), r, ALU.mult).then_inc(s["o_sc"], 1)

                def o_mix(n):
                    dve.wait_ge(s["o_sc"], n * SUB + SUB)
                    dve.wait_ge(s["v_ld"], n * 16 + 16)
                    vf = V[:, :, :].rearrange("p s c -> p (s c)")
                    stt(vf, vf, 0.5, OS, ALU.mult, ALU.add).then_inc(s["o_mx"], 1)

                def o_norm(n):
                    dve.wait_ge(s["o_sq"], n + 1)
                    dve.tensor_reduce(on[:, :], heads(OS), AX.X, ALU.add).then_inc(s["o_red"], 1)

                def o_final(n):
                    dve.wait_ge(s["ro_s"], n + 1)
                    v = heads(V[:, :, :].rearrange("p s c -> p (s c)"))
                    tt(v, v, ro[:, :].unsqueeze(2).to_broadcast([TS, SUB * NH1, HD]), ALU.mult).then_inc(s["o_fin"], 1)

                def split_xr(n, first):
                    dve.wait_ge(s["xsr"], n + 1)
                    if not first:
                        dve.wait_ge(s["f1"], n * JC)
                    cp(XRH[:, :, :], X[:, :, :]).then_inc(s["xrh"], 1)
                    dve.wait_ge(s["xrh"], n + 1)
                    tt(XRL[:, :, :], X[:, :, :], f(XRH[:, :, :]), ALU.subtract).then_inc(s["xrl"], 1)

                def split_s(n, j):
                    dve.wait_ge(s["sh"], n * JC + j + 1)
                    tt(SL[:, j % 3, :], S[:, j % 2, :], f(SH[:, j % 3, :]), ALU.subtract).then_inc(s["sl"], 1)

                def middle(n):
                    dve.wait_ge(s["ot_ev"], n * KC + KC)
                    dve.wait_ge(s["f2"], HEAD + n * JC + JC)
                    for k in range(KC):
                        stt(OT[:, k, :], bank[2 + k][:, 0:T], b2[:, k:k + 1], OT[:, k, :], ALU.add, ALU.add).then_inc(s["mid"], 1)
                    dve.wait_ge(s["mh"], n + 1)
                    tt(ML[:, :, :], OT[:, :, :], f(MH[:, :, :]), ALU.subtract).then_inc(s["ml"], 1)

                def output(n):
                    dve.wait_ge(s["y_ld"], n * 16 + 16)
                    for k in range(KC):
                        dve.wait_ge(s["pj"], n * KC + k + 1)
                        stt(Y[:, k, :], bank[5 + k][:, 0:T], bp[:, k:k + 1], Y[:, k, :], ALU.add, ALU.add).then_inc(s["y_s"], 1)

                BODY = 14

                def tile(t, n, first, last):
                    m = n + STRIPS
                    if not first:
                        middle(n - 1)
                    split_s(n, 0)
                    if nxt and not first:
                        query_taps(m - 1, BODY, 24 - BODY)
                    o_final(n)
                    split_s(n, 1)
                    if not first:
                        output(n - 1)
                    split_s(n, 2)
                    if not last:
                        split_x(n + 1)
                    if nxt:
                        edges(t, m, 2)
                        value_taps(m, 0, 4)
                    split_s(n, 3)
                    if not last:
                        for u in range(SUB):
                            token_stats(n + 1, u)
                        token_var(n + 1)
                    if nxt:
                        value_taps(m, 4, 4)
                    split_s(n, 4)
                    if not last:
                        token_diag(n + 1)
                    if nxt:
                        value_taps(m, 8, 6)
                    split_s(n, 5)
                    if not last:
                        scale_x(n + 1)
                        query_norm(n + 1)
                    if nxt:
                        value_taps(m, 14, 4)
                    split_s(n, 6)
                    if nxt:
                        value_taps(m, 18, 6)
                    split_s(n, 7)
                    if not last:
                        o_scale(n + 1, 0)
                        o_scale(n + 1, 1)
                    if nxt:
                        query_taps(m, 0, 3)
                    split_s(n, 8)
                    if not last:
                        o_scale(n + 1, 2)
                        o_scale(n + 1, 3)
                    if nxt:
                        query_taps(m, 3, 3)
                    split_s(n, 9)
                    if not last:
                        o_mix(n + 1)
                    if nxt:
                        query_taps(m, 6, 2)
                    split_s(n, 10)
                    if not last:
                        split_xr(n + 1, False)
                    split_s(n, 11)
                    if not last:
                        o_norm(n + 1)
                    if nxt:
                        query_taps(m, 8, BODY - 8)

                split_x(n0)
                for u in range(SUB):
                    token_stats(n0, u)
                token_var(n0)
                if nxt:
                    sampling_points(b + 1)
                token_diag(n0)
                scale_x(n0)
                query_norm(n0)
                split_xr(n0, True)
                for u in range(SUB):
                    o_scale(n0, u)
                o_mix(n0)
                o_norm(n0)
                tile(0, n0, True, False)
                with dve.Fori(1, STRIPS - 1) as t:
                    tile(t, b * STRIPS + t, False, False)
                tile(STRIPS - 1, n0 + STRIPS - 1, False, True)
                middle(n0 + STRIPS - 1)
                if nxt:
                    query_taps(n0 + 2 * STRIPS - 1, BODY, 24 - BODY)
                output(n0 + STRIPS - 1)
                stage_end(dve, stage(b, 3))

            def image(b, nxt):
                for part in (sample, project, keys_values, rest):
                    if isinstance(b, int):
                        part(b, nxt)
                    else:
                        with dve.Fori(b, b + 1) as c:
                            part(c, nxt)

            with dve.Fori(0, B - 1) as b:
                image(b, True)
            image(B - 1, False)


def kernel(**inputs):
    import numpy as _np
    import concourse.bacc as _bacc
    from concourse import mybir as _mybir
    from concourse.bass_utils import run_bass_kernel_spmd as _run

    def a(name):
        return _np.asarray(inputs[name])

    def rows(w):
        k = w.shape[0] // P
        return w.reshape(k, P, -1).transpose(1, 0, 2).reshape(P, -1)

    def cols(v):
        return v.reshape(-1, P).T

    def chunks(w):
        return w.reshape(-1, P, w.shape[-1]).transpose(1, 0, 2)

    x = a("x")
    arrays = dict(constants())
    arrays.update({
        "x": _np.pad(x, ((0, 0), (0, 0), (1, 1), (0, 0))),
        "fc1_w": rows(a("L1_conv_fc1_w")), "fc2_w": rows(a("L1_conv_fc2_w")),
        "qkv_w": rows(a("L1_conv_qkv_w")), "proj_w": rows(a("L1_conv_proj_w")),
        "fc1_b": cols(a("L1_conv_fc1_b")), "fc2_b": cols(a("L1_conv_fc2_b")), "proj_b": cols(a("L1_conv_proj_b")),
        "ln_g": cols(a("L1_conv_ln_g")), "ln_b": cols(a("L1_conv_ln_b")),
        "w_conv": _np.stack([chunks(a("L0_conv_w_" + n).reshape(C, 9)) for n in ("v", "q", "k", "off1")], 1),
        "b_conv": _np.stack([cols(a("L0_conv_b_" + n)) for n in ("v", "q", "k", "off1")], 1),
        "off_g": _np.tile(a("L0_conv_ln_g"), (TK, 1)), "off_b": _np.tile(a("L0_conv_ln_b"), (TK, 1)),
        "w_off2": _np.tile(a("L0_conv_w_off2")[None], (TK, 1, 1)),
        "w_outT": chunks(a("L0_conv_w_out").T),
    })
    nc = _bacc.Bacc("TRN2", target_bir_lowering=False, num_devices=1)
    feed, d = {}, {}
    for name, v in arrays.items():
        v = _np.ascontiguousarray(v)
        feed[f"in_{name}"] = v
        d[name] = nc.dram_tensor(f"in_{name}", v.shape, _mybir.dt.from_np(v.dtype), kind="ExternalInput").ap()
    out = nc.dram_tensor("out_0", x.shape, F32, kind="ExternalOutput").ap()
    build(nc, d, out)
    r = _run(nc, [feed], core_ids=[0])
    return r.results[0]["out_0"]
```
